# Optimizing a Trainium2 kernel written in Bass

```python
import numpy as np
import jax
import jax.numpy as jnp

def _softmax(x, axis=-1):
    return jax.nn.softmax(x, axis=axis)

def _gelu(x):
    return jax.nn.gelu(x, approximate=True)

def _silu(x):
    return jax.nn.silu(x)

def _sigmoid(x):
    return jax.nn.sigmoid(x)

def _layernorm(x, axis=-1, eps=1e-05):
    m = jnp.mean(x, axis=axis, keepdims=True)
    v = jnp.var(x, axis=axis, keepdims=True)
    return (x - m) / jnp.sqrt(v + eps)

def _scatter_add(tgt, idx, src, axis=0):
    return tgt.at[idx].add(src)

def _segment_sum(src, seg, n):
    return jax.ops.segment_sum(src, seg, n)
kernel_name = 'mk_decoder_postln_d1_seqx_r8_79a17d'

def setup_inputs(seed: int=0):
    np.random.seed(seed)
    _w = jnp.asarray

    def _rec_inputs():
        import jax
        import jax.numpy as jnp
        _rk = jax.random.key(seed)
        x = -0.0003929 + 0.9999 * jax.random.normal(jax.random.fold_in(_rk, 1), (32, 64, 256), jnp.float32)
        _lenS = 64 - jax.random.randint(jax.random.fold_in(_rk, 7), (32,), 0, max(1, 64 // 4) + 1, jnp.int32)
        _lenS2 = 64 - jax.random.randint(jax.random.fold_in(_rk, 8), (32,), 0, max(1, 64 // 4) + 1, jnp.int32)
        _ctx_2048P = jax.random.normal(jax.random.fold_in(_rk, 11), (32, 16, 256), jnp.float32)
        _ctx_2048c = jax.random.dirichlet(jax.random.fold_in(_rk, 511), 0.3 * jnp.ones((16,), jnp.float32), (32, 64))
        _ctx_2048t = jnp.einsum('bsk,bkd->bsd', _ctx_2048c, _ctx_2048P)
        _ctx_2048t = _ctx_2048t * jax.lax.rsqrt(jnp.mean(jnp.square(_ctx_2048t)) + 1e-12) * 0.953939
        ctx_2048 = -1.39393e-06 + 0.999914 * (_ctx_2048t + 0.3 * jax.random.normal(jax.random.fold_in(_rk, 611), (32, 64, 256), jnp.float32))
        itok_BxS_0_1023 = jax.random.randint(jax.random.fold_in(_rk, 12), (32, 64), 0, 128, jnp.int32)
        return (x, ctx_2048, itok_BxS_0_1023)
    x, ctx_2048, itok_BxS_0_1023 = _rec_inputs()

    def _L0_attn_setup():
        import jax, jax.numpy as jnp
        import numpy as np
        H = 8
        DH = 128
        NH = 2
        HID = 256
        CONV = 4
        EPS = 1e-05
        KEY_DIM = H * DH

        def _dwconv_silu(x, w):
            y = jax.lax.conv_general_dilated(x.transpose(0, 2, 1), w[:, None, :], (1,), [(w.shape[-1] - 1, 0)], feature_group_count=w.shape[0])
            return jax.nn.silu(y).transpose(0, 2, 1)

        def _l2norm(x):
            return x / jnp.maximum(jnp.linalg.norm(x, axis=-1, keepdims=True), 1e-12)

        def _forward(x, Wq, Wk, Wv, Wb, Wa, Wg, Wo, A_log, dt_bias, conv_q, conv_k, conv_v, o_norm_w):
            B, L, _ = x.shape
            T = L * NH
            q = _dwconv_silu(x @ Wq.T, conv_q).reshape(B, L, H, DH)
            k = _dwconv_silu(x @ Wk.T, conv_k).reshape(B, T, H, DH)
            v = _dwconv_silu(x @ Wv.T, conv_v).reshape(B, T, H, DH)
            beta = jax.nn.sigmoid(x @ Wb.T).reshape(B, T, H) * 2.0
            g = -jnp.exp(A_log) * jax.nn.softplus(x @ Wa.T + dt_bias)
            q = _l2norm(q) / DH ** 0.5
            k = _l2norm(k)
            g_full = jnp.zeros((B, L, NH, H), x.dtype).at[:, :, 0].set(g).reshape(B, T, H)
            q_full = jnp.zeros((B, L, NH, H, DH), x.dtype).at[:, :, -1].set(q).reshape(B, T, H, DH)

            def step(state, inp):
                q_t, k_t, v_t, g_t, b_t = inp
                state = state * jnp.exp(g_t)[..., None, None]
                corr = jnp.einsum('bhk,bhkv->bhv', k_t, state)
                v_new = (v_t - corr) * b_t[..., None]
                state = state + jnp.einsum('bhk,bhv->bhkv', k_t, v_new)
                o_t = jnp.einsum('bhk,bhkv->bhv', q_t, state)
                return (state, o_t)
            xs = (q_full.transpose(1, 0, 2, 3), k.transpose(1, 0, 2, 3), v.transpose(1, 0, 2, 3), g_full.transpose(1, 0, 2), beta.transpose(1, 0, 2))
            state0 = jnp.zeros((B, H, DH, DH), x.dtype)
            final_state, o = jax.lax.scan(step, state0, xs)
            o = o.transpose(1, 0, 2, 3).reshape(B, L, NH, H, DH)[:, :, -1]
            gg = (x @ Wg.T).reshape(B, L, H, DH)
            o = o * jax.lax.rsqrt(jnp.mean(o * o, -1, keepdims=True) + EPS)
            o = o * o_norm_w * jax.nn.silu(gg)
            return (o.reshape(B, L, KEY_DIM) @ Wo.T, final_state)

        def _reference_tuple_inner(x, Wq, Wk, Wv, Wb, Wa, Wg, Wo, A_log, dt_bias, conv_q, conv_k, conv_v, o_norm_w):
            return _forward(x, Wq, Wk, Wv, Wb, Wa, Wg, Wo, A_log, dt_bias, conv_q, conv_k, conv_v, o_norm_w)
        key = jax.random.key(seed)
        ks = jax.random.split(key, 16)
        B, L = (2, 128)
        s = 0.02
        return {'x': jax.random.normal(ks[0], (B, L, HID), jnp.float32), 'Wq': jax.random.normal(ks[1], (KEY_DIM, HID), jnp.float32) * s, 'Wk': jax.random.normal(ks[2], (KEY_DIM * NH, HID), jnp.float32) * s, 'Wv': jax.random.normal(ks[3], (KEY_DIM * NH, HID), jnp.float32) * s, 'Wb': jax.random.normal(ks[4], (H * NH, HID), jnp.float32) * s, 'Wa': jax.random.normal(ks[5], (H, HID), jnp.float32) * s, 'Wg': jax.random.normal(ks[6], (KEY_DIM, HID), jnp.float32) * s, 'Wo': jax.random.normal(ks[7], (HID, KEY_DIM), jnp.float32) * s, 'A_log': jnp.log(jax.random.uniform(ks[8], (H,), jnp.float32, 1.0, 8.0)), 'dt_bias': jax.random.normal(ks[9], (H,), jnp.float32) * 0.1, 'conv_q': jax.random.normal(ks[10], (KEY_DIM, CONV), jnp.float32) * 0.3, 'conv_k': jax.random.normal(ks[11], (KEY_DIM * NH, CONV), jnp.float32) * 0.3, 'conv_v': jax.random.normal(ks[12], (KEY_DIM * NH, CONV), jnp.float32) * 0.3, 'o_norm_w': jnp.ones((DH,), jnp.float32)}
    _L0_attn_all = _L0_attn_setup()
    _L0_attn_in = {k: v for k, v in _L0_attn_all.items() if k in ('Wq', 'Wk', 'Wv', 'Wb', 'Wa', 'Wg', 'Wo', 'A_log', 'dt_bias', 'conv_q', 'conv_k', 'conv_v', 'o_norm_w')}
    del _L0_attn_all

    def _L0_xattn_setup():
        import jax, jax.numpy as jnp
        import numpy as np
        B, Lq, Lk = (2, 512, 128)
        Q_DIM, KV_DIM = (256, 256)
        H, HD = (16, 128)
        KVC, QC, R = (64, 96, 64)
        LOOKBACK = 8
        NEG = -1e+30

        def _rope(x, L):
            half = x.shape[-1] // 2
            inv_freq = 1.0 / 10000.0 ** (jnp.arange(half, dtype=jnp.float32) / half)
            ang = jnp.arange(L, dtype=jnp.float32)[:, None] * inv_freq
            cos, sin = (jnp.cos(ang), jnp.sin(ang))
            x1, x2 = (x[..., :half], x[..., half:])
            return jnp.concatenate([x1 * cos - x2 * sin, x1 * sin + x2 * cos], axis=-1)
        key = jax.random.key(seed)
        ks = jax.random.split(key, 11)

        def w(k, shape, fan_in):
            return jax.random.normal(k, shape, jnp.float32) / np.sqrt(fan_in).astype(np.float32)
        return {'q': jax.random.normal(ks[0], (B, Lq, Q_DIM), jnp.float32), 'kv': jax.random.normal(ks[1], (B, Lk, KV_DIM), jnp.float32), 'seg_id': jnp.sort(jax.random.randint(ks[2], (B, Lq), 0, Lk), axis=-1), 'W_kvc': w(ks[3], (KV_DIM, KVC), KV_DIM), 'W_dq': w(ks[4], (Q_DIM, QC), Q_DIM), 'W_uq': w(ks[5], (QC, H * HD), QC), 'W_qr': w(ks[6], (QC, H * R), QC), 'W_uk': w(ks[7], (KVC, H * HD), KVC), 'W_kr': w(ks[8], (KVC, R), KVC), 'W_uv': w(ks[9], (KVC, H * HD), KVC), 'W_o': w(ks[10], (H * HD, Q_DIM), H * HD)}
    _L0_xattn_all = _L0_xattn_setup()
    _L0_xattn_in = {k: v for k, v in _L0_xattn_all.items() if k in ('W_kvc', 'W_dq', 'W_uq', 'W_qr', 'W_uk', 'W_kr', 'W_uv', 'W_o')}
    del _L0_xattn_all

    def _L0_ffn_setup():
        import jax, jax.numpy as jnp
        import numpy as np
        ZERO_POINT = 128.0

        def _dequant(wq, scale):
            return (wq.astype(jnp.float32) - ZERO_POINT) * scale[:, None]
        key = jax.random.key(seed)
        ks = jax.random.split(key, 7)
        H, I = (256, 1024)
        B, S = (2, 256)
        hidden_state = jax.random.normal(ks[0], (B, S, H), dtype=jnp.float32)
        gate_w = jax.random.randint(ks[1], (I, H), 0, 32, dtype=jnp.int32)
        up_w = jax.random.randint(ks[2], (I, H), 0, 32, dtype=jnp.int32)
        down_w = jax.random.randint(ks[3], (H, I), 0, 32, dtype=jnp.int32)
        gate_scale = jax.random.uniform(ks[4], (I,), dtype=jnp.float32) * 0.02
        up_scale = jax.random.uniform(ks[5], (I,), dtype=jnp.float32) * 0.02
        down_scale = jax.random.uniform(ks[6], (H,), dtype=jnp.float32) * 0.02
        return {'hidden_state': hidden_state, 'gate_w': gate_w, 'gate_scale': gate_scale, 'up_w': up_w, 'up_scale': up_scale, 'down_w': down_w, 'down_scale': down_scale}
    _L0_ffn_all = _L0_ffn_setup()
    _L0_ffn_in = {k: v for k, v in _L0_ffn_all.items() if k in ('gate_w', 'gate_scale', 'up_w', 'up_scale', 'down_w', 'down_scale')}
    del _L0_ffn_all
    return {'x': x, 'ctx_2048': ctx_2048, 'itok_BxS_0_1023': itok_BxS_0_1023, 'L0_attn_Wq': _L0_attn_in['Wq'], 'L0_attn_Wk': _L0_attn_in['Wk'], 'L0_attn_Wv': _L0_attn_in['Wv'], 'L0_attn_Wb': _L0_attn_in['Wb'], 'L0_attn_Wa': _L0_attn_in['Wa'], 'L0_attn_Wg': _L0_attn_in['Wg'], 'L0_attn_Wo': _L0_attn_in['Wo'], 'L0_attn_A_log': _L0_attn_in['A_log'], 'L0_attn_dt_bias': _L0_attn_in['dt_bias'], 'L0_attn_conv_q': _L0_attn_in['conv_q'], 'L0_attn_conv_k': _L0_attn_in['conv_k'], 'L0_attn_conv_v': _L0_attn_in['conv_v'], 'L0_attn_o_norm_w': _L0_attn_in['o_norm_w'], 'L0_xattn_W_kvc': _L0_xattn_in['W_kvc'], 'L0_xattn_W_dq': _L0_xattn_in['W_dq'], 'L0_xattn_W_uq': _L0_xattn_in['W_uq'], 'L0_xattn_W_qr': _L0_xattn_in['W_qr'], 'L0_xattn_W_uk': _L0_xattn_in['W_uk'], 'L0_xattn_W_kr': _L0_xattn_in['W_kr'], 'L0_xattn_W_uv': _L0_xattn_in['W_uv'], 'L0_xattn_W_o': _L0_xattn_in['W_o'], 'L0_ffn_gate_w': _L0_ffn_in['gate_w'], 'L0_ffn_gate_scale': _L0_ffn_in['gate_scale'], 'L0_ffn_up_w': _L0_ffn_in['up_w'], 'L0_ffn_up_scale': _L0_ffn_in['up_scale'], 'L0_ffn_down_w': _L0_ffn_in['down_w'], 'L0_ffn_down_scale': _L0_ffn_in['down_scale']}

def reference(x, ctx_2048, itok_BxS_0_1023, L0_attn_Wq, L0_attn_Wk, L0_attn_Wv, L0_attn_Wb, L0_attn_Wa, L0_attn_Wg, L0_attn_Wo, L0_attn_A_log, L0_attn_dt_bias, L0_attn_conv_q, L0_attn_conv_k, L0_attn_conv_v, L0_attn_o_norm_w, L0_xattn_W_kvc, L0_xattn_W_dq, L0_xattn_W_uq, L0_xattn_W_qr, L0_xattn_W_uk, L0_xattn_W_kr, L0_xattn_W_uv, L0_xattn_W_o, L0_ffn_gate_w, L0_ffn_gate_scale, L0_ffn_up_w, L0_ffn_up_scale, L0_ffn_down_w, L0_ffn_down_scale):
    import jax
    import jax.numpy as jnp

    def _L0_attn_ref(x, Wq, Wk, Wv, Wb, Wa, Wg, Wo, A_log, dt_bias, conv_q, conv_k, conv_v, o_norm_w):
        import jax, jax.numpy as jnp
        import numpy as np
        H = 8
        DH = 128
        NH = 2
        HID = 256
        CONV = 4
        EPS = 1e-05
        KEY_DIM = H * DH

        def _dwconv_silu(x, w):
            y = jax.lax.conv_general_dilated(x.transpose(0, 2, 1), w[:, None, :], (1,), [(w.shape[-1] - 1, 0)], feature_group_count=w.shape[0])
            return jax.nn.silu(y).transpose(0, 2, 1)

        def _l2norm(x):
            return x / jnp.maximum(jnp.linalg.norm(x, axis=-1, keepdims=True), 1e-12)

        def _forward(x, Wq, Wk, Wv, Wb, Wa, Wg, Wo, A_log, dt_bias, conv_q, conv_k, conv_v, o_norm_w):
            B, L, _ = x.shape
            T = L * NH
            q = _dwconv_silu(x @ Wq.T, conv_q).reshape(B, L, H, DH)
            k = _dwconv_silu(x @ Wk.T, conv_k).reshape(B, T, H, DH)
            v = _dwconv_silu(x @ Wv.T, conv_v).reshape(B, T, H, DH)
            beta = jax.nn.sigmoid(x @ Wb.T).reshape(B, T, H) * 2.0
            g = -jnp.exp(A_log) * jax.nn.softplus(x @ Wa.T + dt_bias)
            q = _l2norm(q) / DH ** 0.5
            k = _l2norm(k)
            g_full = jnp.zeros((B, L, NH, H), x.dtype).at[:, :, 0].set(g).reshape(B, T, H)
            q_full = jnp.zeros((B, L, NH, H, DH), x.dtype).at[:, :, -1].set(q).reshape(B, T, H, DH)

            def step(state, inp):
                q_t, k_t, v_t, g_t, b_t = inp
                state = state * jnp.exp(g_t)[..., None, None]
                corr = jnp.einsum('bhk,bhkv->bhv', k_t, state)
                v_new = (v_t - corr) * b_t[..., None]
                state = state + jnp.einsum('bhk,bhv->bhkv', k_t, v_new)
                o_t = jnp.einsum('bhk,bhkv->bhv', q_t, state)
                return (state, o_t)
            xs = (q_full.transpose(1, 0, 2, 3), k.transpose(1, 0, 2, 3), v.transpose(1, 0, 2, 3), g_full.transpose(1, 0, 2), beta.transpose(1, 0, 2))
            state0 = jnp.zeros((B, H, DH, DH), x.dtype)
            final_state, o = jax.lax.scan(step, state0, xs)
            o = o.transpose(1, 0, 2, 3).reshape(B, L, NH, H, DH)[:, :, -1]
            gg = (x @ Wg.T).reshape(B, L, H, DH)
            o = o * jax.lax.rsqrt(jnp.mean(o * o, -1, keepdims=True) + EPS)
            o = o * o_norm_w * jax.nn.silu(gg)
            return (o.reshape(B, L, KEY_DIM) @ Wo.T, final_state)

        def _reference_tuple_inner(x, Wq, Wk, Wv, Wb, Wa, Wg, Wo, A_log, dt_bias, conv_q, conv_k, conv_v, o_norm_w):
            return _forward(x, Wq, Wk, Wv, Wb, Wa, Wg, Wo, A_log, dt_bias, conv_q, conv_k, conv_v, o_norm_w)
        return _reference_tuple_inner(x, Wq, Wk, Wv, Wb, Wa, Wg, Wo, A_log, dt_bias, conv_q, conv_k, conv_v, o_norm_w)[0]

    def _L0_xattn_ref(q, kv, seg_id, W_kvc, W_dq, W_uq, W_qr, W_uk, W_kr, W_uv, W_o):
        import jax, jax.numpy as jnp
        import numpy as np
        B, Lq, Lk = (2, 512, 128)
        Q_DIM, KV_DIM = (256, 256)
        H, HD = (16, 128)
        KVC, QC, R = (64, 96, 64)
        LOOKBACK = 8
        NEG = -1e+30

        def _rope(x, L):
            half = x.shape[-1] // 2
            inv_freq = 1.0 / 10000.0 ** (jnp.arange(half, dtype=jnp.float32) / half)
            ang = jnp.arange(L, dtype=jnp.float32)[:, None] * inv_freq
            cos, sin = (jnp.cos(ang), jnp.sin(ang))
            x1, x2 = (x[..., :half], x[..., half:])
            return jnp.concatenate([x1 * cos - x2 * sin, x1 * sin + x2 * cos], axis=-1)
        b, lq, _ = q.shape
        lk = kv.shape[1]
        kv_c = kv @ W_kvc
        q_c = q @ W_dq
        q_nope = (q_c @ W_uq).reshape(b, lq, H, HD).transpose(0, 2, 1, 3)
        q_rope = (q_c @ W_qr).reshape(b, lq, H, R).transpose(0, 2, 1, 3)
        k_nope = (kv_c @ W_uk).reshape(b, lk, H, HD)
        v = (kv_c @ W_uv).reshape(b, lk, H, HD)
        k_rope = kv_c @ W_kr
        q_rope = _rope(q_rope, lq)
        k_rope = _rope(k_rope, lk)
        scale = 1.0 / np.sqrt(HD + R).astype(np.float32)
        scores = (jnp.einsum('bhqd,bkhd->bhqk', q_nope, k_nope) + jnp.einsum('bhqr,bkr->bhqk', q_rope, k_rope)) * scale
        k_ids = jnp.arange(lk)[None, None, :]
        qs = seg_id[:, :, None]
        good = (k_ids <= qs) & (k_ids >= qs - LOOKBACK)
        scores = jnp.where(good[:, None, :, :], scores, NEG)
        attn = jax.nn.softmax(scores, axis=-1)
        out = jnp.einsum('bhqk,bkhd->bqhd', attn, v).reshape(b, lq, H * HD)
        return out @ W_o

    def _L0_ffn_ref(hidden_state, gate_w, gate_scale, up_w, up_scale, down_w, down_scale):
        import jax, jax.numpy as jnp
        import numpy as np
        ZERO_POINT = 128.0

        def _dequant(wq, scale):
            return (wq.astype(jnp.float32) - ZERO_POINT) * scale[:, None]
        Wg = _dequant(gate_w, gate_scale)
        Wu = _dequant(up_w, up_scale)
        Wd = _dequant(down_w, down_scale)
        g = jnp.einsum('bsh,ih->bsi', hidden_state, Wg)
        u = jnp.einsum('bsh,ih->bsi', hidden_state, Wu)
        h = jax.nn.silu(g) * u
        return jnp.einsum('bsi,hi->bsh', h, Wd)
    x = _layernorm(x + _L0_attn_ref(x, L0_attn_Wq, L0_attn_Wk, L0_attn_Wv, L0_attn_Wb, L0_attn_Wa, L0_attn_Wg, L0_attn_Wo, L0_attn_A_log, L0_attn_dt_bias, L0_attn_conv_q, L0_attn_conv_k, L0_attn_conv_v, L0_attn_o_norm_w), axis=-1)
    x = _layernorm(x + _L0_xattn_ref(x, ctx_2048, itok_BxS_0_1023, L0_xattn_W_kvc, L0_xattn_W_dq, L0_xattn_W_uq, L0_xattn_W_qr, L0_xattn_W_uk, L0_xattn_W_kr, L0_xattn_W_uv, L0_xattn_W_o), axis=-1)
    x = _layernorm(x + _L0_ffn_ref(x, L0_ffn_gate_w, L0_ffn_gate_scale, L0_ffn_up_w, L0_ffn_up_scale, L0_ffn_down_w, L0_ffn_down_scale), axis=-1)
    return x

_drawn_inputs = setup_inputs


def setup_inputs(seed=0):
    import zlib

    import numpy as np

    out = dict(_drawn_inputs(seed))
    spreads = {'L0_attn_o_norm_w': (1.0, 0.6)}
    factors = {'L0_attn_Wb': 5.147, 'L0_attn_Wa': 8.0, 'L0_attn_A_log': 3.339, 'L0_attn_dt_bias': 38.623}
    for name, (base, spread) in spreads.items():
        noise = np.random.default_rng([zlib.crc32(name.encode()), seed]).standard_normal(out[name].shape)
        drawn = base * np.exp(spread * noise) if base else spread * noise
        out[name] = jnp.asarray(drawn.astype(out[name].dtype))
    for name, factor in factors.items():
        out[name] = (out[name] * factor).astype(out[name].dtype)
    return out
```

```python
from contextlib import ExitStack

import concourse.bass as bass
from concourse import mybir

F32 = mybir.dt.float32
I32 = mybir.dt.int32
ALU = mybir.AluOpType
ACT = mybir.ActivationFunctionType
AX = mybir.AxisListType

B, S, D = 32, 64, 256
TOK = B * S
KD = D // 128
H, DH, NH, CONV = 8, 128, 2, 4
T = S * NH
GB = 8
NG = B // GB
GT = GB * S
LEVELS = 7
XH, HD, KVC, QC, R = 16, 128, 64, 96, 64
LOOKBACK = 8
FI = 1024
FJ = FI // 128
TILE = 128
NT = TOK // TILE
EPS = 1e-5
NEG = -1e30
ZERO_POINT = 128.0
N_TILES = 6
WCOLS = KD * N_TILES * 128
TAPS = WCOLS
ONORM = WCOLS + 5 * CONV
BLOB = ONORM + 1
K_SHIFT, O_SHIFT = 20, 34


class Engine:

    def __init__(self, name):
        self.name, self.steps, self.index = name, [], {}

    def do(self, name, waits, emit, apart=False):
        assert name not in self.index, name
        self.steps.append((name, waits, emit, apart))
        self.index[name] = len(self.steps)

    def dma(self, name, waits, emit):
        self.steps.append((name, waits, emit, True))


class Phase:

    def __init__(self, nc, ctx, label, names, loads):
        self.q = {n: Engine(n) for n in names}
        self.sem = {n: ctx.enter_context(nc.semaphore(f"{label}_{n}")) for n in names}
        self.per = {n: 16 * k for n, k in loads.items()}
        self.dma = {n: ctx.enter_context(nc.semaphore(f"{label}_dma_{n}")) for n in loads}
        self.tick = ctx.enter_context(nc.semaphore(f"{label}_tick"))

    def close(self):
        self.count = max(len(q.steps) for q in self.q.values()) + 1

    def run(self, eng, name, no, at):
        q = self.q[name]
        turn = eng.snap(no * self.count)
        used = {who for _, waits, _, _ in q.steps for who, _, _ in waits if who in self.dma}
        moved = {who: eng.snap(no * self.per[who]) for who in sorted(used)}
        seen, done = {}, 0
        for _, waits, emit, apart in q.steps:
            for who, what, back in waits:
                if who in self.dma:
                    sem, value, reg = self.dma[who], self.per[who] * (2 - back), moved[who]
                else:
                    sem, reg = self.sem[who], turn
                    value = self.count * (2 - back) + self.q[who].index[what]
                if seen.get(who, -10**9) >= value:
                    continue
                seen[who] = value
                eng.wait_ge(sem, reg + value)
                if apart:
                    eng.sem_inc(self.tick, 1)
            ins = emit(eng, at)
            if ins is not None:
                done += 1
                ins.then_inc(self.sem[name], 1 if done < len(q.index) else self.count - done + 1)

    def open(self, eng, name):
        if name == "sp":
            for who, n in self.per.items():
                eng.sem_inc(self.dma[who], n)
        else:
            eng.sem_inc(self.sem[name], 2 * self.count)


def build(nc, a):
    ctx = ExitStack()
    with ctx:
        resident = ExitStack()
        ctx.enter_context(resident)

        def tensor(stack, name, shape, dt=F32):
            return stack.enter_context(nc.sbuf_tensor(name, shape, dt))

        bank = [ctx.enter_context(nc.psum_tensor(f"bank{i}", [128, 512], F32)) for i in range(8)]
        o_scratch = nc.dram_tensor("o_scratch", (128, NT, H, TILE), F32, kind="Internal").ap()

        ident = tensor(ctx, "ident", [128, 128])
        mask = tensor(ctx, "attn_mask", [128, B, S])
        w_q = tensor(ctx, "w_q_nope_rope", [QC, XH, KVC + R])
        w_qs = tensor(ctx, "w_q_rope_swapped", [QC, XH, R])
        w_uvo = tensor(ctx, "w_uv_o", [128, XH // 2, D])
        w_gate = tensor(ctx, "w_gate", [128, KD, FI])
        w_up = tensor(ctx, "w_up", [128, KD, FI])
        w_down = tensor(ctx, "w_down", [128, FJ, D])

        prologue(nc, a, tensor, bank, ident, mask, w_q, w_qs, w_uvo, w_gate, w_up, w_down)
        with ExitStack() as st:
            delta_phase(nc, st, a, tensor, bank, ident, o_scratch)
        with ExitStack() as st:
            tile_phase(nc, st, a, tensor, bank, ident, mask, w_q, w_qs, w_uvo, w_gate, w_up, w_down, o_scratch)


def prologue(nc, a, tensor, bank, ident, mask, w_q, w_qs, w_uvo, w_gate, w_up, w_down):
    with ExitStack() as st:
        uq = tensor(st, "uq", [128, XH, QC])
        uk = tensor(st, "uk", [128, XH, KVC])
        uv = tensor(st, "uv", [128, XH, KVC])
        wo = tensor(st, "wo", [128, XH, D])
        ints = [tensor(st, f"ints{i}", [128, 2048], I32) for i in range(3)]
        scales = [tensor(st, "gate_scale", [128, FI]), tensor(st, "up_scale", [128, FI]),
                  tensor(st, "down_scale", [128, D])]
        seg_i = tensor(st, "seg_i", [128, B], I32)
        seg = tensor(st, "seg", [128, B])
        keys = tensor(st, "keys", [128, S])
        keys_ahead = tensor(st, "keys_ahead", [128, S])
        below = tensor(st, "below", [128, B, S])
        sem = lambda n: st.enter_context(nc.semaphore(n))
        s_uqk, s_uvo, s_seg, s_int, s_id = sem("p_uqk"), sem("p_uvo"), sem("p_seg"), sem("p_int"), sem("p_id")
        s_pe, s_act, s_dve = sem("p_pe"), sem("p_act"), sem("p_dve")
        with nc.Block() as block:
            @block.sync
            def _(e):
                e.dma_start(uq[:], a["uqT"]).then_inc(s_uqk, 16)
                e.dma_start(uk[:], a["ukT"]).then_inc(s_uqk, 16)
                e.dma_start(uv[:], a["uvT"]).then_inc(s_uvo, 16)
                e.dma_start(wo[:], a["xwo"]).then_inc(s_uvo, 16)
                e.dma_start(w_q[:, :, KVC:], a["qr"]).then_inc(s_id, 16)
                e.dma_start(w_qs[:], a["qrs"]).then_inc(s_id, 16)
                e.dma_start(ident[:], a["ident"]).then_inc(s_id, 16)
                e.wait_ge(s_id, 48)

            @block.scalar
            def _(e):
                e.dma_start(seg_i[:], a["seg"]).then_inc(s_seg, 16)
                e.dma_start(keys[:], a["keys"]).then_inc(s_seg, 16)
                for i, n in enumerate(("gate_w", "up_w", "down_w")):
                    e.dma_start(ints[i][:], a[n]).then_inc(s_int, 16)
                for i, n in enumerate(("gate_scale", "up_scale", "down_scale")):
                    e.dma_start(scales[i][:], a[n]).then_inc(s_int, 16)
                for i in range(2):
                    e.wait_ge(s_pe, i + 1)
                    e.activation(w_q[:, 8 * i:8 * i + 8, 0:KVC],
                                 bank[i][0:QC, :].rearrange("p (h c) -> p h c", c=KVC), ACT.Copy).then_inc(s_act, 1)
                for i in range(4):
                    e.wait_ge(s_pe, i + 3)
                    e.activation(w_uvo[:, 2 * i:2 * i + 2, :],
                                 bank[2 + i][:, :].rearrange("p (h c) -> p h c", c=D), ACT.Copy).then_inc(s_act, 1)

            @block.tensor
            def _(e):
                e.wait_ge(s_uqk, 32)
                for h in range(XH):
                    mm = e.matmul(bank[h // 8][0:QC, (h % 8) * KVC:(h % 8 + 1) * KVC], uq[:, h, :], uk[:, h, :],
                                  start=True, stop=True)
                    if h % 8 == 7:
                        mm.then_inc(s_pe, 1)
                e.wait_ge(s_uvo, 32)
                for h in range(XH):
                    hp, h2 = h // 2, h % 2
                    mm = e.matmul(bank[2 + hp // 2][64 * h2:64 * h2 + 64, (hp % 2) * D:(hp % 2 + 1) * D],
                                  uv[:, h, :], wo[:, h, :], start=True, stop=True)
                    if h % 4 == 3:
                        mm.then_inc(s_pe, 1)

            @block.vector
            def _(e):
                e.wait_ge(s_seg, 32)
                e.tensor_copy(seg[:], seg_i[:]).then_inc(s_dve, 1)
                e.tensor_scalar(keys_ahead[:], keys[:], float(LOOKBACK), None, ALU.add).then_inc(s_dve, 1)
                e.wait_ge(s_dve, 2)
                many = lambda t: t[:, None, :].broadcast_to([128, B, S])
                each = seg[:, :, None].broadcast_to([128, B, S])
                e.tensor_tensor(mask[:], many(keys), each, ALU.is_le).then_inc(s_dve, 1)
                e.tensor_tensor(below[:], many(keys_ahead), each, ALU.is_ge).then_inc(s_dve, 1)
                e.wait_ge(s_dve, 4)
                e.tensor_tensor(mask[:], mask[:], below[:], ALU.mult).then_inc(s_dve, 1)
                e.wait_ge(s_dve, 5)
                e.tensor_scalar(mask[:], mask[:], -1.0, -NEG, ALU.add, ALU.mult).then_inc(s_dve, 1)
                e.wait_ge(s_int, 96)
                for w, i in ((w_gate, 0), (w_up, 1)):
                    for k in range(KD):
                        e.scalar_tensor_tensor(w[:, k, :], ints[i][:, k * FI:(k + 1) * FI], -ZERO_POINT,
                                               scales[i][:], ALU.add, ALU.mult).then_inc(s_dve, 1)
                e.scalar_tensor_tensor(w_down[:], ints[2][:].rearrange("p (j n) -> p j n", n=D), -ZERO_POINT,
                                       scales[2][:, None, :].broadcast_to([128, FJ, D]),
                                       ALU.add, ALU.mult).then_inc(s_dve, 1)


def delta_phase(nc, st, a, tensor, bank, ident, o_scratch):
    t = lambda name, shape, dt=F32: tensor(st, name, shape, dt)
    xT = t("xT", [128, KD, TOK])
    blob = [t(f"head_weights{i}", [128, BLOB]) for i in range(2)]
    level = t("level_masks", [128, LEVELS, T])
    after = t("after", [128, T])
    upto = t("upto", [128, S])
    ones_mean = t("ones_mean", [128, 128])
    ones_q = t("ones_q", [128, 128])
    ones = t("ones", [128, 1])
    decay = t("decay", [128, H, B])
    beta = t("beta", [128, H, B])

    steps_rhs = t("steps_rhs", [128, GB, S])
    consts = ((xT[:], "xT"), (level[:], "level"), (after[:], "after"), (upto[:], "upto"), (ones[:], "ones"),
              (ones_mean[:], "ones_mean"), (ones_q[:], "ones_q"), (steps_rhs[S:], "before"))
    gates(nc, a, tensor, bank, consts, decay, beta)

    conv = [t(f"conv{i}", [128, GB, S]) for i in range(2)]
    kT = t("kT", [128, GB, NH, S])
    vT = t("vT", [128, GB, NH, S])
    qT = t("qT", [128, GB, S])
    gate = t("gate", [128, GT])
    k_sq = t("k_sq", [128, GB, T])
    q_sq = t("q_sq", [128, GT])
    ET = t("ET", [128, GB, S])
    PT = t("PT", [128, GB, NH, S])
    MT = t("MT", [128, GB, S])
    RBV = t("RBV", [128, GB, DH])
    X = t("X", [128, GB, T])
    XT = t("XT", [128, GB, T])
    Y = t("Y", [128, GB, T])
    Z = t("Z", [128, GB, DH])
    small = t("small", [128, 6, GB])
    qn = t("qn", [128, GT])
    o_sq = t("o_sq", [128, GT])
    o_ln = t("o_ln", [128, GT])
    o_rs = t("o_rs", [128, GT])
    oT = t("oT", [128, GT])
    n2, inv, rho, ln_n2, r_k, r_beta = (small[:, i, :] for i in range(6))

    proj, A, Bk, C0, C1 = bank[0:2], bank[2:4], bank[4:6], bank[6], bank[7]
    ph = Phase(nc, st, "delta", ("pe", "act", "dve", "pool", "sp"), {"weights": 1, "out": 1})
    pe, act, dve, pool, sp = (ph.q[n] for n in ("pe", "act", "dve", "pool", "sp"))

    def half(tile, n):
        return tile[:, 4 * n:4 * n + 4]

    def dma(e, at):
        e.dma_start(blob[at["par"]][:], a["head_w"][bass.ds(at["h"], 1)].rearrange("o p n -> p (o n)"))\
            .then_inc(ph.dma["weights"], 16)
    sp.dma("weights", [("dve", "gated", 2)], dma)

    KINDS = ("k0", "k1", "q", "v0", "v1", "g")
    dest = {"k0": kT[:, :, 0, :], "k1": kT[:, :, 1, :], "q": qT[:], "v0": vT[:, :, 0, :], "v1": vT[:, :, 1, :],
            "g": gate[:]}
    readers = {"k0": [("pe", "kq1", 1), ("act", "k_sq", 1)], "k1": [("pe", "kq1", 1), ("act", "k_sq", 1)],
               "q": [("pe", "kq1", 1), ("act", "q_sq", 1)], "v0": [("pe", "vt1", 1)], "v1": [("pe", "vt1", 1)],
               "g": [("dve", "gate_o", 1)]}
    for c, kind in enumerate(KINDS):
        P = proj[c % 2]
        free = {0: ("dve", "conv3_v1", 1), 1: ("act", "silu_g", 1)}.get(c) or ("dve", f"conv3_{KINDS[c - 2]}", 0)

        def project(e, at, c=c, P=P):
            for k in range(KD):
                ins = e.matmul(P[:], blob[at["par"]][:, (k * N_TILES + c) * 128:(k * N_TILES + c + 1) * 128],
                               xT[:, k, bass.ds(at["tok"], GT)], start=(k == 0), stop=(k == KD - 1))
            return ins
        pe.do(f"proj_{kind}", [("weights", None, 0), free], project)
        if kind == "g":
            act.do("silu_g", [("pe", "proj_g", 0)] + readers["g"],
                   lambda e, at: e.activation(gate[:], proj[1][:], ACT.Silu))
            continue
        acc = conv[c % 2]
        tap = lambda at, c, j: blob[at["par"]][:, TAPS + c * CONV + j:TAPS + c * CONV + j + 1]
        acc_free = ("act", f"silu_{KINDS[c - 2]}", 0) if c >= 2 else ("act", f"silu_{('v1', 'v0')[c % 2]}", 1)
        act.do(f"tap_{kind}", [("pe", f"proj_{kind}", 0), acc_free],
               lambda e, at, c=c, P=P, acc=acc, tap=tap: e.activation(
                   acc[:], P[:].rearrange("p (b l) -> p b l", l=S), ACT.Copy, scale=tap(at, c, CONV - 1)))
        for s in range(1, CONV):
            def shifted(e, at, c=c, P=P, acc=acc, s=s, tap=tap):
                return e.scalar_tensor_tensor(acc[:, :, s:], P[:].rearrange("p (b l) -> p b l", l=S)[:, :, 0:S - s],
                                              tap(at, c, CONV - 1 - s), acc[:, :, s:], ALU.mult, ALU.add)
            dve.do(f"conv{s}_{kind}", [("act", f"tap_{kind}", 0) if s == 1 else ("dve", f"conv{s - 1}_{kind}", 0)],
                   shifted)
        if c >= 1:
            p = KINDS[c - 1]
            act.do(f"silu_{p}", [("dve", f"conv3_{p}", 0)] + readers[p],
                   lambda e, at, p=p, acc=conv[(c - 1) % 2]: e.activation(dest[p], acc[:], ACT.Silu))
    act.do("silu_v1", [("dve", "conv3_v1", 0)] + readers["v1"],
           lambda e, at: e.activation(dest["v1"], conv[0][:], ACT.Silu))

    act.do("k_sq", [("act", "silu_k1", 0), ("pe", "norms", 1)],
           lambda e, at: e.activation(k_sq[:], kT[:].rearrange("p b j l -> p b (j l)"), ACT.Square))
    act.do("q_sq", [("act", "silu_q", 0), ("pe", "norms", 1)],
           lambda e, at: e.activation(q_sq[:], qT[:].rearrange("p b l -> p (b l)"), ACT.Square))

    def norms(e, at):
        for b in range(GB):
            e.matmul(C0[:, b:b + 1], k_sq[:, b, :], ones[:], start=True, stop=True)
        return e.matmul(C1[:], ones_q[:], q_sq[:], start=True, stop=True)
    pe.do("norms", [("act", "q_sq", 0), ("dve", "gated", 1), ("dve", "o_var", 1)], norms)
    tiny = 1e-24
    dve.do("n2", [("pe", "norms", 0), ("act", "ln_n2", 1)],
           lambda e, at: e.tensor_scalar(n2, C0[:, 0:GB], tiny, None, ALU.max))
    dve.do("qn", [("pe", "norms", 0), ("dve", "o_var", 1)],
           lambda e, at: e.tensor_scalar(qn[:], C1[:], tiny * EPS * DH, None, ALU.max))
    dve.do("inv", [("dve", "n2", 0)], lambda e, at: e.reciprocal(inv, n2))
    flat = lambda tile, at: tile[:].rearrange("p h b -> p (h b)")[:, bass.ds(at["hb"], GB)]
    dve.do("rho", [("dve", "inv", 0)], lambda e, at: e.tensor_tensor(rho, inv, flat(beta, at), ALU.mult))

    pool.do("steps_rhs", [("pe", "decays", 1)],
            lambda e, at: e.tensor_tensor(steps_rhs[0:S], flat(decay, at)[0:S, :, None].broadcast_to([S, GB, S]),
                                          upto[0:S, None, :].broadcast_to([S, GB, S]), ALU.mult))
    pe.do("decays", [("pool", "steps_rhs", 0), ("dve", "qn", 0)],
          lambda e, at: e.matmul(C1[:], after[:], steps_rhs[:].rearrange("p b l -> p (b l)"), start=True, stop=True))
    act.do("ln_n2", [("dve", "n2", 0), ("act", "r_k", 1)],
           lambda e, at: e.activation(ln_n2, n2, ACT.Ln, scale=float(2 ** K_SHIFT)))
    act.do("r_k", [("act", "ln_n2", 0), ("dve", "r_beta", 1)],
           lambda e, at: e.activation(r_k, ln_n2, ACT.Exp, scale=-0.5))
    act.do("ET", [("pe", "decays", 0), ("dve", "MT", 1), ("dve", "PT1", 1)],
           lambda e, at: e.activation(ET[:].rearrange("p b l -> p (b l)"), C1[:], ACT.Exp))
    dve.do("r_beta", [("act", "r_k", 0)],
           lambda e, at: e.scalar_tensor_tensor(r_beta, r_k, float(2 ** (K_SHIFT // 2)), flat(beta, at),
                                                ALU.mult, ALU.mult))

    def pairs(n):
        return range(4 * n, 4 * n + 4)

    def cols(n, b):
        return slice((b - 4 * n) * 128, (b - 4 * n + 1) * 128)

    def each_pair(n, out, lhs, rhs):
        def emit(e, at):
            for b in pairs(n):
                ins = e.matmul(out[:, cols(n, b)], lhs[:, b], rhs[:, b], start=True, stop=True)
            return ins
        return emit

    keys = kT[:].rearrange("p b j l -> p b (j l)")
    vals = vT[:].rearrange("p b j l -> p b (j l)")
    PTf = PT[:].rearrange("p b j l -> p b (j l)")

    def turned(out, src, n):
        def emit(e, at):
            for b in pairs(n):
                ins = e.transpose(out[:, cols(n, b)], src[:, b], ident[:])
            return ins
        return emit

    for n in range(2):
        pe.do(f"gram{n}", [("act", "silu_k1", 0), ("act", f"Z{n}", 1)],
              each_pair(n, A[n], keys, keys))
    def kq(e, at):
        for b in range(GB):
            ins = e.matmul(C0[:, b * S:(b + 1) * S], keys[:, b], qT[:, b], start=True, stop=True)
        return ins
    pe.do("kq1", [("act", "silu_q", 0), ("dve", "n2", 0)], kq)

    def masked(n, lv):
        for b in pairs(n):
            dve.do(f"Y{lv}_{b}", [("pe", f"gram{n}" if lv == 0 else f"CX{lv}_{n}", 0), ("dve", "rho", 0),
                                 ("pe", f"XY{lv - 1}_{n}", 0) if lv else ("pe", f"XY{LEVELS - 1}_{n}", 1)],
                   lambda e, at, b=b: e.scalar_tensor_tensor(Y[:, b], A[n][:, cols(n, b)], rho[:, b:b + 1],
                                                             level[:, lv, :], ALU.mult, ALU.mult))
    four = lambda ap: ap[:, None, :].broadcast_to([128, 4, 128])
    quad = lambda bk: bk[:].rearrange("p (b s) -> p b s", b=4)

    for n in range(2):
        masked(n, 0)
        pe.do(f"XY0_{n}", [("dve", f"Y0_{4 * n + 3}", 0), ("dve", f"XT{LEVELS - 1}_{n}", 1)], turned(Bk[n], Y, n))
        dve.do(f"X0_{n}", [("dve", f"Y0_{4 * n + 3}", 0)],
               lambda e, at, n=n: e.tensor_tensor(half(X, n), four(ident[:]), half(Y, n), ALU.subtract))
        dve.do(f"PT{n}", [("act", "ET", 0), ("pe", f"gram{n}", 0)],
               lambda e, at, n=n: e.tensor_tensor(half(PT, n), A[n][:].rearrange("p (b j l) -> p b j l", b=4, j=NH),
                                                  half(ET, n)[:, :, None, :].broadcast_to([128, 4, NH, S]), ALU.mult))
        dve.do(f"XT0_{n}", [("pe", f"XY0_{n}", 0), ("pe", f"Z{n}", 1)],
               lambda e, at, n=n: e.tensor_tensor(half(XT, n), four(ident[:]), quad(Bk[n]), ALU.subtract))
    dve.do("MT", [("pe", "kq1", 0), ("act", "ET", 0), ("pe", "o", 1)],
           lambda e, at: e.tensor_tensor(MT[:].rearrange("p b l -> p (b l)"), C0[:],
                                         ET[:].rearrange("p b l -> p (b l)"), ALU.mult))
    for lv in range(1, LEVELS):
        last = lv == LEVELS - 1
        for n in range(2):
            pe.do(f"CX{lv}_{n}", [("dve", f"X{lv - 1}_{n}", 0), ("dve", f"PT{n}", 0)], each_pair(n, A[n], PTf, X))
        for n in range(2):
            masked(n, lv)
        for n in range(2):
            def xy(e, at, n=n, last=last):
                if not last:
                    each_pair(n, A[n], XT, Y)(e, at)
                return each_pair(n, Bk[n], Y, XT)(e, at)
            pe.do(f"XY{lv}_{n}", [("dve", f"Y{lv}_{4 * n + 3}", 0), ("dve", f"XT{lv - 1}_{n}", 0)], xy)
            if not last:
                dve.do(f"X{lv}_{n}", [("pe", f"XY{lv}_{n}", 0)],
                       lambda e, at, n=n: e.tensor_tensor(half(X, n), half(X, n), quad(A[n]), ALU.subtract))
            dve.do(f"XT{lv}_{n}", [("pe", f"XY{lv}_{n}", 0)],
                   lambda e, at, n=n: e.tensor_tensor(half(XT, n), half(XT, n), quad(Bk[n]), ALU.subtract))
    for n in range(2):
        pe.do(f"vt{n}", [("act", "silu_v1", 0), ("dve", f"Y{LEVELS - 1}_{4 * n + 3}", 0)], turned(A[n], vals, n))
        dve.do(f"RBV{n}", [("pe", f"vt{n}", 0), ("dve", "r_beta", 0), ("pe", f"Z{n}", 1)],
               lambda e, at, n=n: e.tensor_tensor(half(RBV, n), quad(A[n]),
                                                  r_beta[:, 4 * n:4 * n + 4, None].broadcast_to([128, 4, DH]),
                                                  ALU.mult))
    for n in range(2):
        pe.do(f"Z{n}", [("dve", f"RBV{n}", 0), ("dve", f"XT{LEVELS - 1}_{n}", 0)], each_pair(n, A[n], XT, RBV))
        act.do(f"Z{n}", [("pe", f"Z{n}", 0), ("pe", "o", 1)],
               lambda e, at, n=n: e.activation(half(Z, n), quad(A[n]), ACT.Copy))

    def out(e, at):
        for b in range(GB):
            ins = e.matmul(C0[:, b * S:(b + 1) * S], Z[:, b], MT[:, b], start=True, stop=True)
        return ins
    pe.do("o", [("act", "Z1", 0), ("dve", "MT", 0)], out)
    act.do("o_sq", [("pe", "o", 0)], lambda e, at: e.activation(o_sq[:], C0[:], ACT.Square))
    pe.do("o_mean", [("act", "o_sq", 0), ("act", "ET", 0)],
          lambda e, at: e.matmul(C1[:], ones_mean[:], o_sq[:], start=True, stop=True))
    dve.do("o_var", [("pe", "o_mean", 0), ("dve", "qn", 0)],
           lambda e, at: e.tensor_tensor(qn[:], C1[:], qn[:], ALU.add))
    act.do("o_ln", [("dve", "o_var", 0)], lambda e, at: e.activation(o_ln[:], qn[:], ACT.Ln, scale=float(2 ** O_SHIFT)))
    act.do("o_rs", [("act", "o_ln", 0), ("dve", "gate_o", 1)],
           lambda e, at: e.activation(o_rs[:], o_ln[:], ACT.Exp, scale=-0.5))
    dve.do("gate_o", [("act", "o_rs", 0), ("act", "silu_g", 0), ("dve", "gated", 1)],
           lambda e, at: e.scalar_tensor_tensor(o_rs[:], gate[:], blob[at["par"]][:, ONORM:ONORM + 1], o_rs[:],
                                                ALU.mult, ALU.mult))
    dve.do("gated", [("dve", "gate_o", 0), ("out", None, 1)],
           lambda e, at: e.scalar_tensor_tensor(oT[:], C0[:], float(2 ** (O_SHIFT // 2)), o_rs[:],
                                                ALU.mult, ALU.mult))

    def dma(e, at):
        e.dma_start(o_scratch.rearrange("v t h n -> v t (h n)")[:, bass.ds(at["tile"], GT // TILE),
                                                               bass.ds(at["h128"], TILE)],
                    oT[:].rearrange("v (t n) -> v t n", n=TILE)).then_inc(ph.dma["out"], 16)
    sp.dma("store", [("dve", "gated", 0)], dma)

    ph.close()
    with nc.Block() as block:
        def program(name):
            def _(e):
                ph.open(e, name)
                with e.Fori(0, NG) as g:
                    with e.Fori(0, H // 2) as hp:
                        for par in range(2):
                            no = g * H + hp * 2 + par
                            h = hp * 2 + par
                            at = {"par": par, "h": h, "tok": g * GT, "hb": h * B + g * GB,
                                  "tile": g * (GT // TILE), "h128": h * TILE}
                            ph.run(e, name, no, at)
                if name == "sp":
                    e.wait_ge(ph.dma["out"], 16 * (NG * H + 1))
            return _
        block.tensor(program("pe"))
        block.scalar(program("act"))
        block.vector(program("dve"))
        block.gpsimd(program("pool"))
        block.sync(program("sp"))


def gates(nc, a, tensor, bank, consts, decay, beta):
    with ExitStack() as st:
        t = lambda name, shape: tensor(st, name, shape)
        xg = t("xg", [128, KD, GT])
        w = t("w_ab", [128, KD, NH, 2 * H])
        dt = t("dt_bias", [128, H])
        rate = t("rate", [128, H])
        raw = t("raw", [128, B * 2 * H])
        z, mag, e_z, w1, w2, p, pos = (t(n, [128, H, B]) for n in ("z", "mag", "e_z", "w1", "w2", "p", "pos"))
        sem = lambda n: st.enter_context(nc.semaphore(n))
        s_const, s_more, s_x, s_pe = sem("g_const"), sem("g_more"), sem("g_x"), sem("g_pe")
        s_act, s_dve, s_raw, s_tick = sem("g_act"), sem("g_dve"), sem("g_raw"), sem("g_tick")
        cols = GB * 2 * H
        rawv = raw[:].rearrange("p (b n) -> p n b", b=B)
        with nc.Block() as block:
            @block.sync
            def _(e):
                e.sem_inc(s_x, 1)
                with e.Fori(0, NG) as g:
                    read = e.snap(g + 1)
                    e.wait_ge(s_pe, read)
                    e.sem_inc(s_tick, 1)
                    e.dma_start(xg[:], a["xT"][:, :, bass.ds(g * GT, GT)]).then_inc(s_x, 16)
                for tile, n in consts:
                    e.dma_start(tile, a[n]).then_inc(s_more, 16)
                e.wait_ge(s_more, 16 * len(consts))

            @block.scalar
            def _(e):
                for tile, n in ((w, "w_ab"), (dt, "dt_bias"), (rate, "A_log")):
                    e.dma_start(tile[:], a[n]).then_inc(s_const, 16)
                e.wait_ge(s_const, 48)
                e.activation(rate[:], rate[:], ACT.Exp).then_inc(s_act, 1)
                e.wait_ge(s_raw, NG + 1)
                e.activation(beta[:], rawv[:, H:, :], ACT.Exp, scale=-1.0).then_inc(s_act, 1)
                e.wait_ge(s_dve, 1)
                e.activation(mag[:], z[:], ACT.Abs).then_inc(s_act, 1)
                e.wait_ge(s_act, 3)
                e.activation(e_z[:], mag[:], ACT.Exp, scale=-1.0).then_inc(s_act, 1)

            @block.tensor
            def _(e):
                e.wait_ge(s_const, 48)
                e.sem_inc(s_pe, 1)
                with e.Fori(0, NG) as g:
                    e.wait_ge(s_x, g * 16 + 17)
                    e.wait_ge(s_raw, g + 1)
                    for b in range(GB):
                        for j in range(NH):
                            for k in range(KD):
                                mm = e.matmul(bank[0][S * j:S * j + S, 2 * H * b:2 * H * (b + 1)],
                                              xg[:, k, b * S:(b + 1) * S], w[:, k, j, :],
                                              start=(k == 0), stop=(k == KD - 1))
                    mm.then_inc(s_pe, 1)

            @block.vector
            def _(e):
                e.sem_inc(s_raw, 1)
                with e.Fori(0, NG) as g:
                    e.wait_ge(s_pe, g + 2)
                    e.tensor_copy(raw[:, bass.ds(g * cols, cols)], bank[0][:, 0:cols]).then_inc(s_raw, 1)
                e.wait_ge(s_const, 48)
                e.wait_ge(s_raw, NG + 1)
                count = [0]

                def step(ins):
                    count[0] += 1
                    ins.then_inc(s_dve, 1)
                    e.wait_ge(s_dve, count[0])

                step(e.tensor_tensor(z[:], rawv[:, 0:H, :], dt[:, :, None].broadcast_to([128, H, B]), ALU.add))
                step(e.tensor_scalar(pos[:], z[:], 0.0, None, ALU.max))
                e.wait_ge(s_act, 4)
                step(e.tensor_scalar(w1[:], e_z[:], 2.0, None, ALU.add))
                step(e.reciprocal(w1[:], w1[:]))
                step(e.tensor_tensor(w1[:], w1[:], e_z[:], ALU.mult))
                step(e.tensor_tensor(w2[:], w1[:], w1[:], ALU.mult))
                step(e.tensor_scalar(p[:], w2[:], 1.0 / 17, None, ALU.mult))
                for k in range(7, 0, -1):
                    step(e.scalar_tensor_tensor(p[:], p[:], 1.0 / (2 * k + 1), w2[:], ALU.add, ALU.mult))
                step(e.scalar_tensor_tensor(p[:], p[:], 1.0, w1[:], ALU.add, ALU.mult))
                step(e.scalar_tensor_tensor(p[:], p[:], 2.0, pos[:], ALU.mult, ALU.add))
                step(e.scalar_tensor_tensor(decay[:], p[:], -1.0, rate[:, :, None].broadcast_to([128, H, B]),
                                            ALU.mult, ALU.mult))
                step(e.tensor_scalar(beta[:], beta[:], 0.5, 0.5, ALU.mult, ALU.add))
                step(e.reciprocal(beta[:], beta[:]))


def tile_phase(nc, st, a, tensor, bank, ident, mask, w_q, w_qs, w_uvo, w_gate, w_up, w_down, o_scratch):
    t = lambda name, shape, dt=F32: tensor(st, name, shape, dt)
    SL = 2
    w_out = t("w_out", [128, H, D])
    w_dq = t("w_dq", [128, KD, QC])
    w_kvc = t("w_kvc", [128, KD, KVC])
    w_kr = t("w_kr", [KVC, 2 * R])
    cos = t("cos", [128, S])
    sin = t("sin", [128, S])
    two = lambda name, shape: [t(f"{name}{i}", shape) for i in range(SL)]
    o_in, x_in, c_in = two("o_in", [128, H, TILE]), two("x_in", [128, D]), two("c_in", [128, KD, TILE])
    res, xn, xnT = two("res", [128, D]), two("xn", [128, D]), two("xnT", [128, KD, TILE])
    stats, mv, rstd = two("stats", [128, 6]), two("mv", [128, 2]), two("rstd", [128, 2])
    qc, kcat, kvtok = two("qc", [QC, TILE]), two("kcat", [128, TILE]), two("kvtok", [128, KVC])
    qcat = two("qcat", [128, 2, XH, S])
    rope1, rope2 = two("rope1", [128, 4 * TILE]), two("rope2", [128, 4 * TILE])
    att = two("att", [128, XH // 2, 2, S])
    attT = two("attT", [128, XH // 2, 2, S])
    high = two("high", [128, XH])
    ctxT = two("ctxT", [128, XH // 2, 2, S])
    hid = att
    gact = attT

    ph = Phase(nc, st, "tile", ("pe", "act", "dve", "pool", "sp"), {"in": 3 * SL, "out": SL})
    pe, act, dve, pool, sp = (ph.q[n] for n in ("pe", "act", "dve", "pool", "sp"))
    rows = lambda ap, at, s: ap[bass.ds(at["tok"] + s * TILE, TILE), :]

    def load(e, at):
        for s in range(SL):
            e.dma_start(o_in[s][:].rearrange("v h n -> v (h n)"),
                        o_scratch.rearrange("v t h n -> v t (h n)")[:, bass.ds(at["tile"] + s, 1), :]
                        .rearrange("v t n -> v (t n)")).then_inc(ph.dma["in"], 16)
            e.dma_start(x_in[s][:], rows(a["x"], at, s)).then_inc(ph.dma["in"], 16)
            e.dma_start(c_in[s][:], a["ctxT"][:, :, bass.ds(at["tok"] + s * TILE, TILE)]).then_inc(ph.dma["in"], 16)
    sp.dma("load", [("pe", f"out{SL - 1}", 1), ("pe", f"kv{SL - 1}", 1), ("dve", f"res0_{SL - 1}", 1)], load)

    def norm(i, s, psum, base, after_pe, out_free):
        dve.do(f"res{i}_{s}", [("pe", after_pe, 0), ("in", None, 0), ("dve", f"xn{(i - 1) % 3}_{s}", 0 if i else 1)],
               lambda e, at: e.tensor_tensor(res[s][:], psum[:, 0:D], base[:], ALU.add))
        dve.do(f"stats{i}_{s}", [("dve", f"res{i}_{s}", 0)], lambda e, at: e.bn_stats(stats[s][:], res[s][:]))
        dve.do(f"mv{i}_{s}", [("dve", f"stats{i}_{s}", 0)], lambda e, at: e.bn_aggr(mv[s][:], stats[s][:]), apart=True)
        dve.do(f"var{i}_{s}", [("dve", f"mv{i}_{s}", 0)],
               lambda e, at: e.tensor_scalar(rstd[s][:, 0:1], mv[s][:, 1:2], EPS, None, ALU.add))
        act.do(f"ln{i}_{s}", [("dve", f"var{i}_{s}", 0)],
               lambda e, at: e.activation(rstd[s][:, 1:2], rstd[s][:, 0:1], ACT.Ln))
        act.do(f"rstd{i}_{s}", [("act", f"ln{i}_{s}", 0)],
               lambda e, at: e.activation(rstd[s][:, 0:1], rstd[s][:, 1:2], ACT.Exp, scale=-0.5))
        dve.do(f"xn{i}_{s}", [("act", f"rstd{i}_{s}", 0)] + out_free,
               lambda e, at: e.tensor_scalar(xn[s][:], res[s][:], mv[s][:, 0:1], rstd[s][:, 0:1],
                                             ALU.subtract, ALU.mult))

    def turn_xn(i, s, bk, free):
        def emit(e, at):
            for k in range(KD):
                ins = e.transpose(bk[:, k * TILE:(k + 1) * TILE], xn[s][:, k * 128:(k + 1) * 128], ident[:])
            return ins
        pe.do(f"xT{i}_{s}", [("dve", f"xn{i}_{s}", 0)] + free, emit)
        act.do(f"xT{i}_{s}", [("pe", f"xT{i}_{s}", 0)],
               lambda e, at: e.activation(xnT[s][:], bk[:, 0:KD * TILE].rearrange("p (k n) -> p k n", k=KD), ACT.Copy))

    def chunks(e, out, lhs, rhs, n):
        for k in range(n):
            ins = e.matmul(out, lhs(k), rhs(k), start=(k == 0), stop=(k == n - 1))
        return ins

    banks = [bank[4 * s:4 * s + 4] for s in range(SL)]
    both = range(SL)
    for s in both:
        a0, b0, c0, d0 = banks[s]
        pe.do(f"out{s}", [("in", None, 0), ("dve", f"res2_{s}", 1)],
              lambda e, at, s=s, a0=a0: chunks(e, a0[:, 0:D], lambda k: o_in[s][:, k, :], lambda k: w_out[:, k, :], H))

        def kv(e, at, s=s, c0=c0):
            chunks(e, c0[0:KVC, 0:TILE], lambda k: w_kvc[:, k, :], lambda k: c_in[s][:, k, :], KD)
            return chunks(e, c0[:, TILE:TILE + KVC], lambda k: c_in[s][:, k, :], lambda k: w_kvc[:, k, :], KD)
        pe.do(f"kv{s}", [("in", None, 0), ("dve", f"hid1_{s}", 1)], kv)
        act.do(f"kcat{s}", [("pe", f"kv{s}", 0), ("pe", f"score{s}", 1)],
               lambda e, at, s=s, c0=c0: e.activation(kcat[s][0:KVC, :], c0[0:KVC, 0:TILE], ACT.Copy))
        act.do(f"kvtok{s}", [("pe", f"kv{s}", 0), ("pe", f"mix{s}", 1)],
               lambda e, at, s=s, c0=c0: e.activation(kvtok[s][:], c0[:, TILE:TILE + KVC], ACT.Copy))
        norm(0, s, a0, x_in[s], f"out{s}", [("dve", f"xn2_{s}", 1), ("out", None, 1)])

        def kr(e, at, s=s, d0=d0):
            e.matmul(d0[64:128, 0:TILE], w_kr[:, 0:R], kcat[s][0:KVC, :], start=True, stop=True)
            return e.matmul(d0[64:128, TILE:2 * TILE], w_kr[:, R:], kcat[s][0:KVC, :], start=True, stop=True)
        pe.do(f"kr{s}", [("act", f"kcat{s}", 0), ("dve", f"hid1_{s}", 1)], kr, apart=True)
    seq = lambda ap: ap.rearrange("p (b k) -> p b k", k=S)

    def table(tab, n):
        return tab[64:128, None, :].broadcast_to([64, n, S])
    for s in both:
        d0 = banks[s][3]
        dve.do(f"krc{s}", [("pe", f"kr{s}", 0)],
               lambda e, at, s=s, d0=d0: e.tensor_tensor(seq(rope1[s][64:128, 0:TILE]), seq(d0[64:128, 0:TILE]),
                                                         table(cos, 2), ALU.mult))
        dve.do(f"krs{s}", [("pe", f"kr{s}", 0)],
               lambda e, at, s=s, d0=d0: e.tensor_tensor(seq(rope2[s][64:128, 0:TILE]),
                                                         seq(d0[64:128, TILE:2 * TILE]), table(sin, 2), ALU.mult))
        pool.do(f"kr{s}", [("dve", f"krs{s}", 0), ("pe", f"score{s}", 1)],
                lambda e, at, s=s: e.tensor_tensor(kcat[s][64:128, :], rope1[s][64:128, 0:TILE],
                                                   rope2[s][64:128, 0:TILE], ALU.add))
    for s in both:
        a0, b0, c0, d0 = banks[s]
        turn_xn(0, s, b0, [("act", f"silu1_{s}", 1)])
    for s in both:
        a0, b0, c0, d0 = banks[s]
        pe.do(f"qc{s}", [("act", f"xT0_{s}", 0), ("act", f"kvtok{s}", 0)],
              lambda e, at, s=s, c0=c0: chunks(e, c0[0:QC, 0:TILE], lambda k: w_dq[:, k, :],
                                               lambda k: xnT[s][:, k, :], KD))
        act.do(f"qc{s}", [("pe", f"qc{s}", 0), ("pe", f"q3_{s}", 1)],
               lambda e, at, s=s, c0=c0: e.activation(qc[s][:], c0[0:QC, 0:TILE], ACT.Copy))
    for r in range(4):
        for s in both:
            m0, m1 = banks[s][0:2] if r % 2 == 0 else banks[s][2:4]
            free = [("act", f"nope{r - 2}_{s}", 0), ("dve", f"qs{r - 2}_{s}", 0)] if r >= 2 else \
                [("act", f"xT0_{s}", 0), ("dve", f"res0_{s}", 0), ("act", f"qc{s}", 0), ("dve", f"krs{s}", 0)]

            def q_heads(e, at, r=r, s=s, m0=m0, m1=m1):
                for i in range(4):
                    e.matmul(m0[:, i * TILE:(i + 1) * TILE], w_q[:, 4 * r + i, :], qc[s][:], start=True, stop=True)
                    ins = e.matmul(m1[64:128, i * TILE:(i + 1) * TILE], w_qs[:, 4 * r + i, :], qc[s][:],
                                   start=True, stop=True)
                return ins
            pe.do(f"q{r}_{s}", [("act", f"qc{s}", 0)] + free, q_heads)
            act.do(f"nope{r}_{s}", [("pe", f"q{r}_{s}", 0), ("pe", f"score{s}", 1)],
                   lambda e, at, r=r, s=s, m0=m0: e.activation(
                       qcat[s][0:KVC, :, 4 * r:4 * r + 4, :],
                       m0[0:KVC, :].rearrange("p (h b q) -> p b h q", h=4, b=2), ACT.Copy))
            rope_free = ("pool", f"rope{r - 1}_{s}" if r else f"kr{s}", 0)
            dve.do(f"qcos{r}_{s}", [("pe", f"q{r}_{s}", 0), rope_free],
                   lambda e, at, s=s, m0=m0: e.tensor_tensor(seq(rope1[s][64:128, :]), seq(m0[64:128, :]),
                                                             table(cos, 8), ALU.mult))
            dve.do(f"qs{r}_{s}", [("pe", f"q{r}_{s}", 0), rope_free],
                   lambda e, at, s=s, m1=m1: e.tensor_tensor(seq(rope2[s][64:128, :]), seq(m1[64:128, :]),
                                                             table(sin, 8), ALU.mult))
            view = lambda ap: ap.rearrange("p (h b q) -> p b h q", h=4, b=2)

            def rope(e, at, r=r, s=s, view=view):
                return e.tensor_tensor(qcat[s][64:128, :, 4 * r:4 * r + 4, :], view(rope1[s][64:128, :]),
                                       view(rope2[s][64:128, :]), ALU.add)
            pool.do(f"rope{r}_{s}", [("dve", f"qs{r}_{s}", 0), ("pe", f"score{s}", 1)], rope)
    scale = float(1.0 / (HD + R) ** 0.5)
    for s in both:
        a0, b0, c0, d0 = banks[s]

        def score(e, at, s=s):
            for b in range(2):
                for hp in range(XH // 2):
                    ins = e.matmul(banks[s][b][:, hp * S:(hp + 1) * S], qcat[s][:, b, 2 * hp:2 * hp + 2, :],
                                   kcat[s][:, b * S:(b + 1) * S], start=True, stop=True)
            return ins
        pe.do(f"score{s}", [("act", f"nope3_{s}", 0), ("pool", f"rope3_{s}", 0), ("dve", f"qs2_{s}", 0)], score)
        for b in range(2):
            dve.do(f"mask{b}_{s}", [("pe", f"score{s}", 0), ("pe", f"down{s}", 1)],
                   lambda e, at, s=s, b=b: e.scalar_tensor_tensor(
                       att[s][:, :, b, :], banks[s][b][:].rearrange("p (h k) -> p h k", k=S), scale,
                       mask[:, bass.ds(at["seq"] + 2 * s + b, 1), :].broadcast_to([128, XH // 2, S]),
                       ALU.mult, ALU.add))
    for s in both:
        rows16 = lambda tile: tile[:].rearrange("p h b k -> p (h b) k")
        wide = lambda ap: ap[:, :, None].broadcast_to([128, XH, S])
        dve.do(f"high{s}", [("dve", f"mask1_{s}", 0)],
               lambda e, at, s=s: e.tensor_reduce(high[s][:], rows16(att[s]), AX.X, ALU.max))
        dve.do(f"shift{s}", [("dve", f"high{s}", 0)],
               lambda e, at, s=s: e.tensor_tensor(rows16(att[s]), rows16(att[s]), wide(high[s]), ALU.subtract))
        act.do(f"exp{s}", [("dve", f"shift{s}", 0)],
               lambda e, at, s=s: e.activation(rows16(att[s]), rows16(att[s]), ACT.Exp))
    for s in both:
        dve.do(f"sum{s}", [("act", f"exp{s}", 0)],
               lambda e, at, s=s: e.tensor_reduce(high[s][:], rows16(att[s]), AX.X, ALU.add))
        dve.do(f"rsum{s}", [("dve", f"sum{s}", 0)], lambda e, at, s=s: e.reciprocal(high[s][:], high[s][:]))
        dve.do(f"prob{s}", [("dve", f"rsum{s}", 0)],
               lambda e, at, s=s: e.tensor_tensor(rows16(att[s]), rows16(att[s]), wide(high[s]), ALU.mult))
    for s in both:
        def turn_att(e, at, s=s):
            for hp in range(XH // 2):
                ins = e.transpose(banks[s][2 + hp // 4][:, (hp % 4) * 128:(hp % 4 + 1) * 128],
                                  att[s][:, hp].rearrange("p b k -> p (b k)"), ident[:])
            return ins
        pe.do(f"attT{s}", [("dve", f"prob{s}", 0), ("dve", f"qs3_{s}", 0), ("act", f"nope3_{s}", 0)], turn_att)
        for i in range(2):
            act.do(f"attT{i}_{s}", [("pe", f"attT{s}", 0), ("dve", f"hid1_{s}", 1)],
                   lambda e, at, s=s, i=i: e.activation(
                       attT[s][:, 4 * i:4 * i + 4], banks[s][2 + i][:].rearrange("p (h c q) -> p h c q", h=4, c=2),
                       ACT.Copy))

        def mix(e, at, s=s):
            for b in range(2):
                for h2 in range(2):
                    ins = e.matmul(banks[s][b][64 * h2:64 * h2 + 64, :], kvtok[s][64 * b:64 * b + 64, :],
                                   attT[s][64 * b:64 * b + 64, :, h2, :], start=True, stop=True)
            return ins
        pe.do(f"mix{s}", [("act", f"attT1_{s}", 0), ("dve", f"mask1_{s}", 0)], mix, apart=True)
        for b in range(2):
            act.do(f"ctx{b}_{s}", [("pe", f"mix{s}", 0), ("pe", f"cross{s}", 1)],
                   lambda e, at, s=s, b=b: e.activation(ctxT[s][:, :, b, :],
                                                        banks[s][b][:].rearrange("p (h q) -> p h q", q=S), ACT.Copy))
    for s in both:
        c0, d0 = banks[s][2:4]
        pe.do(f"cross{s}", [("act", f"ctx1_{s}", 0), ("act", f"attT0_{s}", 0)],
              lambda e, at, s=s, c0=c0: chunks(e, c0[:, 0:D],
                                               lambda k: ctxT[s][:, k].rearrange("p b q -> p (b q)"),
                                               lambda k: w_uvo[:, k, :], XH // 2))
        norm(1, s, c0, xn[s], f"cross{s}", [("act", f"xT0_{s}", 0)])
        turn_xn(1, s, d0, [("act", f"attT1_{s}", 0)])
    for s in both:
        def ffn(e, at, s=s):
            for i, w in ((0, w_gate), (2, w_up)):
                for j in range(FJ):
                    ins = chunks(e, banks[s][i + j // 4][:, (j % 4) * TILE:(j % 4 + 1) * TILE],
                                 lambda k: w[:, k, j * 128:(j + 1) * 128], lambda k: xnT[s][:, k, :], KD)
            return ins
        pe.do(f"ffn{s}", [("act", f"xT1_{s}", 0), ("act", f"ctx1_{s}", 0), ("dve", f"res1_{s}", 0)], ffn)
    flat = lambda tile: tile[:].rearrange("p h b k -> p (h b k)")
    for s in both:
        for i in range(2):
            act.do(f"silu{i}_{s}", [("pe", f"ffn{s}", 0), ("pe", f"mix{s}", 0)],
                   lambda e, at, s=s, i=i: e.activation(flat(gact[s])[:, 512 * i:512 * (i + 1)], banks[s][i][:],
                                                        ACT.Silu))
            dve.do(f"hid{i}_{s}", [("act", f"silu{i}_{s}", 0), ("pe", f"attT{s}", 0)],
                   lambda e, at, s=s, i=i: e.tensor_tensor(flat(hid[s])[:, 512 * i:512 * (i + 1)],
                                                           flat(gact[s])[:, 512 * i:512 * (i + 1)],
                                                           banks[s][2 + i][:], ALU.mult))
    for s in both:
        a0 = banks[s][0]
        pe.do(f"down{s}", [("dve", f"hid1_{s}", 0), ("act", f"silu0_{s}", 0)],
              lambda e, at, s=s, a0=a0: chunks(e, a0[:, 0:D], lambda k: flat(hid[s])[:, k * 128:(k + 1) * 128],
                                               lambda k: w_down[:, k, :], FJ))
        norm(2, s, a0, xn[s], f"down{s}", [("act", f"xT1_{s}", 0)])

    def store(e, at):
        for s in range(SL):
            e.dma_start(rows(a["y"], at, s), xn[s][:]).then_inc(ph.dma["out"], 8 * 2)
    sp.dma("store", [("dve", f"xn2_{s}", 0) for s in both], store)

    ph.close()
    with nc.Block() as block:
        loads = ((w_out, "w_out"), (w_dq, "w_dq"), (w_kvc, "w_kvc"), (w_kr, "w_kr"), (cos, "cos"), (sin, "sin"))
        s_load = st.enter_context(nc.semaphore("tile_weights"))

        def program(name):
            def _(e):
                if name == "sp":
                    for tile, n in loads:
                        e.dma_start(tile[:], a[n]).then_inc(s_load, 16)
                else:
                    e.wait_ge(s_load, 16 * len(loads))
                ph.open(e, name)
                with e.Fori(0, NT // SL) as i:
                    at = {"tile": i * SL, "tok": i * (SL * TILE), "seq": i * (SL * 2)}
                    ph.run(e, name, i + 0, at)
                if name == "sp":
                    e.wait_ge(ph.dma["out"], 16 * (NT + SL))
            return _
        block.tensor(program("pe"))
        block.scalar(program("act"))
        block.vector(program("dve"))
        block.gpsimd(program("pool"))
        block.sync(program("sp"))


def shape_constants():
    import numpy as np
    f = np.float32
    p = np.arange(T)
    step = NH * (p % S) + p // S
    level = np.zeros((T, LEVELS, T), f)
    for lv in range(LEVELS):
        bt, bs = step[:, None] >> lv, step[None, :] >> lv
        level[:, lv, :] = (bt == bs + 1) & (bt % 2 == 1)
    token = p % S
    u = np.arange(S)
    after = np.zeros((T, T), f)
    after[:S] = u[:, None] > token[None, :]
    after[S:] = u[:, None] == token[None, :]
    upto = np.zeros((128, S), f)
    upto[:S] = u[:, None] <= u[None, :]
    before = np.tile((u[None, :] < u[:, None])[:, None, :], (1, GB, 1)).astype(f) * f(-30000.0)
    half = R // 2
    inv_freq = (f(1.0) / f(10000.0) ** (np.arange(half, dtype=f) / f(half))).astype(f)
    ang = np.arange(S, dtype=f)[:, None] * inv_freq
    c, s = np.cos(ang).T, np.sin(ang).T
    cos, sin = np.zeros((128, S), f), np.zeros((128, S), f)
    cos[64:] = np.concatenate([c, c])
    sin[64:] = np.concatenate([-s, s])
    return {
        "ident": np.eye(128, dtype=f), "level": level, "after": after, "upto": upto, "before": before,
        "cos": cos, "sin": sin, "keys": np.tile(np.arange(S, dtype=f), (128, 1)),
        "ones": np.ones((128, 1), f), "ones_mean": np.full((128, 128), 1.0 / DH, f),
        "ones_q": np.full((128, 128), EPS * DH, f),
    }


def kernel(**inputs):
    import numpy as np
    import concourse.bacc as bacc
    from concourse.bass_utils import run_bass_kernel_spmd

    i = {k.replace("L0_", ""): np.asarray(v) for k, v in inputs.items()}
    tile = lambda w, n: np.ascontiguousarray(w.reshape(-1, 128, n).transpose(1, 0, 2))
    arrays = dict(shape_constants())
    x = np.ascontiguousarray(i["x"].reshape(TOK, D))
    arrays["x"] = x
    arrays["xT"] = tile(x.T, TOK)
    arrays["ctxT"] = tile(i["ctx_2048"].reshape(TOK, D).T, TOK)
    heads = lambda w, n: w.reshape(n, H, DH, -1)
    wk, wv = heads(i["attn_Wk"], NH), heads(i["attn_Wv"], NH)
    wq, wg = heads(i["attn_Wq"], 1), heads(i["attn_Wg"], 1)
    w6 = np.stack([wk[0], wk[1], wq[0], wv[0], wv[1], wg[0]])
    w6 = w6.reshape(6, H, DH, KD, 128).transpose(1, 4, 3, 0, 2).reshape(H, 128, WCOLS)
    ck, cv, cq = heads(i["attn_conv_k"], NH), heads(i["attn_conv_v"], NH), heads(i["attn_conv_q"], 1)
    taps = np.stack([ck[0], ck[1], cq[0], cv[0], cv[1]]).transpose(1, 2, 0, 3).reshape(H, 128, 5 * CONV)
    onorm = np.broadcast_to(i["attn_o_norm_w"][None, :, None], (H, DH, 1))
    arrays["head_w"] = np.concatenate([w6, taps, onorm], axis=2)
    wa, wb = i["attn_Wa"], i["attn_Wb"].reshape(NH, H, D)
    ab = np.stack([np.concatenate([wa, wb[j]]) for j in range(NH)])
    arrays["w_ab"] = np.ascontiguousarray(ab.reshape(NH, 2 * H, KD, 128).transpose(3, 2, 0, 1))
    arrays["dt_bias"] = np.ascontiguousarray(np.broadcast_to(i["attn_dt_bias"], (128, H)))
    arrays["A_log"] = np.ascontiguousarray(np.broadcast_to(i["attn_A_log"], (128, H)))
    arrays["w_out"] = tile(i["attn_Wo"].T, D)
    arrays["seg"] = np.ascontiguousarray(np.concatenate([i["itok_BxS_0_1023"].T] * 2))
    by_head = lambda w: np.ascontiguousarray(w.reshape(-1, XH, HD).transpose(2, 1, 0))
    arrays["uqT"], arrays["ukT"], arrays["uvT"] = (by_head(i[f"xattn_W_{n}"]) for n in ("uq", "uk", "uv"))
    arrays["xwo"] = tile(i["xattn_W_o"], D)
    qr = i["xattn_W_qr"].reshape(QC, XH, R)
    swap = lambda w: np.concatenate([w[..., R // 2:], w[..., :R // 2]], axis=-1)
    arrays["qr"], arrays["qrs"] = qr, swap(qr)
    arrays["w_kr"] = np.concatenate([i["xattn_W_kr"], swap(i["xattn_W_kr"])], axis=1)
    arrays["w_dq"], arrays["w_kvc"] = tile(i["xattn_W_dq"], QC), tile(i["xattn_W_kvc"], KVC)
    for n in ("gate", "up"):
        arrays[f"{n}_w"] = tile(i[f"ffn_{n}_w"].T, FI).reshape(128, KD * FI)
        arrays[f"{n}_scale"] = np.ascontiguousarray(np.broadcast_to(i[f"ffn_{n}_scale"], (128, FI)))
    arrays["down_w"] = tile(i["ffn_down_w"].T, D).reshape(128, FJ * D)
    arrays["down_scale"] = np.ascontiguousarray(np.broadcast_to(i["ffn_down_scale"], (128, D)))

    nc = bacc.Bacc("TRN2", target_bir_lowering=False, num_devices=1)
    arrays = {n: np.ascontiguousarray(v) for n, v in arrays.items()}
    a = {n: nc.dram_tensor(f"in_{n}", v.shape, mybir.dt.from_np(v.dtype), kind="ExternalInput").ap()
         for n, v in arrays.items()}
    a["y"] = nc.dram_tensor("out_y", (TOK, D), F32, kind="ExternalOutput").ap()
    build(nc, a)
    r = run_bass_kernel_spmd(nc, [{f"in_{n}": v for n, v in arrays.items()}], core_ids=[0])
    return r.results[0]["out_y"].reshape(B, S, D)
```

```python
from contextlib import ExitStack

import concourse.bass as bass
from concourse import mybir

F32 = mybir.dt.float32
I32 = mybir.dt.int32
ALU = mybir.AluOpType
ACT = mybir.ActivationFunctionType
AX = mybir.AxisListType

B, S, D = 32, 64, 256
TOK = B * S
KD = D // 128
H, DH, NH, CONV = 8, 128, 2, 4
T = S * NH
GB = 8
NG = B // GB
GT = GB * S
LEVELS = 7
XH, HD, KVC, QC, R = 16, 128, 64, 96, 64
LOOKBACK = 8
FI = 1024
FJ = FI // 128
TILE = 128
NT = TOK // TILE
EPS = 1e-5
NEG = -1e30
MASKED = -30000.0
ZERO_POINT = 128.0
N_TILES = 6
WCOLS = KD * N_TILES * 128
TAPS = WCOLS
BLOB = TAPS + 5 * CONV
K_SHIFT, O_SHIFT = 20, 34


class Engine:

    def __init__(self, name):
        self.name, self.steps, self.index, self.stage = name, [], {}, {}

    def do(self, name, waits, emit, apart=False, stage=0):
        assert name not in self.index, name
        self.index[name] = len(self.index) + 1
        self.stage[name] = stage
        self.steps.append((name, waits, emit, apart, stage))

    def dma(self, name, waits, emit, stage=0):
        self.steps.append((name, waits, emit, True, stage))


class Phase:

    def __init__(self, nc, ctx, label, names, loads):
        self.q = {n: Engine(n) for n in names}
        self.sem = {n: ctx.enter_context(nc.semaphore(f"{label}_{n}")) for n in names}
        self.per = {n: 16 * k for n, k in loads.items()}
        self.dma = {n: ctx.enter_context(nc.semaphore(f"{label}_dma_{n}")) for n in loads}
        self.tick = ctx.enter_context(nc.semaphore(f"{label}_tick"))

    def close(self):
        self.count = max(len(q.index) for q in self.q.values()) + 1

    def run(self, eng, name, no, at, stages=(-1, 0, 1)):
        q = self.q[name]
        steps = [x for x in q.steps if x[4] in stages]
        used = {who for _, waits, _, _, _ in steps for who, _, _ in waits}
        fixed = isinstance(no, int)
        base = {who: no * self.per[who] for who in sorted(used) if who in self.dma}
        turn = no * self.count
        if not fixed:
            turn = eng.snap(turn)
            base = {who: eng.snap(v) for who, v in base.items()}
        names = [x[0] for x in steps if x[0] in q.index]
        seen, done = {}, 0
        for step, waits, emit, apart, _ in steps:
            for who, what, back in waits:
                if back == 0 and who in self.q and self.q[who].stage[what] not in stages:
                    continue
                if who in self.dma:
                    sem, value, reg = self.dma[who], self.per[who] * (2 - back), base[who]
                else:
                    sem, reg = self.sem[who], turn
                    value = self.count * (2 - back) + self.q[who].index[what]
                if seen.get(who, -10**9) >= value:
                    continue
                seen[who] = value
                eng.wait_ge(sem, reg + value)
                if apart:
                    eng.sem_inc(self.tick, 1)
            ins = emit(eng, at)
            if step in q.index:
                to = self.count if step == names[-1] else q.index[step]
                ins.then_inc(self.sem[name], to - done)
                done = to

    def open(self, eng, name, first, moves):
        if name == "sp":
            for who, n in self.per.items():
                eng.sem_inc(self.dma[who], n * (1 + moves[who]))
        else:
            eng.sem_inc(self.sem[name], (2 + first) * self.count)


def build(nc, a):
    ctx = ExitStack()
    with ctx:
        resident = ExitStack()
        ctx.enter_context(resident)

        def tensor(stack, name, shape, dt=F32):
            return stack.enter_context(nc.sbuf_tensor(name, shape, dt))

        bank = [ctx.enter_context(nc.psum_tensor(f"bank{i}", [128, 512], F32)) for i in range(8)]
        o_scratch = nc.dram_tensor("o_scratch", (128, NT, H, TILE), F32, kind="Internal").ap()

        ident = tensor(ctx, "ident", [128, 128])
        mask = tensor(ctx, "attn_mask", [128, B, S])
        w_q = tensor(ctx, "w_q_nope_rope", [QC, XH, KVC + R])
        w_qs = tensor(ctx, "w_q_rope_swapped", [QC, XH, R])
        w_uvo = tensor(ctx, "w_uv_o", [128, XH // 2, D])
        w_gate = tensor(ctx, "w_gate", [128, KD, FI])
        w_up = tensor(ctx, "w_up", [128, KD, FI])
        w_down = tensor(ctx, "w_down", [128, FJ, D])

        prologue(nc, a, tensor, bank, ident, mask, w_q, w_qs, w_uvo, w_gate, w_up, w_down)
        with ExitStack() as st:
            delta_phase(nc, st, a, tensor, bank, ident, o_scratch)
        with ExitStack() as st:
            tile_phase(nc, st, a, tensor, bank, ident, mask, w_q, w_qs, w_uvo, w_gate, w_up, w_down, o_scratch)


def prologue(nc, a, tensor, bank, ident, mask, w_q, w_qs, w_uvo, w_gate, w_up, w_down):
    with ExitStack() as st:
        uq = tensor(st, "uq", [128, XH, QC])
        uk = tensor(st, "uk", [128, XH, KVC])
        uv = tensor(st, "uv", [128, XH, KVC])
        wo = tensor(st, "wo", [128, XH, D])
        ints = [tensor(st, f"ints{i}", [128, 2048], I32) for i in range(3)]
        scales = [tensor(st, "gate_scale", [128, FI]), tensor(st, "up_scale", [128, FI]),
                  tensor(st, "down_scale", [128, D])]
        seg_i = tensor(st, "seg_i", [128, B], I32)
        seg = tensor(st, "seg", [128, B])
        keys = tensor(st, "keys", [128, S])
        keys_ahead = tensor(st, "keys_ahead", [128, S])
        below = tensor(st, "below", [128, B, S])
        sem = lambda n: st.enter_context(nc.semaphore(n))
        s_uqk, s_uvo, s_seg, s_int, s_id = sem("p_uqk"), sem("p_uvo"), sem("p_seg"), sem("p_int"), sem("p_id")
        s_pe, s_act, s_dve = sem("p_pe"), sem("p_act"), sem("p_dve")
        with nc.Block() as block:
            @block.sync
            def _(e):
                e.dma_start(uq[:], a["uqT"]).then_inc(s_uqk, 16)
                e.dma_start(uk[:], a["ukT"]).then_inc(s_uqk, 16)
                e.dma_start(uv[:], a["uvT"]).then_inc(s_uvo, 16)
                e.dma_start(wo[:], a["xwo"]).then_inc(s_uvo, 16)
                e.dma_start(w_q[:, :, KVC:], a["qr"]).then_inc(s_id, 16)
                e.dma_start(w_qs[:], a["qrs"]).then_inc(s_id, 16)
                e.dma_start(ident[:], a["ident"]).then_inc(s_id, 16)
                e.wait_ge(s_id, 48)

            @block.scalar
            def _(e):
                e.dma_start(seg_i[:], a["seg"]).then_inc(s_seg, 16)
                e.dma_start(keys[:], a["keys"]).then_inc(s_seg, 16)
                for i, n in enumerate(("gate_w", "up_w", "down_w")):
                    e.dma_start(ints[i][:], a[n]).then_inc(s_int, 16)
                for i, n in enumerate(("gate_scale", "up_scale", "down_scale")):
                    e.dma_start(scales[i][:], a[n]).then_inc(s_int, 16)
                for i in range(2):
                    e.wait_ge(s_pe, i + 1)
                    e.activation(w_q[:, 8 * i:8 * i + 8, 0:KVC],
                                 bank[i][0:QC, :].rearrange("p (h c) -> p h c", c=KVC), ACT.Copy).then_inc(s_act, 1)
                for i in range(4):
                    e.wait_ge(s_pe, i + 3)
                    e.activation(w_uvo[:, 2 * i:2 * i + 2, :],
                                 bank[2 + i][:, :].rearrange("p (h c) -> p h c", c=D), ACT.Copy).then_inc(s_act, 1)

            @block.tensor
            def _(e):
                e.wait_ge(s_uqk, 32)
                for h in range(XH):
                    mm = e.matmul(bank[h // 8][0:QC, (h % 8) * KVC:(h % 8 + 1) * KVC], uq[:, h, :], uk[:, h, :],
                                  start=True, stop=True)
                    if h % 8 == 7:
                        mm.then_inc(s_pe, 1)
                e.wait_ge(s_uvo, 32)
                for h in range(XH):
                    hp, h2 = h // 2, h % 2
                    mm = e.matmul(bank[2 + hp // 2][64 * h2:64 * h2 + 64, (hp % 2) * D:(hp % 2 + 1) * D],
                                  uv[:, h, :], wo[:, h, :], start=True, stop=True)
                    if h % 4 == 3:
                        mm.then_inc(s_pe, 1)

            @block.vector
            def _(e):
                e.wait_ge(s_seg, 32)
                e.tensor_copy(seg[:], seg_i[:]).then_inc(s_dve, 1)
                e.tensor_scalar(keys_ahead[:], keys[:], float(LOOKBACK), None, ALU.add).then_inc(s_dve, 1)
                e.wait_ge(s_dve, 2)
                many = lambda t: t[:, None, :].broadcast_to([128, B, S])
                each = seg[:, :, None].broadcast_to([128, B, S])
                e.tensor_tensor(mask[:], many(keys), each, ALU.is_le).then_inc(s_dve, 1)
                e.tensor_tensor(below[:], many(keys_ahead), each, ALU.is_ge).then_inc(s_dve, 1)
                e.wait_ge(s_dve, 4)
                e.tensor_tensor(mask[:], mask[:], below[:], ALU.mult).then_inc(s_dve, 1)
                e.wait_ge(s_dve, 5)
                e.tensor_scalar(mask[:], mask[:], -1.0, -NEG, ALU.add, ALU.mult).then_inc(s_dve, 1)
                e.wait_ge(s_int, 96)
                for w, i in ((w_gate, 0), (w_up, 1)):
                    for k in range(KD):
                        e.scalar_tensor_tensor(w[:, k, :], ints[i][:, k * FI:(k + 1) * FI], -ZERO_POINT,
                                               scales[i][:], ALU.add, ALU.mult).then_inc(s_dve, 1)
                e.scalar_tensor_tensor(w_down[:], ints[2][:].rearrange("p (j n) -> p j n", n=D), -ZERO_POINT,
                                       scales[2][:, None, :].broadcast_to([128, FJ, D]),
                                       ALU.add, ALU.mult).then_inc(s_dve, 1)


def delta_phase(nc, st, a, tensor, bank, ident, o_scratch):
    t = lambda name, shape, dt=F32: tensor(st, name, shape, dt)
    xT = t("xT", [128, KD, TOK])
    blob = [t(f"head_weights{i}", [128, BLOB]) for i in range(2)]
    level = t("level_masks", [128, LEVELS, T // 2])
    after = t("after", [128, T])
    upto = t("upto", [128, S])
    ones_mean = t("ones_mean", [128, 128])
    ones_q = t("ones_q", [128, 128])
    ones = t("ones", [128, 1])
    onorm = t("o_norm_w", [128, 1])
    decay = t("decay", [128, H, B])
    beta = t("beta", [128, H, B])
    consts = ((xT[:], "xT"), (level[:], "level"), (after[:], "after"), (upto[:], "upto"), (ones[:], "ones"),
              (ones_mean[:], "ones_mean"), (ones_q[:], "ones_q"), (onorm[:], "o_norm_w"))
    gates(nc, a, tensor, bank, consts, decay, beta)

    two = lambda name, shape: [t(f"{name}{i}", shape) for i in range(2)]
    kT, vT, qT = two("kT", [128, GB, S, NH]), two("vT", [128, GB, S, NH]), two("qT", [128, GB, S])
    gate, ET, qn, small = two("gate", [128, GT]), two("ET", [128, GB, S]), two("qn", [128, GT]), two("small", [128, 6, GB])
    conv = two("conv", [128, GB, S])
    k_sq = t("k_sq", [128, GB, T])
    q_sq = t("q_sq", [128, GT])
    steps_rhs = t("steps_rhs", [128, GB, S])
    PT = t("PT", [128, GB, T])
    MT = t("MT", [128, GB, S])
    RBV = t("RBV", [128, GB, DH])
    X = t("X", [128, GB, T])
    XT = t("XT", [128, GB, T])
    Y = [t(f"Y{lv}", [128, GB, T]) for lv in range(LEVELS)]
    Z = t("Z", [128, GB, DH])
    o_sq = t("o_sq", [128, GT])
    o_ln = t("o_ln", [128, GT])
    o_rs = t("o_rs", [128, GT])
    oT = t("oT", [128, GT])
    N2, INV, RHO, LN, RK, RBETA = range(6)

    proj, A, Bk, C0, C1 = bank[0:2], bank[2:4], bank[4:6], bank[6], bank[7]
    half_cols = slice(4 * T // 2, 4 * T)
    ph = Phase(nc, st, "delta", ("pe", "act", "dve", "pool", "sp"), {"weights": 1, "out": 1})
    pe, act, dve, pool, sp = (ph.q[n] for n in ("pe", "act", "dve", "pool", "sp"))
    FRONT, TAIL = 1, -1

    def load_weights(e, buf, h):
        e.dma_start(buf[:], a["head_w"][bass.ds(h, 1)].rearrange("o p n -> p (o n)")).then_inc(ph.dma["weights"], 16)

    def lane(buf, at, stage):
        return buf[(at["par"] + stage) % 2]

    KINDS = ("k0", "k1", "q", "v0", "v1", "g")

    def dest(kind, at):
        if kind == "g":
            return lane(gate, at, FRONT)[:]
        if kind == "q":
            return lane(qT, at, FRONT)[:]
        return lane(kT if kind[0] == "k" else vT, at, FRONT)[:, :, :, int(kind[1])]

    def pe_proj(c):
        kind, P = KINDS[c], proj[c % 2]
        free = [("act", "ET", 1), ("dve", "qn", 1)] if c < 2 else [("dve", f"conv3_{KINDS[c - 2]}", 0)]

        def project(e, at):
            for k in range(KD):
                ins = e.matmul(P[:], lane(blob, at, FRONT)[:, (k * N_TILES + c) * 128:(k * N_TILES + c + 1) * 128],
                               xT[:, k, bass.ds(at["tok1"], GT)], start=(k == 0), stop=(k == KD - 1))
            return ins
        pe.do(f"proj_{kind}", [("weights", None, -1)] + free, project, stage=FRONT)

    def act_tap(c):
        kind, P, acc = KINDS[c], proj[c % 2], conv[c % 2]
        acc_free = ("act", f"silu_{KINDS[c - 2]}", 0) if c >= 2 else ("act", f"silu_{('v1', 'v0')[c % 2]}", 1)
        j = TAPS + c * CONV + CONV - 1
        act.do(f"tap_{kind}", [("pe", f"proj_{kind}", 0), acc_free],
               lambda e, at: e.activation(acc[:], P[:].rearrange("p (b l) -> p b l", l=S), ACT.Copy,
                                          scale=lane(blob, at, FRONT)[:, j:j + 1]), stage=FRONT)

    def dve_conv(c):
        kind, P, acc = KINDS[c], proj[c % 2], conv[c % 2]
        for s in range(1, CONV):
            j = TAPS + c * CONV + CONV - 1 - s
            dve.do(f"conv{s}_{kind}", [("act", f"tap_{kind}", 0) if s == 1 else ("dve", f"conv{s - 1}_{kind}", 0)],
                   lambda e, at, s=s, j=j: e.scalar_tensor_tensor(
                       acc[:, :, s:], P[:].rearrange("p (b l) -> p b l", l=S)[:, :, 0:S - s],
                       lane(blob, at, FRONT)[:, j:j + 1], acc[:, :, s:], ALU.mult, ALU.add), stage=FRONT)

    def act_silu(c):
        kind = KINDS[c]
        last = {"k": ("pe", "kq", 1), "q": ("pe", "kq", 1), "v": ("pe", "vt1", 1), "g": ("dve", "gate_o", 0)}[kind[0]]
        ready = ("pe", "proj_g", 0) if kind == "g" else ("dve", f"conv3_{kind}", 0)
        src = proj[c % 2] if kind == "g" else conv[c % 2]
        act.do(f"silu_{kind}", [ready, last],
               lambda e, at: e.activation(dest(kind, at), src[:], ACT.Silu), stage=FRONT)

    def pairs(n):
        return range(4 * n, 4 * n + 4)

    def wide(b):
        return slice(b % 4 * T, (b % 4 + 1) * T)

    def narrow(b, at=0):
        return slice(at + b % 4 * (T // 2), at + (b % 4 + 1) * (T // 2))

    def blocks(ap, lv, odd):
        return ap.rearrange("p (n two w) -> p n two w", two=2, w=2 ** lv)[:, :, odd, :]

    def packed(ap, lv):
        return ap.rearrange("p (n w) -> p n w", w=2 ** lv)

    def merged(tile, n):
        return tile[:, 4 * n:4 * n + 4, :].rearrange("p b s -> p (b s)")

    def each(n, emit):
        for b in pairs(n):
            ins = emit(b)
        return ins

    keys = lambda at: lane(kT, at, 0)[:].rearrange("p b l j -> p b (l j)")
    vals = lambda at: lane(vT, at, 0)[:].rearrange("p b l j -> p b (l j)")
    of = lambda at, stage, i: lane(small, at, stage)[:, i, :]

    def make_y(n, lv):
        for b in pairs(n):
            src = lambda b: blocks(A[n][:, wide(b)], 0, 0) if lv == 0 else packed(A[n][:, narrow(b)], lv)
            dve.do(f"Y{lv}_{b}", [("pe", f"gram{n}" if lv == 0 else f"CX{lv}_{n}", 0), ("dve", "rho", 1),
                                 ("pe", f"XY{lv}_{n}", 1)],
                   lambda e, at, b=b: e.scalar_tensor_tensor(
                       blocks(Y[lv][:, b, :], lv, 0), src(b), of(at, 0, RHO)[:, b:b + 1],
                       packed(level[:, lv, :], lv), ALU.mult, ALU.mult))

    def turned(out, src, n):
        return lambda e, at: each(n, lambda b: e.transpose(out[:, wide(b)], src(at)[:, b], ident[:]))

    four = lambda ap: ap[:, None, :].broadcast_to([128, 4, 128])
    quad = lambda bk: bk[:].rearrange("p (b s) -> p b s", b=4)
    part = lambda tile, n: tile[:, 4 * n:4 * n + 4, :]

    sp.dma("weights", [("weights", None, -1), ("dve", "conv3_v1", 1), ("pe", "proj_g", 1), ("act", "tap_v1", 1)],
           lambda e, at: load_weights(e, blob[at["par"]], at["h2"]), stage=2)

    for n in range(2):
        pe.do(f"gram{n}", [("act", "silu_k1", 1), ("dve", f"Y{LEVELS - 1}_{4 * n + 3}", 1)],
              lambda e, at, n=n: each(n, lambda b: e.matmul(A[n][:, wide(b)], keys(at)[:, b], keys(at)[:, b],
                                                           start=True, stop=True)))

    def kq(e, at):
        for b in range(GB):
            ins = e.matmul(C0[:, b * S:(b + 1) * S], keys(at)[:, b], lane(qT, at, 0)[:, b], start=True, stop=True)
        return ins

    def out(e, at):
        for b in range(GB):
            ins = e.matmul(C1[:, b * S:(b + 1) * S], Z[:, b], MT[:, b], start=True, stop=True)
        return ins
    pe.do("o", [("act", "Z1", 1), ("dve", "MT", 1), ("dve", "RBV0", 1)], out, stage=TAIL)
    pe.do("kq", [("act", "silu_q", 1), ("dve", "RBV1", 1)], kq)
    pe_proj(0)
    act.do("o_sq", [("pe", "o", 0), ("pe", "o_mean", 1)],
           lambda e, at: e.activation(o_sq[:], C1[:], ACT.Square), stage=TAIL)
    for n in range(2):
        make_y(n, 0)
        pe.do(f"XY0_{n}", [("dve", f"Y0_{4 * n + 3}", 0), ("act", f"Z{n}", 1)], turned(Bk[n], lambda at: Y[0], n))
        dve.do(f"X0_{n}", [("dve", f"Y0_{4 * n + 3}", 0), ("pe", f"CX{LEVELS - 1}_{n}", 1)],
               lambda e, at, n=n: e.tensor_tensor(part(X, n), four(ident[:]), part(Y[0], n), ALU.subtract))
        dve.do(f"PT{n}", [("act", "ET", 1), ("pe", f"gram{n}", 0), ("pe", f"CX{LEVELS - 1}_{n}", 1)],
               lambda e, at, n=n: e.tensor_tensor(
                   merged(PT, n).rearrange("p (l j) -> p l j", j=NH), A[n][:].rearrange("p (l j) -> p l j", j=NH),
                   merged(lane(ET, at, 0), n)[:, :, None].broadcast_to([128, 4 * S, NH]), ALU.mult))
    for n in range(2):
        dve.do(f"XT0_{n}", [("pe", f"XY0_{n}", 0), ("pe", f"Z{n}", 1)],
               lambda e, at, n=n: e.tensor_tensor(part(XT, n), four(ident[:]), quad(Bk[n]), ALU.subtract))
    dve.do("MT", [("pe", "kq", 0), ("act", "ET", 1), ("pe", "o", 0)],
           lambda e, at: e.tensor_tensor(MT[:].rearrange("p b l -> p (b l)"), C0[:],
                                         lane(ET, at, 0)[:].rearrange("p b l -> p (b l)"), ALU.mult))
    pe.do("o_mean", [("act", "o_sq", 0), ("dve", "MT", 0)],
          lambda e, at: e.matmul(C0[:], ones_mean[:], o_sq[:], start=True, stop=True), stage=TAIL)
    dve.do("o_var", [("pe", "o_mean", 0), ("dve", "qn", 1)],
           lambda e, at: e.tensor_tensor(lane(qn, at, TAIL)[:], C0[:], lane(qn, at, TAIL)[:], ALU.add), stage=TAIL)
    act.do("o_ln", [("dve", "o_var", 0)],
           lambda e, at: e.activation(o_ln[:], lane(qn, at, TAIL)[:], ACT.Ln, scale=float(2 ** O_SHIFT)), stage=TAIL)
    act.do("o_rs", [("act", "o_ln", 0), ("dve", "gated", 1)],
           lambda e, at: e.activation(o_rs[:], o_ln[:], ACT.Exp, scale=-0.5), stage=TAIL)
    act_tap(0)

    for lv in range(1, LEVELS):
        last = lv == LEVELS - 1
        for n in range(2):
            pe.do(f"CX{lv}_{n}", [("dve", f"X{lv - 1}_{n}", 0), ("dve", f"PT{n}", 0)],
                  lambda e, at, n=n, lv=lv: each(n, lambda b: e.matmul(
                      A[n][:, narrow(b)], PT[:, b], blocks(X[:, b, :], lv, 0), start=True, stop=True)))
        if not last:
            pe_proj(lv)
        if lv == 3:
            for n, C in enumerate((C1, C0)):
                pe.do(f"vt{n}", [("act", "silu_v1", 1), ("dve", "gated", 0)], turned(C, vals, n))
        if last:
            def norms(e, at):
                for b in range(GB):
                    e.matmul(proj[1][:, b:b + 1], k_sq[:, b, :], ones[:], start=True, stop=True)
                return e.matmul(proj[0][:], ones_q[:], q_sq[:], start=True, stop=True)
            pe.do("norms", [("act", "q_sq", 0), ("dve", "conv3_v1", 0), ("act", "silu_g", 0)], norms, stage=FRONT)
        for n in range(2):
            make_y(n, lv)
        if last:
            tiny = 1e-24
            dve.do("n2", [("pe", "norms", 0)],
                   lambda e, at: e.tensor_scalar(of(at, FRONT, N2), proj[1][:, 0:GB], tiny, None, ALU.max), stage=FRONT)
            dve.do("qn", [("pe", "norms", 0), ("dve", "o_var", 0), ("act", "o_ln", 0)],
                   lambda e, at: e.tensor_scalar(lane(qn, at, FRONT)[:], proj[0][:], tiny * EPS * DH, None, ALU.max),
                   stage=FRONT)
            dve.do("inv", [("dve", "n2", 0)], lambda e, at: e.reciprocal(of(at, FRONT, INV), of(at, FRONT, N2)), stage=FRONT)
            dve.do("rho", [("dve", "inv", 0)],
                   lambda e, at: e.tensor_tensor(of(at, FRONT, RHO), of(at, FRONT, INV), flat(beta, at), ALU.mult), stage=FRONT)
        if lv == 2:
            dve.do("gate_o", [("act", "o_rs", 0), ("act", "silu_g", 1)],
                   lambda e, at: e.scalar_tensor_tensor(o_rs[:], lane(gate, at, TAIL)[:], onorm[:, 0:1], o_rs[:],
                                                        ALU.mult, ALU.mult), stage=TAIL)
            dve.do("gated", [("dve", "gate_o", 0), ("out", None, 1)],
                   lambda e, at: e.scalar_tensor_tensor(oT[:], C1[:], float(2 ** (O_SHIFT // 2)), o_rs[:],
                                                        ALU.mult, ALU.mult), stage=TAIL)
        if lv == 4:
            for n, C in enumerate((C1, C0)):
                dve.do(f"RBV{n}", [("pe", f"vt{n}", 0), ("dve", "r_beta", 1), ("pe", f"Z{n}", 1)],
                       lambda e, at, n=n, C=C: e.tensor_tensor(
                           part(RBV, n), quad(C), of(at, 0, RBETA)[:, 4 * n:4 * n + 4, None].broadcast_to([128, 4, DH]),
                           ALU.mult))
        if lv < 6:
            dve_conv(lv - 1)
            act_silu(lv - 1)
            if lv < 5:
                act_tap(lv)
            else:
                act_silu(5)
        for n in range(2):
            def xy(e, at, n=n, lv=lv, last=last):
                if not last:
                    each(n, lambda b: e.matmul(A[n][:, narrow(b, 256)], XT[:, b], blocks(Y[lv][:, b, :], lv, 0),
                                               start=True, stop=True))
                return each(n, lambda b: e.matmul(Bk[n][:, narrow(b)], Y[lv][:, b], blocks(XT[:, b, :], lv, 1),
                                                  start=True, stop=True))
            pe.do(f"XY{lv}_{n}", [("dve", f"Y{lv}_{4 * n + 3}", 0), ("dve", f"XT{lv - 1}_{n}", 0)], xy)
            if not last:
                dve.do(f"X{lv}_{n}", [("pe", f"XY{lv}_{n}", 0)],
                       lambda e, at, n=n, lv=lv: e.tensor_tensor(
                           blocks(merged(X, n), lv, 0), blocks(merged(X, n), lv, 0),
                           packed(A[n][:, half_cols], lv), ALU.subtract))
            dve.do(f"XT{lv}_{n}", [("pe", f"XY{lv}_{n}", 0)],
                   lambda e, at, n=n, lv=lv: e.tensor_tensor(
                       blocks(merged(XT, n), lv, 1), blocks(merged(XT, n), lv, 1),
                       packed(Bk[n][:, 0:4 * T // 2], lv), ALU.subtract))
        if lv == 5:
            act.do("k_sq", [("act", "silu_k1", 0), ("pe", "norms", 1)],
                   lambda e, at: e.activation(k_sq[:], lane(kT, at, FRONT)[:].rearrange("p b l j -> p b (l j)"),
                                              ACT.Square), stage=FRONT)
            act.do("q_sq", [("act", "silu_q", 0), ("pe", "norms", 1)],
                   lambda e, at: e.activation(q_sq[:], lane(qT, at, FRONT)[:].rearrange("p b l -> p (b l)"),
                                              ACT.Square), stage=FRONT)

            flat = lambda tile, at: tile[:].rearrange("p h b -> p (h b)")[:, bass.ds(at["hb1"], GB)]
            pool.do("steps_rhs", [("pe", "decays", 1)],
                    lambda e, at: e.tensor_tensor(steps_rhs[:], flat(decay, at)[:, :, None].broadcast_to([128, GB, S]),
                                                  upto[:, None, :].broadcast_to([128, GB, S]), ALU.mult), stage=FRONT)
    pe.do("decays", [("pool", "steps_rhs", 0), ("dve", "n2", 0)],
          lambda e, at: e.matmul(proj[1][:], after[:], steps_rhs[:].rearrange("p b l -> p (b l)"),
                                 start=True, stop=True), stage=FRONT)
    act.do("ln_n2", [("dve", "n2", 0)],
           lambda e, at: e.activation(of(at, FRONT, LN), of(at, FRONT, N2), ACT.Ln, scale=float(2 ** K_SHIFT)),
           stage=FRONT)
    act.do("r_k", [("act", "ln_n2", 0)],
           lambda e, at: e.activation(of(at, FRONT, RK), of(at, FRONT, LN), ACT.Exp, scale=-0.5), stage=FRONT)
    act.do("ET", [("pe", "decays", 0), ("dve", "MT", 0)],
           lambda e, at: e.activation(lane(ET, at, FRONT)[:].rearrange("p b l -> p (b l)"), proj[1][:], ACT.Exp),
           stage=FRONT)
    dve.do("r_beta", [("act", "r_k", 0)],
           lambda e, at: e.scalar_tensor_tensor(of(at, FRONT, RBETA), of(at, FRONT, RK), float(2 ** (K_SHIFT // 2)),
                                                flat(beta, at), ALU.mult, ALU.mult), stage=FRONT)
    for n in range(2):
        pe.do(f"Z{n}", [("dve", f"RBV{n}", 0), ("dve", f"XT{LEVELS - 1}_{n}", 0), ("dve", "n2", 0)],
              lambda e, at, n=n: each(n, lambda b: e.matmul(Bk[n][:, wide(b)], XT[:, b], RBV[:, b],
                                                           start=True, stop=True)))
        act.do(f"Z{n}", [("pe", f"Z{n}", 0), ("pe", "o", 0)],
               lambda e, at, n=n: e.activation(part(Z, n), quad(Bk[n]), ACT.Copy))

    def store(e, at):
        e.dma_start(o_scratch.rearrange("v t h n -> v t (h n)")[:, bass.ds(at["tile0"], GT // TILE),
                                                               bass.ds(at["h128"], TILE)],
                    oT[:].rearrange("v (t n) -> v t n", n=TILE)).then_inc(ph.dma["out"], 16)
    sp.dma("store", [("dve", "gated", 0)], store, stage=TAIL)

    ph.close()
    units = NG * H

    def place(no, par):
        g1, h1 = (no + 1) // H, (no + 1) % H
        g0, h0 = (no + units - 1) // H % NG, (no + H - 1) % H
        return {"par": par, "tok1": g1 * GT, "hb1": h1 * B + g1 * GB, "h2": (no + 2) % H,
                "tile0": g0 * (GT // TILE), "h128": h0 * TILE}

    zero = st.enter_context(nc.semaphore("delta_zero"))
    with nc.Block() as block:
        def program(name):
            def _(e):
                if name == "pool":
                    for lv in range(LEVELS):
                        e.memset(Y[lv][:], 0.0).then_inc(zero, 1)
                if name in ("dve", "pe"):
                    e.wait_ge(zero, LEVELS)
                ph.open(e, name, -1, {"weights": 0, "out": 1})
                if name == "sp":
                    load_weights(e, blob[0], 0)
                    e.wait_ge(ph.dma["weights"], 32)
                    load_weights(e, blob[1], 1)
                ph.run(e, name, -1, place(-1, 1), stages=(1,))
                ph.run(e, name, 0, place(0, 0), stages=(0, 1, 2))
                with e.Fori(0, (units - 2) // 2) as i:
                    for par in (1, 0):
                        no = 2 * i + (1 if par else 2)
                        ph.run(e, name, no, place(no, par), stages=(-1, 0, 1, 2))
                ph.run(e, name, units - 1, place(units - 1, 1), stages=(-1, 0))
                ph.run(e, name, units, place(units, 0), stages=(-1,))
                if name == "sp":
                    e.wait_ge(ph.dma["weights"], 16 * (units + 2))
                    e.wait_ge(ph.dma["out"], 16 * (units + 2))
            return _
        block.tensor(program("pe"))
        block.scalar(program("act"))
        block.vector(program("dve"))
        block.gpsimd(program("pool"))
        block.sync(program("sp"))


def gates(nc, a, tensor, bank, consts, decay, beta):
    with ExitStack() as st:
        t = lambda name, shape: tensor(st, name, shape)
        xg = t("xg", [128, KD, GT])
        w = t("w_ab", [128, KD, NH, 2 * H])
        spread = [t(f"spread{j}", [128, KD, GT, NH]) for j in range(NH)]
        even, odd_decay = t("even", [128, 1]), t("odd_decay", [128, 1])
        dt = t("dt_bias", [128, H])
        rate = t("rate", [128, H])
        raw = t("raw", [128, B * 2 * H])
        z, mag, e_z, w1, w2, p, pos = (t(n, [128, H, B]) for n in ("z", "mag", "e_z", "w1", "w2", "p", "pos"))
        sem = lambda n: st.enter_context(nc.semaphore(n))
        s_const, s_more, s_x, s_pe = sem("g_const"), sem("g_more"), sem("g_x"), sem("g_pe")
        s_act, s_dve, s_raw, s_tick = sem("g_act"), sem("g_dve"), sem("g_raw"), sem("g_tick")
        s_zero, s_spread = sem("g_zero"), sem("g_spread")
        cols = GB * 2 * H
        rawv = raw[:].rearrange("p (b n) -> p n b", b=B)
        with nc.Block() as block:
            @block.sync
            def _(e):
                e.sem_inc(s_x, 1)
                with e.Fori(0, NG) as g:
                    read = e.snap(g + 1)
                    e.wait_ge(s_spread, read)
                    e.sem_inc(s_tick, 1)
                    e.dma_start(xg[:], a["xT"][:, :, bass.ds(g * GT, GT)]).then_inc(s_x, 16)
                for tile, n in consts:
                    e.dma_start(tile, a[n]).then_inc(s_more, 16)
                e.wait_ge(s_more, 16 * len(consts))

            @block.scalar
            def _(e):
                for tile, n in ((w, "w_ab"), (dt, "dt_bias"), (rate, "A_log"), (even, "even"),
                                (odd_decay, "odd_decay")):
                    e.dma_start(tile[:], a[n]).then_inc(s_const, 16)
                e.wait_ge(s_const, 80)
                e.activation(rate[:], rate[:], ACT.Exp).then_inc(s_act, 1)
                e.wait_ge(s_raw, NG + 1)
                e.activation(beta[:], rawv[:, H:, :], ACT.Exp, scale=-1.0).then_inc(s_act, 1)
                e.wait_ge(s_dve, 1)
                e.activation(mag[:], z[:], ACT.Abs).then_inc(s_act, 1)
                e.wait_ge(s_act, 3)
                e.activation(e_z[:], mag[:], ACT.Exp, scale=-1.0).then_inc(s_act, 1)

            @block.gpsimd
            def _(e):
                e.memset(spread[0][:], 0.0).then_inc(s_zero, 1)
                e.memset(spread[1][:], 0.0).then_inc(s_zero, 1)
                e.wait_ge(s_zero, 2)
                e.sem_inc(s_spread, 1)
                with e.Fori(0, NG) as g:
                    e.wait_ge(s_x, g * 16 + 17)
                    e.wait_ge(s_pe, g + 1)
                    e.sem_inc(s_tick, 1)
                    e.tensor_copy(spread[0][:, :, :, 0], xg[:]).then_inc(s_zero, 1)
                    e.tensor_copy(spread[1][:, :, :, 1], xg[:]).then_inc(s_spread, 1)

            @block.tensor
            def _(e):
                e.wait_ge(s_const, 80)
                e.sem_inc(s_pe, 1)
                with e.Fori(0, NG) as g:
                    e.wait_ge(s_spread, g + 2)
                    e.wait_ge(s_zero, g + 3)
                    e.wait_ge(s_raw, g + 1)
                    for b in range(GB):
                        for n in range(NH * KD):
                            j, k = n // KD, n % KD
                            mm = e.matmul(bank[0][:, 2 * H * b:2 * H * (b + 1)],
                                          spread[j][:, k, b * S:(b + 1) * S, :].rearrange("p l j -> p (l j)"),
                                          w[:, k, j, :], start=(n == 0), stop=(n == NH * KD - 1))
                    mm.then_inc(s_pe, 1)

            @block.vector
            def _(e):
                e.sem_inc(s_raw, 1)
                with e.Fori(0, NG) as g:
                    e.wait_ge(s_pe, g + 2)
                    e.tensor_copy(raw[:, bass.ds(g * cols, cols)], bank[0][:, 0:cols]).then_inc(s_raw, 1)
                e.wait_ge(s_const, 80)
                e.wait_ge(s_raw, NG + 1)
                count = [0]

                def step(ins):
                    count[0] += 1
                    ins.then_inc(s_dve, 1)
                    e.wait_ge(s_dve, count[0])

                step(e.tensor_tensor(z[:], rawv[:, 0:H, :], dt[:, :, None].broadcast_to([128, H, B]), ALU.add))
                step(e.tensor_scalar(pos[:], z[:], 0.0, None, ALU.max))
                e.wait_ge(s_act, 4)
                step(e.tensor_scalar(w1[:], e_z[:], 2.0, None, ALU.add))
                step(e.reciprocal(w1[:], w1[:]))
                step(e.tensor_tensor(w1[:], w1[:], e_z[:], ALU.mult))
                step(e.tensor_tensor(w2[:], w1[:], w1[:], ALU.mult))
                step(e.tensor_scalar(p[:], w2[:], 1.0 / 17, None, ALU.mult))
                for k in range(7, 0, -1):
                    step(e.scalar_tensor_tensor(p[:], p[:], 1.0 / (2 * k + 1), w2[:], ALU.add, ALU.mult))
                step(e.scalar_tensor_tensor(p[:], p[:], 1.0, w1[:], ALU.add, ALU.mult))
                step(e.scalar_tensor_tensor(p[:], p[:], 2.0, pos[:], ALU.mult, ALU.add))
                step(e.scalar_tensor_tensor(decay[:], p[:], -1.0, rate[:, :, None].broadcast_to([128, H, B]),
                                            ALU.mult, ALU.mult))
                step(e.tensor_scalar(decay[:], decay[:], even[:, 0:1], odd_decay[:, 0:1], ALU.mult, ALU.add))
                step(e.tensor_scalar(beta[:], beta[:], 0.5, 0.5, ALU.mult, ALU.add))
                step(e.reciprocal(beta[:], beta[:]))


def tile_phase(nc, st, a, tensor, bank, ident, mask, w_q, w_qs, w_uvo, w_gate, w_up, w_down, o_scratch):
    t = lambda name, shape, dt=F32: tensor(st, name, shape, dt)
    SL = 2
    w_out = t("w_out", [128, H, D])
    w_dq = t("w_dq", [128, KD, QC])
    w_kvc = t("w_kvc", [128, KD, KVC])
    w_kr = t("w_kr", [KVC, 2 * R])
    cos = t("cos", [128, S])
    sin = t("sin", [128, S])
    two = lambda name, shape: [t(f"{name}{i}", shape) for i in range(SL)]
    o_in, x_in, c_in = two("o_in", [128, H, TILE]), two("x_in", [128, D]), two("c_in", [128, KD, TILE])
    res, xn, xnT = two("res", [128, D]), two("xn", [128, D]), two("xnT", [128, KD, TILE])
    stats, mv, rstd = two("stats", [128, 6]), two("mv", [128, 2]), two("rstd", [128, 2])
    qc, kcat, kvtok = two("qc", [QC, TILE]), two("kcat", [128, TILE]), two("kvtok", [128, KVC])
    qcat = two("qcat", [128, 2, XH, S])
    rope1, rope2 = two("rope1", [128, 4 * TILE]), two("rope2", [128, 4 * TILE])
    att = two("att", [128, XH // 2, 2, S])
    attT = two("attT", [128, XH // 2, 2, S])
    high = two("high", [128, XH])
    ctxT = two("ctxT", [128, XH // 2, 2, S])
    hid = att
    gact = attT

    ph = Phase(nc, st, "tile", ("pe", "act", "dve", "pool", "sp"), {"in": 3 * SL, "out": SL})
    pe, act, dve, pool, sp = (ph.q[n] for n in ("pe", "act", "dve", "pool", "sp"))
    rows = lambda ap, at, s: ap[bass.ds(at["tok"] + s * TILE, TILE), :]

    def load(e, at):
        for s in range(SL):
            e.dma_start(o_in[s][:].rearrange("v h n -> v (h n)"),
                        o_scratch.rearrange("v t h n -> v t (h n)")[:, bass.ds(at["tile"] + s, 1), :]
                        .rearrange("v t n -> v (t n)")).then_inc(ph.dma["in"], 16)
            e.dma_start(x_in[s][:], rows(a["x"], at, s)).then_inc(ph.dma["in"], 16)
            e.dma_start(c_in[s][:], a["ctxT"][:, :, bass.ds(at["tok"] + s * TILE, TILE)]).then_inc(ph.dma["in"], 16)
    sp.dma("load", [("pe", f"out{SL - 1}", 1), ("pe", f"kv{SL - 1}", 1), ("dve", f"res0_{SL - 1}", 1)], load)

    def norm(i, s, psum, base, after_pe, out_free):
        dve.do(f"res{i}_{s}", [("pe", after_pe, 0), ("in", None, 0), ("dve", f"xn{(i - 1) % 3}_{s}", 0 if i else 1)],
               lambda e, at: e.tensor_tensor(res[s][:], psum[:, 0:D], base[:], ALU.add))
        dve.do(f"stats{i}_{s}", [("dve", f"res{i}_{s}", 0)], lambda e, at: e.bn_stats(stats[s][:], res[s][:]))
        dve.do(f"mv{i}_{s}", [("dve", f"stats{i}_{s}", 0)], lambda e, at: e.bn_aggr(mv[s][:], stats[s][:]), apart=True)
        dve.do(f"var{i}_{s}", [("dve", f"mv{i}_{s}", 0)],
               lambda e, at: e.tensor_scalar(rstd[s][:, 0:1], mv[s][:, 1:2], EPS, None, ALU.add))
        act.do(f"ln{i}_{s}", [("dve", f"var{i}_{s}", 0)],
               lambda e, at: e.activation(rstd[s][:, 1:2], rstd[s][:, 0:1], ACT.Ln))
        act.do(f"rstd{i}_{s}", [("act", f"ln{i}_{s}", 0)],
               lambda e, at: e.activation(rstd[s][:, 0:1], rstd[s][:, 1:2], ACT.Exp, scale=-0.5))
        dve.do(f"xn{i}_{s}", [("act", f"rstd{i}_{s}", 0)] + out_free,
               lambda e, at: e.tensor_scalar(xn[s][:], res[s][:], mv[s][:, 0:1], rstd[s][:, 0:1],
                                             ALU.subtract, ALU.mult))

    def turn_xn(i, s, bk, free):
        def emit(e, at):
            for k in range(KD):
                ins = e.transpose(bk[:, k * TILE:(k + 1) * TILE], xn[s][:, k * 128:(k + 1) * 128], ident[:])
            return ins
        pe.do(f"xT{i}_{s}", [("dve", f"xn{i}_{s}", 0)] + free, emit)
        act.do(f"xT{i}_{s}", [("pe", f"xT{i}_{s}", 0)],
               lambda e, at: e.activation(xnT[s][:], bk[:, 0:KD * TILE].rearrange("p (k n) -> p k n", k=KD), ACT.Copy))

    def chunks(e, out, lhs, rhs, n):
        for k in range(n):
            ins = e.matmul(out, lhs(k), rhs(k), start=(k == 0), stop=(k == n - 1))
        return ins

    banks = [bank[4 * s:4 * s + 4] for s in range(SL)]
    both = range(SL)
    for s in both:
        a0, b0, c0, d0 = banks[s]
        pe.do(f"out{s}", [("in", None, 0), ("dve", f"res2_{s}", 1)],
              lambda e, at, s=s, a0=a0: chunks(e, a0[:, 0:D], lambda k: o_in[s][:, k, :], lambda k: w_out[:, k, :], H))

        def kv(e, at, s=s, c0=c0):
            chunks(e, c0[0:KVC, 0:TILE], lambda k: w_kvc[:, k, :], lambda k: c_in[s][:, k, :], KD)
            return chunks(e, c0[:, TILE:TILE + KVC], lambda k: c_in[s][:, k, :], lambda k: w_kvc[:, k, :], KD)
        pe.do(f"kv{s}", [("in", None, 0), ("dve", f"hid1_{s}", 1)], kv)
        act.do(f"kcat{s}", [("pe", f"kv{s}", 0), ("pe", f"score{s}", 1)],
               lambda e, at, s=s, c0=c0: e.activation(kcat[s][0:KVC, :], c0[0:KVC, 0:TILE], ACT.Copy))
        act.do(f"kvtok{s}", [("pe", f"kv{s}", 0), ("pe", f"mix{s}", 1)],
               lambda e, at, s=s, c0=c0: e.activation(kvtok[s][:], c0[:, TILE:TILE + KVC], ACT.Copy))
        norm(0, s, a0, x_in[s], f"out{s}", [("dve", f"xn2_{s}", 1), ("out", None, 1)])

        def kr(e, at, s=s, d0=d0):
            e.matmul(d0[64:128, 0:TILE], w_kr[:, 0:R], kcat[s][0:KVC, :], start=True, stop=True)
            return e.matmul(d0[64:128, TILE:2 * TILE], w_kr[:, R:], kcat[s][0:KVC, :], start=True, stop=True)
        pe.do(f"kr{s}", [("act", f"kcat{s}", 0), ("dve", f"hid1_{s}", 1)], kr, apart=True)
    seq = lambda ap: ap.rearrange("p (b k) -> p b k", k=S)

    def table(tab, n):
        return tab[64:128, None, :].broadcast_to([64, n, S])
    for s in both:
        d0 = banks[s][3]
        dve.do(f"krc{s}", [("pe", f"kr{s}", 0)],
               lambda e, at, s=s, d0=d0: e.tensor_tensor(seq(rope1[s][64:128, 0:TILE]), seq(d0[64:128, 0:TILE]),
                                                         table(cos, 2), ALU.mult))
        dve.do(f"krs{s}", [("pe", f"kr{s}", 0)],
               lambda e, at, s=s, d0=d0: e.tensor_tensor(seq(rope2[s][64:128, 0:TILE]),
                                                         seq(d0[64:128, TILE:2 * TILE]), table(sin, 2), ALU.mult))
        pool.do(f"kr{s}", [("dve", f"krs{s}", 0), ("pe", f"score{s}", 1)],
                lambda e, at, s=s: e.tensor_tensor(kcat[s][64:128, :], rope1[s][64:128, 0:TILE],
                                                   rope2[s][64:128, 0:TILE], ALU.add))
    for s in both:
        a0, b0, c0, d0 = banks[s]
        turn_xn(0, s, b0, [("act", f"silu1_{s}", 1)])
    for s in both:
        a0, b0, c0, d0 = banks[s]
        pe.do(f"qc{s}", [("act", f"xT0_{s}", 0), ("act", f"kvtok{s}", 0)],
              lambda e, at, s=s, c0=c0: chunks(e, c0[0:QC, 0:TILE], lambda k: w_dq[:, k, :],
                                               lambda k: xnT[s][:, k, :], KD))
        act.do(f"qc{s}", [("pe", f"qc{s}", 0), ("pe", f"q3_{s}", 1)],
               lambda e, at, s=s, c0=c0: e.activation(qc[s][:], c0[0:QC, 0:TILE], ACT.Copy))
    for r in range(4):
        for s in both:
            m0, m1 = banks[s][0:2] if r % 2 == 0 else banks[s][2:4]
            free = [("act", f"nope{r - 2}_{s}", 0), ("dve", f"qs{r - 2}_{s}", 0)] if r >= 2 else \
                [("act", f"xT0_{s}", 0), ("dve", f"res0_{s}", 0), ("act", f"qc{s}", 0), ("dve", f"krs{s}", 0)]

            def q_heads(e, at, r=r, s=s, m0=m0, m1=m1):
                for i in range(4):
                    e.matmul(m0[:, i * TILE:(i + 1) * TILE], w_q[:, 4 * r + i, :], qc[s][:], start=True, stop=True)
                    ins = e.matmul(m1[64:128, i * TILE:(i + 1) * TILE], w_qs[:, 4 * r + i, :], qc[s][:],
                                   start=True, stop=True)
                return ins
            pe.do(f"q{r}_{s}", [("act", f"qc{s}", 0)] + free, q_heads)
            act.do(f"nope{r}_{s}", [("pe", f"q{r}_{s}", 0), ("pe", f"score{s}", 1)],
                   lambda e, at, r=r, s=s, m0=m0: e.activation(
                       qcat[s][0:KVC, :, 4 * r:4 * r + 4, :],
                       m0[0:KVC, :].rearrange("p (h b q) -> p b h q", h=4, b=2), ACT.Copy))
            rope_free = ("pool", f"rope{r - 1}_{s}" if r else f"kr{s}", 0)
            dve.do(f"qcos{r}_{s}", [("pe", f"q{r}_{s}", 0), rope_free],
                   lambda e, at, s=s, m0=m0: e.tensor_tensor(seq(rope1[s][64:128, :]), seq(m0[64:128, :]),
                                                             table(cos, 8), ALU.mult))
            dve.do(f"qs{r}_{s}", [("pe", f"q{r}_{s}", 0), rope_free],
                   lambda e, at, s=s, m1=m1: e.tensor_tensor(seq(rope2[s][64:128, :]), seq(m1[64:128, :]),
                                                             table(sin, 8), ALU.mult))
            view = lambda ap: ap.rearrange("p (h b q) -> p b h q", h=4, b=2)

            def rope(e, at, r=r, s=s, view=view):
                return e.tensor_tensor(qcat[s][64:128, :, 4 * r:4 * r + 4, :], view(rope1[s][64:128, :]),
                                       view(rope2[s][64:128, :]), ALU.add)
            pool.do(f"rope{r}_{s}", [("dve", f"qs{r}_{s}", 0), ("pe", f"score{s}", 1)], rope)
    scale = float(1.0 / (HD + R) ** 0.5)
    for s in both:
        a0, b0, c0, d0 = banks[s]

        def score(e, at, s=s):
            for b in range(2):
                for hp in range(XH // 2):
                    ins = e.matmul(banks[s][b][:, hp * S:(hp + 1) * S], qcat[s][:, b, 2 * hp:2 * hp + 2, :],
                                   kcat[s][:, b * S:(b + 1) * S], start=True, stop=True)
            return ins
        pe.do(f"score{s}", [("act", f"nope3_{s}", 0), ("pool", f"rope3_{s}", 0), ("dve", f"qs2_{s}", 0)], score)
        for b in range(2):
            dve.do(f"mask{b}_{s}", [("pe", f"score{s}", 0), ("pe", f"down{s}", 1)],
                   lambda e, at, s=s, b=b: e.scalar_tensor_tensor(
                       att[s][:, :, b, :], banks[s][b][:].rearrange("p (h k) -> p h k", k=S), scale,
                       mask[:, bass.ds(at["seq"] + 2 * s + b, 1), :].broadcast_to([128, XH // 2, S]),
                       ALU.mult, ALU.add))
    for s in both:
        rows16 = lambda tile: tile[:].rearrange("p h b k -> p (h b) k")
        wide = lambda ap: ap[:, :, None].broadcast_to([128, XH, S])
        dve.do(f"high{s}", [("dve", f"mask1_{s}", 0)],
               lambda e, at, s=s: e.tensor_reduce(high[s][:], rows16(att[s]), AX.X, ALU.max))
        dve.do(f"shift{s}", [("dve", f"high{s}", 0)],
               lambda e, at, s=s: e.tensor_tensor(rows16(att[s]), rows16(att[s]), wide(high[s]), ALU.subtract))
        act.do(f"exp{s}", [("dve", f"shift{s}", 0)],
               lambda e, at, s=s: e.activation(rows16(att[s]), rows16(att[s]), ACT.Exp))
    for s in both:
        dve.do(f"sum{s}", [("act", f"exp{s}", 0)],
               lambda e, at, s=s: e.tensor_reduce(high[s][:], rows16(att[s]), AX.X, ALU.add))
        dve.do(f"rsum{s}", [("dve", f"sum{s}", 0)], lambda e, at, s=s: e.reciprocal(high[s][:], high[s][:]))
        dve.do(f"prob{s}", [("dve", f"rsum{s}", 0)],
               lambda e, at, s=s: e.tensor_tensor(rows16(att[s]), rows16(att[s]), wide(high[s]), ALU.mult))
    for s in both:
        def turn_att(e, at, s=s):
            for hp in range(XH // 2):
                ins = e.transpose(banks[s][2 + hp // 4][:, (hp % 4) * 128:(hp % 4 + 1) * 128],
                                  att[s][:, hp].rearrange("p b k -> p (b k)"), ident[:])
            return ins
        pe.do(f"attT{s}", [("dve", f"prob{s}", 0), ("dve", f"qs3_{s}", 0), ("act", f"nope3_{s}", 0)], turn_att)
        for i in range(2):
            act.do(f"attT{i}_{s}", [("pe", f"attT{s}", 0), ("dve", f"hid1_{s}", 1)],
                   lambda e, at, s=s, i=i: e.activation(
                       attT[s][:, 4 * i:4 * i + 4], banks[s][2 + i][:].rearrange("p (h c q) -> p h c q", h=4, c=2),
                       ACT.Copy))

        def mix(e, at, s=s):
            for b in range(2):
                for h2 in range(2):
                    ins = e.matmul(banks[s][b][64 * h2:64 * h2 + 64, :], kvtok[s][64 * b:64 * b + 64, :],
                                   attT[s][64 * b:64 * b + 64, :, h2, :], start=True, stop=True)
            return ins
        pe.do(f"mix{s}", [("act", f"attT1_{s}", 0), ("dve", f"mask1_{s}", 0)], mix, apart=True)
        for b in range(2):
            act.do(f"ctx{b}_{s}", [("pe", f"mix{s}", 0), ("pe", f"cross{s}", 1)],
                   lambda e, at, s=s, b=b: e.activation(ctxT[s][:, :, b, :],
                                                        banks[s][b][:].rearrange("p (h q) -> p h q", q=S), ACT.Copy))
    for s in both:
        c0, d0 = banks[s][2:4]
        pe.do(f"cross{s}", [("act", f"ctx1_{s}", 0), ("act", f"attT0_{s}", 0)],
              lambda e, at, s=s, c0=c0: chunks(e, c0[:, 0:D],
                                               lambda k: ctxT[s][:, k].rearrange("p b q -> p (b q)"),
                                               lambda k: w_uvo[:, k, :], XH // 2))
        norm(1, s, c0, xn[s], f"cross{s}", [("act", f"xT0_{s}", 0)])
        turn_xn(1, s, d0, [("act", f"attT1_{s}", 0)])
    for s in both:
        def ffn(e, at, s=s):
            for i, w in ((0, w_gate), (2, w_up)):
                for j in range(FJ):
                    ins = chunks(e, banks[s][i + j // 4][:, (j % 4) * TILE:(j % 4 + 1) * TILE],
                                 lambda k: w[:, k, j * 128:(j + 1) * 128], lambda k: xnT[s][:, k, :], KD)
            return ins
        pe.do(f"ffn{s}", [("act", f"xT1_{s}", 0), ("act", f"ctx1_{s}", 0), ("dve", f"res1_{s}", 0)], ffn)
    flat = lambda tile: tile[:].rearrange("p h b k -> p (h b k)")
    for s in both:
        for i in range(2):
            act.do(f"silu{i}_{s}", [("pe", f"ffn{s}", 0), ("pe", f"mix{s}", 0)],
                   lambda e, at, s=s, i=i: e.activation(flat(gact[s])[:, 512 * i:512 * (i + 1)], banks[s][i][:],
                                                        ACT.Silu))
            dve.do(f"hid{i}_{s}", [("act", f"silu{i}_{s}", 0), ("pe", f"attT{s}", 0)],
                   lambda e, at, s=s, i=i: e.tensor_tensor(flat(hid[s])[:, 512 * i:512 * (i + 1)],
                                                           flat(gact[s])[:, 512 * i:512 * (i + 1)],
                                                           banks[s][2 + i][:], ALU.mult))
    for s in both:
        a0 = banks[s][0]
        pe.do(f"down{s}", [("dve", f"hid1_{s}", 0), ("act", f"silu0_{s}", 0)],
              lambda e, at, s=s, a0=a0: chunks(e, a0[:, 0:D], lambda k: flat(hid[s])[:, k * 128:(k + 1) * 128],
                                               lambda k: w_down[:, k, :], FJ))
        norm(2, s, a0, xn[s], f"down{s}", [("act", f"xT1_{s}", 0)])

    def store(e, at):
        for s in range(SL):
            e.dma_start(rows(a["y"], at, s), xn[s][:]).then_inc(ph.dma["out"], 8 * 2)
    sp.dma("store", [("dve", f"xn2_{s}", 0) for s in both], store)

    ph.close()
    with nc.Block() as block:
        loads = ((w_out, "w_out"), (w_dq, "w_dq"), (w_kvc, "w_kvc"), (w_kr, "w_kr"), (cos, "cos"), (sin, "sin"))
        s_load = st.enter_context(nc.semaphore("tile_weights"))

        def program(name):
            def _(e):
                if name == "sp":
                    for tile, n in loads:
                        e.dma_start(tile[:], a[n]).then_inc(s_load, 16)
                else:
                    e.wait_ge(s_load, 16 * len(loads))
                ph.open(e, name, 0, {"in": 0, "out": 0})
                with e.Fori(0, NT // SL) as i:
                    at = {"tile": i * SL, "tok": i * (SL * TILE), "seq": i * (SL * 2)}
                    ph.run(e, name, i + 0, at)
                if name == "sp":
                    e.wait_ge(ph.dma["out"], 16 * (NT + SL))
            return _
        block.tensor(program("pe"))
        block.scalar(program("act"))
        block.vector(program("dve"))
        block.gpsimd(program("pool"))
        block.sync(program("sp"))


def shape_constants():
    import numpy as np
    f = np.float32
    step = np.arange(T)
    token, key = step // NH, step % NH
    level = np.zeros((T, LEVELS, T // 2), f)
    for lv in range(LEVELS):
        cols = step[(step >> lv) % 2 == 0]
        level[:, lv, :] = (step[:, None] >> lv) == (cols[None, :] >> lv) + 1
    u = np.arange(S)
    after = np.where(key[:, None] == 0, token[:, None] > token[None, :], token[:, None] == token[None, :]).astype(f)
    upto = np.where(key[:, None] == 0, token[:, None] <= u[None, :], token[:, None] > u[None, :]).astype(f)
    even = (key[:, None] == 0).astype(f)
    half = R // 2
    inv_freq = (f(1.0) / f(10000.0) ** (np.arange(half, dtype=f) / f(half))).astype(f)
    ang = np.arange(S, dtype=f)[:, None] * inv_freq
    c, s = np.cos(ang).T, np.sin(ang).T
    cos, sin = np.zeros((128, S), f), np.zeros((128, S), f)
    cos[64:] = np.concatenate([c, c])
    sin[64:] = np.concatenate([-s, s])
    return {
        "ident": np.eye(128, dtype=f), "level": level, "after": after, "upto": upto, "even": even,
        "odd_decay": ((1 - even) * MASKED).astype(f),
        "cos": cos, "sin": sin, "keys": np.tile(np.arange(S, dtype=f), (128, 1)),
        "ones": np.ones((128, 1), f), "ones_mean": np.full((128, 128), 1.0 / DH, f),
        "ones_q": np.full((128, 128), EPS * DH, f),
    }


def kernel(**inputs):
    import numpy as np
    import concourse.bacc as bacc
    from concourse.bass_utils import run_bass_kernel_spmd

    i = {k.replace("L0_", ""): np.asarray(v) for k, v in inputs.items()}
    tile = lambda w, n: np.ascontiguousarray(w.reshape(-1, 128, n).transpose(1, 0, 2))
    arrays = dict(shape_constants())
    x = np.ascontiguousarray(i["x"].reshape(TOK, D))
    arrays["x"] = x
    arrays["xT"] = tile(x.T, TOK)
    arrays["ctxT"] = tile(i["ctx_2048"].reshape(TOK, D).T, TOK)
    heads = lambda w, n: w.reshape(n, H, DH, -1)
    wk, wv = heads(i["attn_Wk"], NH), heads(i["attn_Wv"], NH)
    wq, wg = heads(i["attn_Wq"], 1), heads(i["attn_Wg"], 1)
    w6 = np.stack([wk[0], wk[1], wq[0], wv[0], wv[1], wg[0]])
    w6 = w6.reshape(6, H, DH, KD, 128).transpose(1, 4, 3, 0, 2).reshape(H, 128, WCOLS)
    ck, cv, cq = heads(i["attn_conv_k"], NH), heads(i["attn_conv_v"], NH), heads(i["attn_conv_q"], 1)
    taps = np.stack([ck[0], ck[1], cq[0], cv[0], cv[1]]).transpose(1, 2, 0, 3).reshape(H, 128, 5 * CONV)
    arrays["head_w"] = np.concatenate([w6, taps], axis=2)
    arrays["o_norm_w"] = i["attn_o_norm_w"][:, None]
    wa, wb = i["attn_Wa"], i["attn_Wb"].reshape(NH, H, D)
    ab = np.stack([np.concatenate([wa, wb[j]]) for j in range(NH)])
    arrays["w_ab"] = np.ascontiguousarray(ab.reshape(NH, 2 * H, KD, 128).transpose(3, 2, 0, 1))
    arrays["dt_bias"] = np.ascontiguousarray(np.broadcast_to(i["attn_dt_bias"], (128, H)))
    arrays["A_log"] = np.ascontiguousarray(np.broadcast_to(i["attn_A_log"], (128, H)))
    arrays["w_out"] = tile(i["attn_Wo"].T, D)
    arrays["seg"] = np.ascontiguousarray(np.concatenate([i["itok_BxS_0_1023"].T] * 2))
    by_head = lambda w: np.ascontiguousarray(w.reshape(-1, XH, HD).transpose(2, 1, 0))
    arrays["uqT"], arrays["ukT"], arrays["uvT"] = (by_head(i[f"xattn_W_{n}"]) for n in ("uq", "uk", "uv"))
    arrays["xwo"] = tile(i["xattn_W_o"], D)
    qr = i["xattn_W_qr"].reshape(QC, XH, R)
    swap = lambda w: np.concatenate([w[..., R // 2:], w[..., :R // 2]], axis=-1)
    arrays["qr"], arrays["qrs"] = qr, swap(qr)
    arrays["w_kr"] = np.concatenate([i["xattn_W_kr"], swap(i["xattn_W_kr"])], axis=1)
    arrays["w_dq"], arrays["w_kvc"] = tile(i["xattn_W_dq"], QC), tile(i["xattn_W_kvc"], KVC)
    for n in ("gate", "up"):
        arrays[f"{n}_w"] = tile(i[f"ffn_{n}_w"].T, FI).reshape(128, KD * FI)
        arrays[f"{n}_scale"] = np.ascontiguousarray(np.broadcast_to(i[f"ffn_{n}_scale"], (128, FI)))
    arrays["down_w"] = tile(i["ffn_down_w"].T, D).reshape(128, FJ * D)
    arrays["down_scale"] = np.ascontiguousarray(np.broadcast_to(i["ffn_down_scale"], (128, D)))

    nc = bacc.Bacc("TRN2", target_bir_lowering=False, num_devices=1)
    arrays = {n: np.ascontiguousarray(v) for n, v in arrays.items()}
    a = {n: nc.dram_tensor(f"in_{n}", v.shape, mybir.dt.from_np(v.dtype), kind="ExternalInput").ap()
         for n, v in arrays.items()}
    a["y"] = nc.dram_tensor("out_y", (TOK, D), F32, kind="ExternalOutput").ap()
    build(nc, a)
    r = run_bass_kernel_spmd(nc, [{f"in_{n}": v for n, v in arrays.items()}], core_ids=[0])
    return r.results[0]["out_y"].reshape(B, S, D)
```

```python
from contextlib import ExitStack

import concourse.bass as bass
from concourse import mybir

F32 = mybir.dt.float32
I32 = mybir.dt.int32
ALU = mybir.AluOpType
ACT = mybir.ActivationFunctionType
AX = mybir.AxisListType

B, S, D = 32, 64, 256
TOK = B * S
KD = D // 128
H, DH, NH, CONV = 8, 128, 2, 4
T = S * NH
GB = 8
NG = B // GB
GT = GB * S
LEVELS = 7
MASKS = 5
XH, HD, KVC, QC, R = 16, 128, 64, 96, 64
LOOKBACK = 8
FI = 1024
FJ = FI // 128
TILE = 128
NT = TOK // TILE
EPS = 1e-5
NEG = -1e30
LN_EXP = "natural_log_exp_and_others"
MASKED = -30000.0
ZERO_POINT = 128.0
N_TILES = 6
WCOLS = KD * N_TILES * 128
TAPS = WCOLS
BLOB = TAPS + 5 * CONV
K_SHIFT, O_SHIFT = 20, 34


class Engine:

    def __init__(self, name):
        self.name, self.steps, self.keys, self.index, self.stage = name, [], [], {}, {}

    def do(self, name, waits, emit, apart=False, stage=0, key=0):
        assert name not in self.stage, name
        self.stage[name] = stage
        self.steps.append((name, waits, emit, apart, stage))
        self.keys.append(key)

    def dma(self, name, waits, emit, stage=0):
        self.steps.append((name, waits, emit, True, stage))
        self.keys.append(0)

    def order(self):
        self.steps = [self.steps[i] for i in sorted(range(len(self.steps)), key=lambda i: self.keys[i])]
        self.index = {name: n + 1 for n, name in enumerate(x[0] for x in self.steps if x[0] in self.stage)}


class Phase:

    def __init__(self, nc, ctx, label, names, loads):
        self.q = {n: Engine(n) for n in names}
        self.sem = {n: ctx.enter_context(nc.semaphore(f"{label}_{n}")) for n in names}
        self.per = {n: 16 * k for n, k in loads.items()}
        self.dma = {n: ctx.enter_context(nc.semaphore(f"{label}_dma_{n}")) for n in loads}
        self.tick = ctx.enter_context(nc.semaphore(f"{label}_tick"))

    def close(self):
        for q in self.q.values():
            q.order()
        self.count = max(len(q.index) for q in self.q.values()) + 1

    def run(self, eng, name, no, at, stages=(-1, 0, 1)):
        q = self.q[name]
        steps = [x for x in q.steps if x[4] in stages]
        used = {who for _, waits, _, _, _ in steps for who, _, _ in waits}
        fixed = isinstance(no, int)
        base = {who: no * self.per[who] for who in sorted(used) if who in self.dma}
        turn = no * self.count
        if not fixed:
            turn = eng.snap(turn)
            base = {who: eng.snap(v) for who, v in base.items()}
        names = [x[0] for x in steps if x[0] in q.index]
        seen, done = {}, 0
        for step, waits, emit, apart, _ in steps:
            for who, what, back in waits:
                if back == 0 and who in self.q and self.q[who].stage[what] not in stages:
                    continue
                if who in self.dma:
                    sem, value, reg = self.dma[who], self.per[who] * (2 - back), base[who]
                else:
                    sem, reg = self.sem[who], turn
                    value = self.count * (2 - back) + self.q[who].index[what]
                if seen.get(who, -10**9) >= value:
                    continue
                seen[who] = value
                eng.wait_ge(sem, reg + value)
                if apart:
                    eng.sem_inc(self.tick, 1)
            ins = emit(eng, at)
            if step in q.index:
                to = self.count if step == names[-1] else q.index[step]
                ins.then_inc(self.sem[name], to - done)
                done = to

    def open(self, eng, name, first, moves):
        if name == "sp":
            for who, n in self.per.items():
                eng.sem_inc(self.dma[who], n * (1 + moves[who]))
        else:
            eng.sem_inc(self.sem[name], (2 + first) * self.count)


def build(nc, a):
    ctx = ExitStack()
    with ctx:
        resident = ExitStack()
        ctx.enter_context(resident)

        def tensor(stack, name, shape, dt=F32):
            return stack.enter_context(nc.sbuf_tensor(name, shape, dt))

        bank = [ctx.enter_context(nc.psum_tensor(f"bank{i}", [128, 512], F32)) for i in range(8)]
        o_scratch = nc.dram_tensor("o_scratch", (128, NT, H, TILE), F32, kind="Internal").ap()

        ident = tensor(ctx, "ident", [128, 128])
        mask = tensor(ctx, "attn_mask", [128, B, S])
        w_q = tensor(ctx, "w_q_nope_rope", [QC, XH, KVC + R])
        w_qs = tensor(ctx, "w_q_rope_swapped", [QC, XH // 2, 2 * R])
        w_uvo = tensor(ctx, "w_uv_o", [128, XH // 2, D])
        w_gate = tensor(ctx, "w_gate", [128, KD, FI])
        w_up = tensor(ctx, "w_up", [128, KD, FI])
        w_down = tensor(ctx, "w_down", [128, FJ, D])

        prologue(nc, a, tensor, bank, ident, mask, w_q, w_qs, w_uvo, w_gate, w_up, w_down)
        with ExitStack() as st:
            delta_phase(nc, st, a, tensor, bank, ident, o_scratch)
        with ExitStack() as st:
            tile_phase(nc, st, a, tensor, bank, ident, mask, w_q, w_qs, w_uvo, w_gate, w_up, w_down, o_scratch)


def prologue(nc, a, tensor, bank, ident, mask, w_q, w_qs, w_uvo, w_gate, w_up, w_down):
    with ExitStack() as st:
        uq = tensor(st, "uq", [128, XH, QC])
        uk = tensor(st, "uk", [128, XH, KVC])
        uv = tensor(st, "uv", [128, XH, KVC])
        wo = tensor(st, "wo", [128, XH, D])
        ints = [tensor(st, f"ints{i}", [128, 2048], I32) for i in range(3)]
        scales = [tensor(st, "gate_scale", [128, FI]), tensor(st, "up_scale", [128, FI]),
                  tensor(st, "down_scale", [128, D])]
        seg_i = tensor(st, "seg_i", [128, B], I32)
        seg = tensor(st, "seg", [128, B])
        keys = tensor(st, "keys", [128, S])
        keys_ahead = tensor(st, "keys_ahead", [128, S])
        below = tensor(st, "below", [128, B, S])
        sem = lambda n: st.enter_context(nc.semaphore(n))
        s_uqk, s_uvo, s_seg, s_int, s_id = sem("p_uqk"), sem("p_uvo"), sem("p_seg"), sem("p_int"), sem("p_id")
        s_pe, s_act, s_dve = sem("p_pe"), sem("p_act"), sem("p_dve")
        with nc.Block() as block:
            @block.sync
            def _(e):
                e.dma_start(uq[:], a["uqT"]).then_inc(s_uqk, 16)
                e.dma_start(uk[:], a["ukT"]).then_inc(s_uqk, 16)
                e.dma_start(uv[:], a["uvT"]).then_inc(s_uvo, 16)
                e.dma_start(wo[:], a["xwo"]).then_inc(s_uvo, 16)
                e.dma_start(w_q[:, :, KVC:], a["qr"]).then_inc(s_id, 16)
                e.dma_start(w_qs[:], a["qrs"]).then_inc(s_id, 16)
                e.dma_start(ident[:], a["ident"]).then_inc(s_id, 16)
                e.wait_ge(s_id, 48)

            @block.scalar
            def _(e):
                e.dma_start(seg_i[:], a["seg"]).then_inc(s_seg, 16)
                e.dma_start(keys[:], a["keys"]).then_inc(s_seg, 16)
                for i, n in enumerate(("gate_w", "up_w", "down_w")):
                    e.dma_start(ints[i][:], a[n]).then_inc(s_int, 16)
                for i, n in enumerate(("gate_scale", "up_scale", "down_scale")):
                    e.dma_start(scales[i][:], a[n]).then_inc(s_int, 16)
                for i in range(2):
                    e.wait_ge(s_pe, i + 1)
                    e.activation(w_q[:, 8 * i:8 * i + 8, 0:KVC],
                                 bank[i][0:QC, :].rearrange("p (h c) -> p h c", c=KVC), ACT.Copy).then_inc(s_act, 1)
                for i in range(4):
                    e.wait_ge(s_pe, i + 3)
                    e.activation(w_uvo[:, 2 * i:2 * i + 2, :],
                                 bank[2 + i][:, :].rearrange("p (h c) -> p h c", c=D), ACT.Copy).then_inc(s_act, 1)

            @block.tensor
            def _(e):
                e.wait_ge(s_uqk, 32)
                for h in range(XH):
                    mm = e.matmul(bank[h // 8][0:QC, (h % 8) * KVC:(h % 8 + 1) * KVC], uq[:, h, :], uk[:, h, :],
                                  start=True, stop=True)
                    if h % 8 == 7:
                        mm.then_inc(s_pe, 1)
                e.wait_ge(s_uvo, 32)
                for h in range(XH):
                    hp, h2 = h // 2, h % 2
                    mm = e.matmul(bank[2 + hp // 2][64 * h2:64 * h2 + 64, (hp % 2) * D:(hp % 2 + 1) * D],
                                  uv[:, h, :], wo[:, h, :], start=True, stop=True)
                    if h % 4 == 3:
                        mm.then_inc(s_pe, 1)

            @block.vector
            def _(e):
                e.wait_ge(s_seg, 32)
                e.tensor_copy(seg[:], seg_i[:]).then_inc(s_dve, 1)
                e.tensor_scalar(keys_ahead[:], keys[:], float(LOOKBACK), None, ALU.add).then_inc(s_dve, 1)
                e.wait_ge(s_dve, 2)
                many = lambda t: t[:, None, :].broadcast_to([128, B, S])
                each = seg[:, :, None].broadcast_to([128, B, S])
                e.tensor_tensor(mask[:], many(keys), each, ALU.is_le).then_inc(s_dve, 1)
                e.tensor_tensor(below[:], many(keys_ahead), each, ALU.is_ge).then_inc(s_dve, 1)
                e.wait_ge(s_dve, 4)
                e.tensor_tensor(mask[:], mask[:], below[:], ALU.mult).then_inc(s_dve, 1)
                e.wait_ge(s_dve, 5)
                e.tensor_scalar(mask[:], mask[:], -1.0, -NEG, ALU.add, ALU.mult).then_inc(s_dve, 1)
                e.wait_ge(s_int, 96)
                for w, i in ((w_gate, 0), (w_up, 1)):
                    for k in range(KD):
                        e.scalar_tensor_tensor(w[:, k, :], ints[i][:, k * FI:(k + 1) * FI], -ZERO_POINT,
                                               scales[i][:], ALU.add, ALU.mult).then_inc(s_dve, 1)
                e.scalar_tensor_tensor(w_down[:], ints[2][:].rearrange("p (j n) -> p j n", n=D), -ZERO_POINT,
                                       scales[2][:, None, :].broadcast_to([128, FJ, D]),
                                       ALU.add, ALU.mult).then_inc(s_dve, 1)


def delta_phase(nc, st, a, tensor, bank, ident, o_scratch):
    t = lambda name, shape, dt=F32: tensor(st, name, shape, dt)
    xT = t("xT", [128, KD, TOK])
    blob = [t(f"head_weights{i}", [128, BLOB]) for i in range(2)]
    level = t("level_masks", [128, MASKS, T // 2])
    after = t("after", [128, T])
    upto = t("upto", [128, S])
    ones_mean = t("ones_mean", [128, 128])
    ones_q = t("ones_q", [128, 128])
    ones = t("ones", [128, 1])
    onorm = t("o_norm_w", [128, 1])
    decay = t("decay", [128, H, B])
    beta = t("beta", [128, H, B])
    consts = ((xT[:], "xT"), (level[:], "level"), (after[:], "after"), (upto[:], "upto"), (ones[:], "ones"),
              (ones_mean[:], "ones_mean"), (ones_q[:], "ones_q"), (onorm[:], "o_norm_w"))
    gates(nc, a, tensor, bank, consts, decay, beta)

    two = lambda name, shape: [t(f"{name}{i}", shape) for i in range(2)]
    kT, vT, qT = two("kT", [128, GB, S, NH]), two("vT", [128, GB, S, NH]), two("qT", [128, GB, S])
    gate, ET, qn, small = two("gate", [128, GT]), two("ET", [128, GB, S]), two("qn", [128, GT]), two("small", [128, 5, GB])
    conv = two("conv", [128, GB, S])
    k_sq = t("k_sq", [128, GB, T])
    q_sq = t("q_sq", [128, GT])
    steps_rhs = t("steps_rhs", [128, GB, S])
    PT = t("PT", [128, GB, T])
    MT = t("MT", [128, GB, S])
    RBV = t("RBV", [128, GB, DH])
    X = t("X", [128, GB, T])
    XT = t("XT", [128, GB, T])
    Y0T = t("Y0T", [128, GB, T])
    Y = t("Y", [128, GB, T // 2])
    Z = t("Z", [128, GB, DH])
    o_sq = t("o_sq", [128, GT])
    o_ln = t("o_ln", [128, GT])
    o_rs = t("o_rs", [128, GT])
    oT = t("oT", [128, GT])
    N2, INV, RHO, LN, KNORM = range(5)

    proj, A, Bk, C0, C1 = bank[0:2], bank[2:4], bank[4:6], bank[6], bank[7]
    half_cols = slice(4 * T // 2, 4 * T)
    ph = Phase(nc, st, "delta", ("pe", "act", "dve", "pool", "sp"), {"weights": 1, "out": 1})
    pe, act, dve, pool, sp = (ph.q[n] for n in ("pe", "act", "dve", "pool", "sp"))
    FRONT, TAIL = 1, -1

    def load_weights(e, buf, h):
        e.dma_start(buf[:], a["head_w"][bass.ds(h, 1)].rearrange("o p n -> p (o n)")).then_inc(ph.dma["weights"], 16)

    def lane(buf, at, stage):
        return buf[(at["par"] + stage) % 2]

    KINDS = ("k0", "k1", "q", "v0", "v1", "g")

    def dest(kind, at):
        if kind == "g":
            return lane(gate, at, FRONT)[:]
        if kind == "q":
            return lane(qT, at, FRONT)[:]
        return lane(kT if kind[0] == "k" else vT, at, FRONT)[:, :, :, int(kind[1])]

    def pe_proj(c):
        kind, P = KINDS[c], proj[c % 2]
        free = [("act", "ET", 1), ("dve", "qn", 1)] if c < 2 else [("dve", f"conv3_{KINDS[c - 2]}", 0)]

        def project(e, at):
            for k in range(KD):
                ins = e.matmul(P[:], lane(blob, at, FRONT)[:, (k * N_TILES + c) * 128:(k * N_TILES + c + 1) * 128],
                               xT[:, k, bass.ds(at["tok1"], GT)], start=(k == 0), stop=(k == KD - 1))
            return ins
        pe.do(f"proj_{kind}", [("weights", None, -1)] + free, project, stage=FRONT)

    def act_tap(c):
        kind, P, acc = KINDS[c], proj[c % 2], conv[c % 2]
        acc_free = ("act", f"silu_{KINDS[c - 2]}", 0) if c >= 2 else ("act", f"silu_{('v1', 'v0')[c % 2]}", 1)
        j = TAPS + c * CONV + CONV - 1
        act.do(f"tap_{kind}", [("pe", f"proj_{kind}", 0), acc_free],
               lambda e, at: e.activation(acc[:], P[:].rearrange("p (b l) -> p b l", l=S), ACT.Copy,
                                          scale=lane(blob, at, FRONT)[:, j:j + 1]), stage=FRONT)

    def dve_conv(c, taps):
        kind, P, acc = KINDS[c], proj[c % 2], conv[c % 2]
        for s in taps:
            j = TAPS + c * CONV + CONV - 1 - s
            dve.do(f"conv{s}_{kind}", [("act", f"tap_{kind}", 0) if s == 1 else ("dve", f"conv{s - 1}_{kind}", 0)],
                   lambda e, at, s=s, j=j: e.scalar_tensor_tensor(
                       acc[:, :, s:], P[:].rearrange("p (b l) -> p b l", l=S)[:, :, 0:S - s],
                       lane(blob, at, FRONT)[:, j:j + 1], acc[:, :, s:], ALU.mult, ALU.add), stage=FRONT)

    def act_silu(c):
        kind = KINDS[c]
        last = {"k": ("pe", "kq", 1), "q": ("pe", "kq", 1), "v": ("pe", "vt1", 1), "g": ("dve", "gate_o", 0)}[kind[0]]
        ready = ("pe", "proj_g", 0) if kind == "g" else ("dve", f"conv3_{kind}", 0)
        src = proj[c % 2] if kind == "g" else conv[c % 2]
        act.do(f"silu_{kind}", [ready, last],
               lambda e, at: e.activation(dest(kind, at), src[:], ACT.Silu), stage=FRONT)

    def pairs(n):
        return range(4 * n, 4 * n + 4)

    def wide(b):
        return slice(b % 4 * T, (b % 4 + 1) * T)

    def narrow(b, at=0):
        return slice(at + b % 4 * (T // 2), at + (b % 4 + 1) * (T // 2))

    def blocks(ap, lv, odd):
        return ap.rearrange("p (n two w) -> p n two w", two=2, w=2 ** lv)[:, :, odd, :]

    def packed(ap, lv):
        return ap.rearrange("p (n w) -> p n w", w=2 ** lv)

    def merged(tile, n):
        return tile[:, 4 * n:4 * n + 4, :].rearrange("p b s -> p (b s)")

    def each(n, emit):
        for b in pairs(n):
            ins = emit(b)
        return ins

    keys = lambda at: lane(kT, at, 0)[:].rearrange("p b l j -> p b (l j)")
    vals = lambda at: lane(vT, at, 0)[:].rearrange("p b l j -> p b (l j)")
    of = lambda at, stage, i: lane(small, at, stage)[:, i, :]

    def tiles(lv):
        w = 2 ** lv
        return [(slice(lo, lo + w), slice(lo + w, lo + 2 * w)) for lo in range(0, T, 2 * w)]

    def make_y(n, lv):
        w = T // 2 if lv <= 4 else 2 ** lv
        rows = slice(T // 2, T) if lv == 6 else slice(0, T)
        src = A[n][rows, 0:4 * w].rearrange("p (b s) -> p b s", b=4)
        dst = Y[rows, 4 * n:4 * n + 4, 0:w]
        dve.do(f"Y{lv}_{n}", [("pe", f"CX{lv}_{n}", 0)],
               (lambda e, at: e.tensor_tensor(dst, src, level[:, lv:lv + 1, :].broadcast_to([128, 4, w]), ALU.mult))
               if lv <= 4 else (lambda e, at: e.tensor_copy(dst, src)))

    def turned(out, src, n):
        return lambda e, at: each(n, lambda b: e.transpose(out[:, wide(b)], src(at)[:, b], ident[:]))

    four = lambda ap: ap[:, None, :].broadcast_to([128, 4, 128])
    quad = lambda bk: bk[:].rearrange("p (b s) -> p b s", b=4)
    part = lambda tile, n: tile[:, 4 * n:4 * n + 4, :]
    flat = lambda tile, at: tile[:].rearrange("p h b -> p (h b)")[:, bass.ds(at["hb1"], GB)]
    tiny = 1e-24

    def turn_back(lv, n):
        pe.do(f"T{lv}_{n}", [("dve", f"X{lv}_{n}", 0)], turned(Bk[n], lambda at: X, n))
        act.do(f"XT{lv}_{n}", [("pe", f"T{lv}_{n}", 0)],
               lambda e, at: e.activation(part(XT, n), quad(Bk[n]), ACT.Copy))

    def make_rbv(n):
        C = (C1, C0)[n]
        dve.do(f"RBV{n}", [("pe", f"vt{n}", 0), ("act", "k_norm", 1), ("pe", f"Z{n}", 1)],
               lambda e, at: e.scalar_tensor_tensor(
                   part(RBV, n), quad(C), float(2.0 ** (-K_SHIFT // 2)),
                   of(at, 0, KNORM)[:, 4 * n:4 * n + 4, None].broadcast_to([128, 4, DH]),
                   ALU.mult, ALU.mult))

    sp.dma("weights", [("weights", None, -1), ("dve", "conv3_v1", 1), ("pe", "proj_g", 1), ("act", "tap_v1", 1)],
           lambda e, at: load_weights(e, blob[at["par"]], at["h2"]), stage=2)

    for n in range(2):
        pe.do(f"gram{n}", [("act", "silu_k1", 1), ("dve", f"Y{LEVELS - 1}_{n}", 1)],
              lambda e, at, n=n: each(n, lambda b: e.matmul(A[n][:, wide(b)], keys(at)[:, b], keys(at)[:, b],
                                                           start=True, stop=True)))

    def kq(e, at):
        for b in range(GB):
            ins = e.matmul(C0[:, b * S:(b + 1) * S], keys(at)[:, b], lane(qT, at, 0)[:, b], start=True, stop=True)
        return ins

    def out(e, at):
        for b in range(GB):
            ins = e.matmul(C1[:, b * S:(b + 1) * S], Z[:, b], MT[:, b], start=True, stop=True)
        return ins
    pe.do("o", [("act", "Z1", 1), ("dve", "MT", 1), ("dve", "RBV0", 1)], out, stage=TAIL)
    pe.do("kq", [("act", "silu_q", 1), ("dve", "RBV1", 1)], kq)
    pe_proj(0)
    act.do("o_sq", [("pe", "o", 0), ("pe", "o_mean", 1)],
           lambda e, at: e.activation(o_sq[:], C1[:], ACT.Square), stage=TAIL)
    act_tap(0)
    for n in range(2):
        dve.do(f"PT{n}", [("pool", "ET_rho", 1), ("pe", f"gram{n}", 0), ("pe", f"CX{LEVELS - 1}_{n}", 1)],
               lambda e, at, n=n: e.tensor_tensor(
                   merged(PT, n).rearrange("p (l j) -> p l j", j=NH), A[n][:].rearrange("p (l j) -> p l j", j=NH),
                   merged(lane(ET, at, 0), n)[:, :, None].broadcast_to([128, 4 * S, NH]), ALU.mult))
        dve.do(f"Y0T_{n}", [("dve", f"PT{n}", 0)],
               lambda e, at, n=n: e.tensor_tensor(
                   part(Y0T, n).rearrange("p b (l j) -> p b l j", j=NH)[:, :, :, 1],
                   part(PT, n).rearrange("p b (l j) -> p b l j", j=NH)[:, :, :, 1],
                   level[:, 0:1, :].broadcast_to([128, 4, S]), ALU.mult))
        dve.do(f"XT0_{n}", [("dve", f"Y0T_{n}", 0), ("pe", f"Z{n}", 1)],
               lambda e, at, n=n: e.tensor_tensor(part(XT, n), four(ident[:]), part(Y0T, n), ALU.subtract))
        pe.do(f"T0_{n}", [("dve", f"XT0_{n}", 0), ("act", f"Z{n}", 1)], turned(Bk[n], lambda at: XT, n))
        act.do(f"X0_{n}", [("pe", f"T0_{n}", 0)],
               lambda e, at, n=n: e.activation(part(X, n), quad(Bk[n]), ACT.Copy))
    dve.do("MT", [("pe", "kq", 0), ("pool", "ET_rho", 1), ("pe", "o", 0)],
           lambda e, at: e.tensor_tensor(MT[:].rearrange("p b l -> p (b l)"), C0[:],
                                         lane(ET, at, 0)[:].rearrange("p b l -> p (b l)"), ALU.mult))
    dve_conv(0, (1,))
    pe.do("o_mean", [("act", "o_sq", 0), ("dve", "MT", 0)],
          lambda e, at: e.matmul(C0[:], ones_mean[:], o_sq[:], start=True, stop=True), stage=TAIL)
    dve.do("o_var", [("pe", "o_mean", 0), ("dve", "qn", 1)],
           lambda e, at: e.tensor_tensor(lane(qn, at, TAIL)[:], C0[:], lane(qn, at, TAIL)[:], ALU.add), stage=TAIL)
    act.do("o_ln", [("dve", "o_var", 0)],
           lambda e, at: (e.preload_act_table_set(LN_EXP),
                          e.activation(o_ln[:], lane(qn, at, TAIL)[:], ACT.Ln, scale=float(2 ** O_SHIFT)))[1],
           apart=True, stage=TAIL)
    act.do("o_rs", [("act", "o_ln", 0), ("dve", "gated", 1)],
           lambda e, at: e.activation(o_rs[:], o_ln[:], ACT.Exp, scale=-0.5), stage=TAIL)

    for lv in range(1, LEVELS):
        last = lv == LEVELS - 1
        for n in range(2):
            def cx(e, at, n=n, lv=lv):
                if lv <= 4:
                    return each(n, lambda b: e.matmul(A[n][:, narrow(b)], PT[:, b], blocks(X[:, b, :], lv, 0),
                                                      start=True, stop=True))
                w = 2 ** lv
                for even, odd in tiles(lv):
                    ins = each(n, lambda b: e.matmul(A[n][odd, b % 4 * w:(b % 4 + 1) * w], PT[even, b, odd],
                                                     X[even, b, even], start=True, stop=True))
                return ins
            pe.do(f"CX{lv}_{n}", [("act", "X0_%d" % n, 0) if lv == 1 else ("dve", f"X{lv - 1}_{n}", 0)], cx,
                  apart=lv > 4)
            if lv > 4:
                turn_back(lv - 1, n)
        for n in range(2):
            if 1 < lv <= 4:
                turn_back(lv - 1, n)
        if not last:
            pe_proj(lv)
        if lv == 3:
            for n, C in enumerate((C1, C0)):
                pe.do(f"vt{n}", [("act", "silu_v1", 1), ("dve", "gated", 0)], turned(C, vals, n))
        if last:
            def norm_k(e, at):
                for b in range(GB):
                    ins = e.matmul(proj[1][:, b:b + 1], k_sq[:, b, :], ones[:], start=True, stop=True)
                return ins
            pe.do("norm_k", [("act", "k_sq", 0), ("act", "silu_g", 0)], norm_k, stage=FRONT)
        for n in range(2):
            make_y(n, lv)
        if last:
            make_rbv(0)
            make_rbv(1)
            dve.do("n2", [("pe", "norm_k", 0)],
                   lambda e, at: e.tensor_scalar(of(at, FRONT, N2), proj[1][:, 0:GB], tiny, None, ALU.max), stage=FRONT)
        if lv == 2:
            dve.do("gated", [("dve", "gate_o", 0), ("out", None, 1)],
                   lambda e, at: e.scalar_tensor_tensor(oT[:], C1[:], float(2 ** (O_SHIFT // 2)), o_rs[:],
                                                        ALU.mult, ALU.mult), stage=TAIL)
        if lv < 6:
            dve_conv(lv - 1, (2, 3) if lv == 1 else (1, 2, 3))
            if lv == 1:
                dve.do("gate_o", [("act", "o_rs", 0), ("act", "silu_g", 1)],
                       lambda e, at: e.scalar_tensor_tensor(o_rs[:], lane(gate, at, TAIL)[:], onorm[:, 0:1], o_rs[:],
                                                            ALU.mult, ALU.mult), stage=TAIL)
            act_silu(lv - 1)
            if lv < 5:
                act_tap(lv)
            else:
                act_silu(5)
        if lv == 3:
            act.do("k_sq", [("act", "silu_k1", 0), ("pe", "norm_k", 1)],
                   lambda e, at: e.activation(k_sq[:], lane(kT, at, FRONT)[:].rearrange("p b l j -> p b (l j)"),
                                              ACT.Square), stage=FRONT)
        if lv == 4:
            act.do("q_sq", [("act", "silu_q", 0), ("pe", "norm_q", 1)],
                   lambda e, at: e.activation(q_sq[:], lane(qT, at, FRONT)[:].rearrange("p b l -> p (b l)"),
                                              ACT.Square), stage=FRONT)
        for n in range(2):
            def xy(e, at, n=n, lv=lv):
                if lv <= 4:
                    return each(n, lambda b: e.matmul(A[n][:, narrow(b, 256)], XT[:, b], Y[:, b],
                                                      start=True, stop=True))
                w = 2 ** lv
                for even, odd in tiles(lv):
                    ins = each(n, (lambda b: e.matmul(A[n][odd, 256 + b % 4 * w:256 + (b % 4 + 1) * w],
                                                      XT[odd, b, odd], Y[odd, b, 0:w], start=True, stop=True))
                               if lv == 5 else
                               (lambda b: e.matmul(Bk[n][even, narrow(b)], Y[odd, b], XT[odd, b, odd],
                                                   start=True, stop=True)))
                return ins
            pe.do(f"XY{lv}_{n}", [("dve", f"Y{lv}_{n}", 0),
                                  ("dve", f"XT0_{n}", 0) if lv == 1 else ("act", f"XT{lv - 1}_{n}", 0)], xy,
                  apart=lv > 4)
            if lv <= 4:
                dve.do(f"X{lv}_{n}", [("pe", f"XY{lv}_{n}", 0)],
                       lambda e, at, n=n, lv=lv: e.tensor_tensor(
                           blocks(merged(X, n), lv, 0), blocks(merged(X, n), lv, 0),
                           packed(A[n][:, half_cols], lv), ALU.subtract))
            elif lv == 5:
                for i, (even, odd) in enumerate(tiles(lv)):
                    dve.do(f"X{lv}_{n}" if i else f"X{lv}_{n}_first", [("pe", f"XY{lv}_{n}", 0)],
                           lambda e, at, n=n, even=even, odd=odd: e.tensor_scalar(
                               X[odd, 4 * n:4 * n + 4, even],
                               A[n][odd, 256:256 + 4 * 32].rearrange("p (b s) -> p b s", b=4), -1.0, None, ALU.mult))
            else:
                (even, odd), = tiles(lv)
                dve.do(f"XT{lv}_{n}", [("pe", f"XY{lv}_{n}", 0)],
                       lambda e, at, n=n, even=even, odd=odd: e.tensor_scalar(
                           XT[even, 4 * n:4 * n + 4, odd],
                           Bk[n][even, 0:256].rearrange("p (b s) -> p b s", b=4), -1.0, None, ALU.mult))
        if lv == 5:
            pe.do("norm_q", [("act", "q_sq", 0), ("dve", "conv3_v1", 0)],
                  lambda e, at: e.matmul(proj[0][:], ones_q[:], q_sq[:], start=True, stop=True), stage=FRONT)

            pool.do("steps_rhs", [("pe", "decays", 1)],
                    lambda e, at: e.tensor_tensor(steps_rhs[:], flat(decay, at)[:, :, None].broadcast_to([128, GB, S]),
                                                  upto[:, None, :].broadcast_to([128, GB, S]), ALU.mult), stage=FRONT)
    dve.do("inv", [("dve", "n2", 0)], lambda e, at: e.reciprocal(of(at, FRONT, INV), of(at, FRONT, N2)), stage=FRONT)
    dve.do("rho", [("dve", "inv", 0), ("pool", "ET_rho", 1)],
           lambda e, at: e.tensor_tensor(of(at, FRONT, RHO), of(at, FRONT, INV), flat(beta, at), ALU.mult), stage=FRONT)
    dve.do("qn", [("pe", "norm_q", 0), ("dve", "o_var", 0), ("act", "o_ln", 0)],
           lambda e, at: e.tensor_scalar(lane(qn, at, FRONT)[:], proj[0][:], tiny * EPS * DH, None, ALU.max),
           stage=FRONT)
    pe.do("decays", [("pool", "steps_rhs", 0), ("dve", "n2", 0)],
          lambda e, at: e.matmul(proj[1][:], after[:], steps_rhs[:].rearrange("p b l -> p (b l)"),
                                 start=True, stop=True), stage=FRONT)
    act.do("ln_n2", [("dve", "n2", 0)],
           lambda e, at: (e.preload_act_table_set(LN_EXP),
                          e.activation(of(at, FRONT, LN), of(at, FRONT, N2), ACT.Ln, scale=float(2 ** K_SHIFT)))[1],
           apart=True, stage=FRONT)
    act.do("k_norm", [("act", "ln_n2", 0)],
           lambda e, at: e.activation(of(at, FRONT, KNORM), of(at, FRONT, LN), ACT.Exp, scale=0.5), stage=FRONT)
    act.do("ET", [("pe", "decays", 0), ("dve", "MT", 0)],
           lambda e, at: e.activation(lane(ET, at, FRONT)[:].rearrange("p b l -> p (b l)"), proj[1][:], ACT.Exp),
           stage=FRONT)
    pool.do("ET_rho", [("act", "ET", 0), ("dve", "rho", 0)],
            lambda e, at: e.tensor_tensor(lane(ET, at, FRONT)[:], lane(ET, at, FRONT)[:],
                                          of(at, FRONT, RHO)[:, :, None].broadcast_to([128, GB, S]), ALU.mult),
            stage=FRONT)
    for n in range(2):
        pe.do(f"Z{n}", [("dve", f"RBV{n}", 0), ("dve", f"XT{LEVELS - 1}_{n}", 0), ("dve", "n2", 0)],
              lambda e, at, n=n: each(n, lambda b: e.matmul(Bk[n][:, wide(b)], XT[:, b], RBV[:, b],
                                                           start=True, stop=True)))
        act.do(f"Z{n}", [("pe", f"Z{n}", 0), ("pe", "o", 0)],
               lambda e, at, n=n: e.activation(part(Z, n), quad(Bk[n]), ACT.Copy))

    def store(e, at):
        e.dma_start(o_scratch.rearrange("v t h n -> v t (h n)")[:, bass.ds(at["tile0"], GT // TILE),
                                                               bass.ds(at["h128"], TILE)],
                    oT[:].rearrange("v (t n) -> v t n", n=TILE)).then_inc(ph.dma["out"], 16)
    sp.dma("store", [("dve", "gated", 0)], store, stage=TAIL)

    ph.close()
    units = NG * H

    def place(no, par):
        g1, h1 = (no + 1) // H, (no + 1) % H
        g0, h0 = (no + units - 1) // H % NG, (no + H - 1) % H
        return {"par": par, "tok1": g1 * GT, "hb1": h1 * B + g1 * GB, "h2": (no + 2) % H,
                "tile0": g0 * (GT // TILE), "h128": h0 * TILE}

    zero = st.enter_context(nc.semaphore("delta_zero"))
    with nc.Block() as block:
        def program(name):
            def _(e):
                if name == "pool":
                    e.memset(Y0T[:], 0.0).then_inc(zero, 1)
                if name == "dve":
                    e.wait_ge(zero, 1)
                ph.open(e, name, -1, {"weights": 0, "out": 1})
                if name == "sp":
                    load_weights(e, blob[0], 0)
                    e.wait_ge(ph.dma["weights"], 32)
                    load_weights(e, blob[1], 1)
                ph.run(e, name, -1, place(-1, 1), stages=(1,))
                ph.run(e, name, 0, place(0, 0), stages=(0, 1, 2))
                with e.Fori(0, (units - 2) // 2) as i:
                    for par in (1, 0):
                        no = 2 * i + (1 if par else 2)
                        ph.run(e, name, no, place(no, par), stages=(-1, 0, 1, 2))
                ph.run(e, name, units - 1, place(units - 1, 1), stages=(-1, 0))
                ph.run(e, name, units, place(units, 0), stages=(-1,))
                if name == "sp":
                    e.wait_ge(ph.dma["weights"], 16 * (units + 2))
                    e.wait_ge(ph.dma["out"], 16 * (units + 2))
            return _
        block.tensor(program("pe"))
        block.scalar(program("act"))
        block.vector(program("dve"))
        block.gpsimd(program("pool"))
        block.sync(program("sp"))


def gates(nc, a, tensor, bank, consts, decay, beta):
    with ExitStack() as st:
        t = lambda name, shape: tensor(st, name, shape)
        xg = t("xg", [128, KD, GT])
        w = t("w_ab", [128, KD, NH, 2 * H])
        spread = [t(f"spread{j}", [128, KD, GT, NH]) for j in range(NH)]
        even, odd_decay = t("even", [128, 1]), t("odd_decay", [128, 1])
        dt = t("dt_bias", [128, H])
        rate = t("rate", [128, H])
        raw = t("raw", [128, B * 2 * H])
        z, mag, e_z, w1, w2, p, pos = (t(n, [128, H, B]) for n in ("z", "mag", "e_z", "w1", "w2", "p", "pos"))
        sem = lambda n: st.enter_context(nc.semaphore(n))
        s_const, s_more, s_x, s_pe = sem("g_const"), sem("g_more"), sem("g_x"), sem("g_pe")
        s_act, s_dve, s_raw, s_tick = sem("g_act"), sem("g_dve"), sem("g_raw"), sem("g_tick")
        s_zero, s_spread = sem("g_zero"), sem("g_spread")
        cols = GB * 2 * H
        rawv = raw[:].rearrange("p (b n) -> p n b", b=B)
        with nc.Block() as block:
            @block.sync
            def _(e):
                e.sem_inc(s_x, 1)
                with e.Fori(0, NG) as g:
                    read, cleared = e.snap(g + 1), e.snap(g + 2)
                    e.wait_ge(s_spread, read)
                    e.sem_inc(s_tick, 1)
                    e.wait_ge(s_zero, cleared)
                    e.sem_inc(s_tick, 1)
                    e.dma_start(xg[:], a["xT"][:, :, bass.ds(g * GT, GT)]).then_inc(s_x, 16)
                for tile, n in consts:
                    e.dma_start(tile, a[n]).then_inc(s_more, 16)
                e.wait_ge(s_more, 16 * len(consts))

            @block.scalar
            def _(e):
                for tile, n in ((w, "w_ab"), (dt, "dt_bias"), (rate, "A_log"), (even, "even"),
                                (odd_decay, "odd_decay")):
                    e.dma_start(tile[:], a[n]).then_inc(s_const, 16)
                e.wait_ge(s_const, 80)
                e.activation(rate[:], rate[:], ACT.Exp).then_inc(s_act, 1)
                e.wait_ge(s_raw, NG + 1)
                e.activation(beta[:], rawv[:, H:, :], ACT.Exp, scale=-1.0).then_inc(s_act, 1)
                e.wait_ge(s_dve, 1)
                e.activation(mag[:], z[:], ACT.Abs).then_inc(s_act, 1)
                e.wait_ge(s_act, 3)
                e.activation(e_z[:], mag[:], ACT.Exp, scale=-1.0).then_inc(s_act, 1)

            @block.gpsimd
            def _(e):
                e.memset(spread[0][:], 0.0).then_inc(s_zero, 1)
                e.memset(spread[1][:], 0.0).then_inc(s_zero, 1)
                e.wait_ge(s_zero, 2)
                with e.Fori(0, NG) as g:
                    e.wait_ge(s_x, g * 16 + 17)
                    e.wait_ge(s_pe, g + 1)
                    e.sem_inc(s_tick, 1)
                    e.tensor_copy(spread[0][:, :, :, 0], xg[:]).then_inc(s_zero, 1)

            @block.tensor
            def _(e):
                e.wait_ge(s_const, 80)
                e.sem_inc(s_pe, 1)
                with e.Fori(0, NG) as g:
                    e.wait_ge(s_spread, g + 2)
                    e.wait_ge(s_zero, g + 3)
                    e.wait_ge(s_raw, g + 1)
                    for b in range(GB):
                        for n in range(NH * KD):
                            j, k = n // KD, n % KD
                            mm = e.matmul(bank[0][:, 2 * H * b:2 * H * (b + 1)],
                                          spread[j][:, k, b * S:(b + 1) * S, :].rearrange("p l j -> p (l j)"),
                                          w[:, k, j, :], start=(n == 0), stop=(n == NH * KD - 1))
                    mm.then_inc(s_pe, 1)

            @block.vector
            def _(e):
                e.sem_inc(s_raw, 1)
                e.wait_ge(s_zero, 2)
                e.sem_inc(s_spread, 1)
                with e.Fori(0, NG) as g:
                    e.wait_ge(s_x, g * 16 + 17)
                    e.wait_ge(s_pe, g + 1)
                    e.sem_inc(s_tick, 1)
                    e.tensor_copy(spread[1][:, :, :, 1], xg[:]).then_inc(s_spread, 1)
                    e.wait_ge(s_pe, g + 2)
                    e.tensor_copy(raw[:, bass.ds(g * cols, cols)], bank[0][:, 0:cols]).then_inc(s_raw, 1)
                e.wait_ge(s_const, 80)
                e.wait_ge(s_raw, NG + 1)
                count = [0]

                def step(ins):
                    count[0] += 1
                    ins.then_inc(s_dve, 1)
                    e.wait_ge(s_dve, count[0])

                step(e.tensor_tensor(z[:], rawv[:, 0:H, :], dt[:, :, None].broadcast_to([128, H, B]), ALU.add))
                step(e.tensor_scalar(pos[:], z[:], 0.0, None, ALU.max))
                e.wait_ge(s_act, 4)
                step(e.tensor_scalar(w1[:], e_z[:], 2.0, None, ALU.add))
                step(e.reciprocal(w1[:], w1[:]))
                step(e.tensor_tensor(w1[:], w1[:], e_z[:], ALU.mult))
                step(e.tensor_tensor(w2[:], w1[:], w1[:], ALU.mult))
                step(e.tensor_scalar(p[:], w2[:], 1.0 / 17, None, ALU.mult))
                for k in range(7, 0, -1):
                    step(e.scalar_tensor_tensor(p[:], p[:], 1.0 / (2 * k + 1), w2[:], ALU.add, ALU.mult))
                step(e.scalar_tensor_tensor(p[:], p[:], 1.0, w1[:], ALU.add, ALU.mult))
                step(e.scalar_tensor_tensor(p[:], p[:], 2.0, pos[:], ALU.mult, ALU.add))
                step(e.scalar_tensor_tensor(decay[:], p[:], -1.0, rate[:, :, None].broadcast_to([128, H, B]),
                                            ALU.mult, ALU.mult))
                step(e.tensor_scalar(decay[:], decay[:], even[:, 0:1], odd_decay[:, 0:1], ALU.mult, ALU.add))
                step(e.tensor_scalar(beta[:], beta[:], 0.5, 0.5, ALU.mult, ALU.add))
                step(e.reciprocal(beta[:], beta[:]))


def tile_phase(nc, st, a, tensor, bank, ident, mask, w_q, w_qs, w_uvo, w_gate, w_up, w_down, o_scratch):
    t = lambda name, shape, dt=F32: tensor(st, name, shape, dt)
    w_out = t("w_out", [128, H, D])
    w_dq = t("w_dq", [128, KD, QC])
    w_kvc = t("w_kvc", [128, KD, KVC])
    w_kr = t("w_kr", [KVC, 2 * R])
    cos = t("cos", [128, S])
    sin = t("sin", [128, S])
    two = lambda name, shape: [t(f"{name}{i}", shape) for i in range(2)]
    o_in, x_in, c_in = two("o_in", [128, H, TILE]), two("x_in", [128, D]), two("c_in", [128, KD, TILE])
    x1, x2, y = two("x1", [128, D]), two("x2", [128, D]), two("y", [128, D])
    kvtok, att = two("kvtok", [128, KVC]), two("att", [128, XH // 2, 2, S])
    x1T, x2T = t("x1T", [128, KD, TILE]), t("x2T", [128, KD, TILE])
    res, stats, mv, rstd = ([t(f"{n}{i}", [128, w]) for i in range(3)]
                            for n, w in (("res", D), ("stats", 6), ("mv", 2), ("rstd", 2)))
    qc, kcat = t("qc", [QC, TILE]), t("kcat", [128, TILE])
    qcat = t("qcat", [128, 2, XH, S])
    rope1, rope2 = two("rope1_", [128, 2 * TILE]), two("rope2_", [128, 2 * TILE])
    krope1, krope2 = t("krope1", [128, TILE]), t("krope2", [128, TILE])
    attT = t("attT", [128, XH // 2, 2, S])
    high = t("high", [128, XH])
    ctxT = t("ctxT", [128, XH // 2, 2, S])
    gact, hid = t("gact", [128, FJ, TILE]), t("hid", [128, FJ, TILE])

    ph = Phase(nc, st, "tile", ("pe", "act", "dve", "pool", "sp"), {"in": 3, "out": 1})
    pe, act, dve, pool, sp = (ph.q[n] for n in ("pe", "act", "dve", "pool", "sp"))
    FRONT, TAIL = 1, -1
    lane = lambda buf, at, stage: buf[(at["par"] + stage) % 2]
    rows = lambda ap, tok: ap[bass.ds(tok, TILE), :]
    fa, fb, fc, sa, sb, g0, g1, dn = bank
    fbank = (fa, fb, fc)

    def load(e, par, tile):
        e.dma_start(o_in[par][:].rearrange("v h n -> v (h n)"),
                    o_scratch.rearrange("v t h n -> v t (h n)")[:, bass.ds(tile, 1), :]
                    .rearrange("v t n -> v (t n)")).then_inc(ph.dma["in"], 16)
        e.dma_start(x_in[par][:], rows(a["x"], tile * TILE)).then_inc(ph.dma["in"], 16)
        e.dma_start(c_in[par][:], a["ctxT"][:, :, bass.ds(tile * TILE, TILE)]).then_inc(ph.dma["in"], 16)
    sp.dma("load", [("in", None, -1), ("pe", "out", 1), ("pe", "kv", 1), ("dve", "res0", 1)],
           lambda e, at: load(e, at["par"], at["tile2"]), stage=2)

    def norm(i, stage, key, after_pe, psum, base, out, out_free):
        r, s, m, v = res[i], stats[i], mv[i], rstd[i]
        dve.do(f"res{i}", after_pe, lambda e, at: e.tensor_tensor(r[:], psum[:, 0:D], base(at)[:], ALU.add),
               stage=stage, key=key)
        dve.do(f"stats{i}", [("dve", f"res{i}", 0)], lambda e, at: e.bn_stats(s[:], r[:]), stage=stage, key=key + .4)
        dve.do(f"mv{i}", [("dve", f"stats{i}", 0)], lambda e, at: e.bn_aggr(m[:], s[:]), apart=True, stage=stage,
               key=key + .8)
        dve.do(f"var{i}", [("dve", f"mv{i}", 0)],
               lambda e, at: e.tensor_scalar(v[:, 0:1], m[:, 1:2], EPS, None, ALU.add), stage=stage, key=key + 1.0)

        def ln(e, at):
            if i == 0:
                e.preload_act_table_set(LN_EXP)
            return e.activation(v[:, 1:2], v[:, 0:1], ACT.Ln)
        act.do(f"ln{i}", [("dve", f"var{i}", 0)], ln, apart=True, stage=stage, key=key + 1.2)
        act.do(f"rstd{i}", [("act", f"ln{i}", 0)],
               lambda e, at: e.activation(v[:, 0:1], v[:, 1:2], ACT.Exp, scale=-0.5), stage=stage, key=key + 1.5)
        dve.do(f"x{i + 1}", [("act", f"rstd{i}", 0)] + out_free,
               lambda e, at: e.tensor_scalar(out(at)[:], r[:], m[:, 0:1], v[:, 0:1], ALU.subtract, ALU.mult),
               stage=stage, key=key + 2.45)

    def turn_x(name, stage, key, src, waits, bk, dst, dst_free):
        def emit(e, at):
            for k in range(KD):
                ins = e.transpose(bk[:, k * TILE:(k + 1) * TILE], src(at)[:, k * 128:(k + 1) * 128], ident[:])
            return ins
        pe.do(name, waits, emit, stage=stage, key=key)
        act.do(name, [("pe", name, 0)] + dst_free,
               lambda e, at: e.activation(dst[:], bk[:, 0:KD * TILE].rearrange("p (k n) -> p k n", k=KD), ACT.Copy),
               stage=stage, key=key + .3)

    def chunks(e, out, lhs, rhs, n, some=None):
        for k in some or range(n):
            ins = e.matmul(out, lhs(k), rhs(k), start=(k == 0), stop=(k == n - 1))
        return ins
    halves = lambda n: (range(n // 2), range(n // 2, n))
    seq = lambda ap: ap.rearrange("p (b k) -> p b k", k=S)

    def kv(e, at):
        c = lane(c_in, at, FRONT)
        chunks(e, fc[0:KVC, 0:TILE], lambda k: w_kvc[:, k, :], lambda k: c[:, k, :], KD)
        return chunks(e, fc[:, TILE:TILE + KVC], lambda k: c[:, k, :], lambda k: w_kvc[:, k, :], KD)
    pe.do("kv", [("in", None, -1), ("act", "nope7", 1), ("dve", "sin7", 1)], kv, stage=FRONT, key=0)
    act.do("kcat", [("pe", "kv", 0), ("pe", "score1", 1)],
           lambda e, at: e.activation(kcat[0:KVC, :], fc[0:KVC, 0:TILE], ACT.Copy), stage=FRONT, key=1)
    act.do("kvtok", [("pe", "kv", 0), ("pe", "mix", 1)],
           lambda e, at: e.activation(lane(kvtok, at, FRONT)[:], fc[:, TILE:TILE + KVC], ACT.Copy), stage=FRONT,
           key=1.1)
    pe.do("out", [("in", None, -1), ("act", "nope5", 1), ("dve", "sin5", 1)],
          lambda e, at: chunks(e, fa[:, 0:D], lambda k: lane(o_in, at, FRONT)[:, k, :], lambda k: w_out[:, k, :], H),
          stage=FRONT, key=.5)

    def kr(e, at):
        e.matmul(fc[64:128, 0:TILE], w_kr[:, 0:R], kcat[0:KVC, :], start=True, stop=True)
        return e.matmul(fc[64:128, TILE:2 * TILE], w_kr[:, R:], kcat[0:KVC, :], start=True, stop=True)
    pe.do("kr", [("act", "kvtok", 0)], kr, apart=True, stage=FRONT, key=4)
    dve.do("krc", [("pe", "kr", 0), ("pool", "krope", 1)],
           lambda e, at: e.tensor_tensor(seq(krope1[64:128, :]), seq(fc[64:128, 0:TILE]),
                                         cos[64:128, None, :].broadcast_to([64, 2, S]), ALU.mult), stage=FRONT, key=5)
    dve.do("krs", [("pe", "kr", 0), ("pool", "krope", 1)],
           lambda e, at: e.tensor_tensor(seq(krope2[64:128, :]), seq(fc[64:128, TILE:2 * TILE]),
                                         sin[64:128, None, :].broadcast_to([64, 2, S]), ALU.mult), stage=FRONT, key=5.2)
    pool.do("krope", [("dve", "krs", 0), ("pe", "score1", 1)],
            lambda e, at: e.tensor_tensor(kcat[64:128, :], krope1[64:128, :], krope2[64:128, :], ALU.add),
            stage=FRONT, key=6)
    norm(0, FRONT, 9, [("pe", "out", 0), ("in", None, -1)], fa, lambda at: lane(x_in, at, FRONT),
         lambda at: lane(x1, at, FRONT), [("dve", "res1", 1)])
    turn_x("x1T", FRONT, 12, lambda at: lane(x1, at, FRONT), [("dve", "x1", 0), ("act", "nope6", 1), ("dve", "sin6", 1)], fb, x1T,
           [("pe", "qc", 1)])
    pe.do("qc", [("act", "x1T", 0), ("dve", "res0", 0)],
          lambda e, at: chunks(e, fa[0:QC, 0:TILE], lambda k: w_dq[:, k, :], lambda k: x1T[:, k, :], KD),
          stage=FRONT, key=13)
    act.do("qc", [("pe", "qc", 0), ("pe", "q7", 1)],
           lambda e, at: e.activation(qc[:], fa[0:QC, 0:TILE], ACT.Copy), stage=FRONT, key=13.4)

    view = lambda ap: ap.rearrange("p (h b q) -> p b h q", h=2, b=2)
    for r in range(XH // 2):
        m = fbank[(r + 1) % 3]
        key = 14.5 + 1.6 * r
        free = [("act", f"nope{r - 3}", 0), ("dve", f"sin{r - 3}", 0)] if r >= 3 else \
            {0: [("act", "x1T", 0)], 1: [("dve", "krs", 0)], 2: [("act", "qc", 0)]}[r]

        def q_heads(e, at, r=r, m=m):
            for i in range(2):
                e.matmul(m[:, i * TILE:(i + 1) * TILE], w_q[:, 2 * r + i, :], qc[:], start=True, stop=True)
            return e.matmul(m[:, 2 * TILE:3 * TILE], w_qs[:, r, :], qc[:], start=True, stop=True)
        pe.do(f"q{r}", [("act", "qc", 0)] + free, q_heads, stage=FRONT, key=key)
        act.do(f"nope{r}", [("dve", f"sin{r}_even", 0), ("pe", "score1", 1)],
               lambda e, at, r=r, m=m: e.activation(qcat[0:KVC, :, 2 * r:2 * r + 2, :],
                                                    view(m[0:KVC, 0:2 * TILE]), ACT.Copy), stage=FRONT, key=key + .7)
        rope_free = ("pool", f"rope{r - 2}", 0) if r >= 2 else ("pool", f"rope{r + 6}", 1)
        dve.do(f"cos{r}", [("pe", f"q{r}", 0), rope_free],
               lambda e, at, r=r, m=m: e.tensor_tensor(seq(rope1[r % 2][64:128, :]), seq(m[64:128, 0:2 * TILE]),
                                                       cos[64:128, None, :].broadcast_to([64, 4, S]), ALU.mult),
               stage=FRONT, key=key + .75)
        for i in range(2):
            lo = 64 * i
            dve.do(f"sin{r}" if i else f"sin{r}_even", [("pe", f"q{r}", 0), rope_free],
                   lambda e, at, r=r, m=m, i=i, lo=lo: e.tensor_tensor(
                       seq(rope2[r % 2][64:128, i * TILE:(i + 1) * TILE]), seq(m[lo:lo + 64, 2 * TILE:3 * TILE]),
                       sin[lo:lo + 64, None, :].broadcast_to([64, 2, S]), ALU.mult), stage=FRONT,
                   key=key + (.7, .8)[i])
        pool.do(f"rope{r}", [("dve", f"sin{r}", 0), ("pe", "score1", 1)],
                lambda e, at, r=r: e.tensor_tensor(qcat[64:128, :, 2 * r:2 * r + 2, :], view(rope1[r % 2][64:128, :]),
                                                   view(rope2[r % 2][64:128, :]), ALU.add), stage=FRONT, key=key + 1.2)

    for i, some in enumerate(halves(XH // 2)):
        def score(e, at, some=some):
            for b in range(2):
                for hp in some:
                    ins = e.matmul((sa, sb)[b][:, hp * S:(hp + 1) * S], qcat[:, b, 2 * hp:2 * hp + 2, :],
                                   kcat[:, b * S:(b + 1) * S], start=True, stop=True)
            return ins
        r = some[-1]
        pe.do(f"score{i}", [("act", f"nope{r}", 0), ("pool", f"rope{r}", 0), ("pool", "krope", 0),
                            ("act", "ctx1", 0), ("dve", "res1", 0)], score, stage=FRONT, key=27 + i)
    scale = float(1.0 / (HD + R) ** 0.5)
    for b in range(2):
        dve.do(f"mask{b}", [("pe", "score1", 0), ("pe", "attT", 1)],
               lambda e, at, b=b: e.scalar_tensor_tensor(
                   lane(att, at, FRONT)[:, :, b, :], (sa, sb)[b][:].rearrange("p (h k) -> p h k", k=S), scale,
                   mask[:, bass.ds(at["seq1"] + b, 1), :].broadcast_to([128, XH // 2, S]), ALU.mult, ALU.add),
               stage=FRONT, key=31 + b * .6)

    rows16 = lambda at: lane(att, at, 0)[:].rearrange("p h b k -> p (h b) k")
    wide = lambda ap: ap[:, :, None].broadcast_to([128, XH, S])
    dve.do("high", [("dve", "mask1", 1)], lambda e, at: e.tensor_reduce(high[:], rows16(at), AX.X, ALU.max), key=0)
    dve.do("shift", [("dve", "high", 0)],
           lambda e, at: e.tensor_tensor(rows16(at), rows16(at), wide(high[:]), ALU.subtract), key=.5)

    def expo(e, at):
        e.preload_act_table_set(LN_EXP)
        return e.activation(rows16(at), rows16(at), ACT.Exp)
    act.do("exp", [("dve", "shift", 0)], expo, apart=True, key=1.5)
    dve.do("sum", [("act", "exp", 0)], lambda e, at: e.tensor_reduce(high[:], rows16(at), AX.X, ALU.add), key=3)
    dve.do("rsum", [("dve", "sum", 0)], lambda e, at: e.reciprocal(high[:], high[:]), key=3.5)
    dve.do("prob", [("dve", "rsum", 0)],
           lambda e, at: e.tensor_tensor(rows16(at), rows16(at), wide(high[:]), ALU.mult), key=3.8)

    def turn_att(e, at):
        for hp in range(XH // 2):
            ins = e.transpose((sa, sb)[hp // 4][:, (hp % 4) * 128:(hp % 4 + 1) * 128],
                              lane(att, at, 0)[:, hp].rearrange("p b k -> p (b k)"), ident[:])
        return ins
    pe.do("attT", [("dve", "prob", 0), ("dve", "mask1", 1)], turn_att, key=6)
    for i in range(2):
        act.do(f"attT{i}", [("pe", "attT", 0), ("pe", "mix", 1)],
               lambda e, at, i=i: e.activation(attT[:, 4 * i:4 * i + 4],
                                               (sa, sb)[i][:].rearrange("p (h c q) -> p h c q", h=4, c=2), ACT.Copy),
               key=7 + .6 * i)

    def mix(e, at):
        for b in range(2):
            for h2 in range(2):
                ins = e.matmul((sa, sb)[b][64 * h2:64 * h2 + 64, :], lane(kvtok, at, 0)[64 * b:64 * b + 64, :],
                               attT[64 * b:64 * b + 64, :, h2, :], start=True, stop=True)
        return ins
    pe.do("mix", [("act", "attT1", 0)], mix, apart=True, key=9)
    for b in range(2):
        act.do(f"ctx{b}", [("pe", "mix", 0), ("pe", "cross1", 1)],
               lambda e, at, b=b: e.activation(ctxT[:, :, b, :], (sa, sb)[b][:].rearrange("p (h q) -> p h q", q=S),
                                               ACT.Copy), key=10.7 + .1 * b)
    for i, some in enumerate(halves(XH // 2)):
        pe.do(f"cross{i}", [("act", "ctx1", 0)],
              lambda e, at, some=some: chunks(e, sa[:, 0:D], lambda k: ctxT[:, k].rearrange("p b q -> p (b q)"),
                                              lambda k: w_uvo[:, k, :], XH // 2, some), key=12.5 + i)
    norm(1, 0, 14.6, [("pe", "cross1", 0)], sa, lambda at: lane(x1, at, 0), lambda at: lane(x2, at, 0),
         [("dve", "res2", 1)])

    turn_x("x2T", TAIL, 0, lambda at: lane(x2, at, TAIL), [("dve", "x2", 1), ("dve", "res2", 1)], dn, x2T,
           [("pe", "ffn3", 1)])
    for r in range(FJ // 2):
        g = (g0, g1)[r % 2]
        free = [("act", f"silu{r - 2}", 0), ("dve", f"hid{r - 2}", 0)] if r >= 2 else [("dve", f"hid{r + 2}", 1)]

        def ffn(e, at, r=r, g=g):
            for i, w in enumerate((w_gate, w_up)):
                for j in range(2):
                    ins = chunks(e, g[:, (2 * i + j) * TILE:(2 * i + j + 1) * TILE],
                                 lambda k: w[:, k, (2 * r + j) * 128:(2 * r + j + 1) * 128], lambda k: x2T[:, k, :], KD)
            return ins
        pe.do(f"ffn{r}", [("act", "x2T", 0)] + free, ffn, stage=TAIL, key=1.5 + 1.9 * r)
        act.do(f"silu{r}", [("pe", f"ffn{r}", 0), ("dve", f"hid{r}", 1)],
               lambda e, at, r=r, g=g: e.activation(gact[:, 2 * r:2 * r + 2, :].rearrange("p j n -> p (j n)"),
                                                    g[:, 0:2 * TILE], ACT.Silu), stage=TAIL, key=3.2 + 1.9 * r)
        dve.do(f"hid{r}", [("act", f"silu{r}", 0), ("pe", "down1", 1)],
               lambda e, at, r=r, g=g: e.tensor_tensor(hid[:, 2 * r:2 * r + 2, :].rearrange("p j n -> p (j n)"),
                                                       gact[:, 2 * r:2 * r + 2, :].rearrange("p j n -> p (j n)"),
                                                       g[:, 2 * TILE:], ALU.mult), stage=TAIL, key=3.8 + 1.9 * r)
    for i, some in enumerate(halves(FJ)):
        pe.do(f"down{i}", [("dve", f"hid{2 * i + 1}", 0), ("act", "x2T", 0)],
              lambda e, at, some=some: chunks(e, dn[:, 0:D], lambda k: hid[:, k, :], lambda k: w_down[:, k, :],
                                              FJ, some), stage=TAIL, key=(9.5, 27.5)[i])
    norm(2, TAIL, 28.5, [("pe", "down1", 0)], dn, lambda at: lane(x2, at, TAIL), lambda at: lane(y, at, TAIL),
         [("out", None, 1)])
    sp.dma("store", [("dve", "x3", 0)],
           lambda e, at: e.dma_start(rows(a["y"], at["tok0"]), lane(y, at, TAIL)[:]).then_inc(ph.dma["out"], 16),
           stage=TAIL)

    ph.close()

    def place(no, par):
        return {"par": par, "tile2": no + 2, "seq1": (no + 1) * 2, "tok0": (no - 1) * TILE}
    with nc.Block() as block:
        loads = ((w_out, "w_out"), (w_dq, "w_dq"), (w_kvc, "w_kvc"), (w_kr, "w_kr"), (cos, "cos"), (sin, "sin"))
        s_load = st.enter_context(nc.semaphore("tile_weights"))

        def program(name):
            def _(e):
                if name == "sp":
                    for tile, n in loads:
                        e.dma_start(tile[:], a[n]).then_inc(s_load, 16)
                else:
                    e.wait_ge(s_load, 16 * len(loads))
                ph.open(e, name, -1, {"in": 0, "out": 1})
                if name == "sp":
                    load(e, 0, 0)
                    e.wait_ge(ph.dma["in"], 2 * ph.per["in"])
                    load(e, 1, 1)
                ph.run(e, name, -1, place(-1, 1), stages=(1,))
                ph.run(e, name, 0, place(0, 0), stages=(0, 1, 2))
                with e.Fori(0, (NT - 4) // 2) as i:
                    for par in (1, 0):
                        no = 2 * i + (1 if par else 2)
                        ph.run(e, name, no, place(no, par), stages=(-1, 0, 1, 2))
                ph.run(e, name, NT - 3, place(NT - 3, 1), stages=(-1, 0, 1, 2))
                ph.run(e, name, NT - 2, place(NT - 2, 0), stages=(-1, 0, 1))
                ph.run(e, name, NT - 1, place(NT - 1, 1), stages=(-1, 0))
                ph.run(e, name, NT, place(NT, 0), stages=(-1,))
                if name == "sp":
                    e.wait_ge(ph.dma["out"], 16 * (NT + 2))
            return _
        block.tensor(program("pe"))
        block.scalar(program("act"))
        block.vector(program("dve"))
        block.gpsimd(program("pool"))
        block.sync(program("sp"))


def shape_constants():
    import numpy as np
    f = np.float32
    step = np.arange(T)
    token, key = step // NH, step % NH
    level = np.zeros((T, MASKS, T // 2), f)
    level[:, 0, :] = step[:, None] + 1 == step[None, key == 1]
    for lv in range(1, MASKS):
        cols = step[(step >> lv) % 2 == 0]
        level[:, lv, :] = (step[:, None] >> lv) == (cols[None, :] >> lv) + 1
    u = np.arange(S)
    after = np.where(key[:, None] == 0, token[:, None] > token[None, :], token[:, None] == token[None, :]).astype(f)
    upto = np.where(key[:, None] == 0, token[:, None] <= u[None, :], token[:, None] > u[None, :]).astype(f)
    even = (key[:, None] == 0).astype(f)
    half = R // 2
    inv_freq = (f(1.0) / f(10000.0) ** (np.arange(half, dtype=f) / f(half))).astype(f)
    ang = np.arange(S, dtype=f)[:, None] * inv_freq
    c, s = np.cos(ang).T, np.sin(ang).T
    cos, sin = np.zeros((128, S), f), np.zeros((128, S), f)
    cos[64:] = np.concatenate([c, c])
    sin[:64] = sin[64:] = np.concatenate([-s, s])
    return {
        "ident": np.eye(128, dtype=f), "level": level, "after": after, "upto": upto, "even": even,
        "odd_decay": ((1 - even) * MASKED).astype(f),
        "cos": cos, "sin": sin, "keys": np.tile(np.arange(S, dtype=f), (128, 1)),
        "ones": np.ones((128, 1), f), "ones_mean": np.full((128, 128), 1.0 / DH, f),
        "ones_q": np.full((128, 128), EPS * DH, f),
    }


def kernel(**inputs):
    import numpy as np
    import concourse.bacc as bacc
    from concourse.bass_utils import run_bass_kernel_spmd

    i = {k.replace("L0_", ""): np.asarray(v) for k, v in inputs.items()}
    tile = lambda w, n: np.ascontiguousarray(w.reshape(-1, 128, n).transpose(1, 0, 2))
    arrays = dict(shape_constants())
    x = np.ascontiguousarray(i["x"].reshape(TOK, D))
    arrays["x"] = x
    arrays["xT"] = tile(x.T, TOK)
    arrays["ctxT"] = tile(i["ctx_2048"].reshape(TOK, D).T, TOK)
    heads = lambda w, n: w.reshape(n, H, DH, -1)
    wk, wv = heads(i["attn_Wk"], NH), heads(i["attn_Wv"], NH)
    wq, wg = heads(i["attn_Wq"], 1), heads(i["attn_Wg"], 1)
    w6 = np.stack([wk[0], wk[1], wq[0], wv[0], wv[1], wg[0]])
    w6 = w6.reshape(6, H, DH, KD, 128).transpose(1, 4, 3, 0, 2).reshape(H, 128, WCOLS)
    ck, cv, cq = heads(i["attn_conv_k"], NH), heads(i["attn_conv_v"], NH), heads(i["attn_conv_q"], 1)
    taps = np.stack([ck[0], ck[1], cq[0], cv[0], cv[1]]).transpose(1, 2, 0, 3).reshape(H, 128, 5 * CONV)
    arrays["head_w"] = np.concatenate([w6, taps], axis=2)
    arrays["o_norm_w"] = i["attn_o_norm_w"][:, None]
    wa, wb = i["attn_Wa"], i["attn_Wb"].reshape(NH, H, D)
    ab = np.stack([np.concatenate([wa, wb[j]]) for j in range(NH)])
    arrays["w_ab"] = np.ascontiguousarray(ab.reshape(NH, 2 * H, KD, 128).transpose(3, 2, 0, 1))
    arrays["dt_bias"] = np.ascontiguousarray(np.broadcast_to(i["attn_dt_bias"], (128, H)))
    arrays["A_log"] = np.ascontiguousarray(np.broadcast_to(i["attn_A_log"], (128, H)))
    arrays["w_out"] = tile(i["attn_Wo"].T, D)
    arrays["seg"] = np.ascontiguousarray(np.concatenate([i["itok_BxS_0_1023"].T] * 2))
    by_head = lambda w: np.ascontiguousarray(w.reshape(-1, XH, HD).transpose(2, 1, 0))
    arrays["uqT"], arrays["ukT"], arrays["uvT"] = (by_head(i[f"xattn_W_{n}"]) for n in ("uq", "uk", "uv"))
    arrays["xwo"] = tile(i["xattn_W_o"], D)
    qr = i["xattn_W_qr"].reshape(QC, XH, R)
    swap = lambda w: np.concatenate([w[..., R // 2:], w[..., :R // 2]], axis=-1)
    arrays["qr"], arrays["qrs"] = qr, swap(qr).reshape(QC, XH // 2, 2 * R)
    arrays["w_kr"] = np.concatenate([i["xattn_W_kr"], swap(i["xattn_W_kr"])], axis=1)
    arrays["w_dq"], arrays["w_kvc"] = tile(i["xattn_W_dq"], QC), tile(i["xattn_W_kvc"], KVC)
    for n in ("gate", "up"):
        arrays[f"{n}_w"] = tile(i[f"ffn_{n}_w"].T, FI).reshape(128, KD * FI)
        arrays[f"{n}_scale"] = np.ascontiguousarray(np.broadcast_to(i[f"ffn_{n}_scale"], (128, FI)))
    arrays["down_w"] = tile(i["ffn_down_w"].T, D).reshape(128, FJ * D)
    arrays["down_scale"] = np.ascontiguousarray(np.broadcast_to(i["ffn_down_scale"], (128, D)))

    nc = bacc.Bacc("TRN2", target_bir_lowering=False, num_devices=1)
    arrays = {n: np.ascontiguousarray(v) for n, v in arrays.items()}
    a = {n: nc.dram_tensor(f"in_{n}", v.shape, mybir.dt.from_np(v.dtype), kind="ExternalInput").ap()
         for n, v in arrays.items()}
    a["y"] = nc.dram_tensor("out_y", (TOK, D), F32, kind="ExternalOutput").ap()
    build(nc, a)
    r = run_bass_kernel_spmd(nc, [{f"in_{n}": v for n, v in arrays.items()}], core_ids=[0])
    return r.results[0]["out_y"].reshape(B, S, D)
```
